# Optimizing a Trainium2 kernel written in Bass

```python
import numpy as np
import jax
import jax.numpy as jnp

def _softmax(x, axis=-1):
    return jax.nn.softmax(x, axis=axis)

def _gelu(x):
    return jax.nn.gelu(x, approximate=True)

def _silu(x):
    return jax.nn.silu(x)

def _sigmoid(x):
    return jax.nn.sigmoid(x)

def _layernorm(x, axis=-1, eps=1e-05):
    m = jnp.mean(x, axis=axis, keepdims=True)
    v = jnp.var(x, axis=axis, keepdims=True)
    return (x - m) / jnp.sqrt(v + eps)

def _scatter_add(tgt, idx, src, axis=0):
    return tgt.at[idx].add(src)

def _segment_sum(src, seg, n):
    return jax.ops.segment_sum(src, seg, n)
kernel_name = 'mk_gps_d1_gnn_r8_3b8bc5'

def setup_inputs(seed: int=0):
    np.random.seed(seed)
    _w = jnp.asarray

    def _rec_inputs():
        import jax
        import jax.numpy as jnp
        _gk = jax.random.key(seed)
        x = -8.776e-05 + 1 * jax.random.normal(jax.random.fold_in(_gk, 1), (1250, 512), jnp.float32)
        src = jax.random.randint(jax.random.fold_in(_gk, 2), (20000,), 0, 1250, jnp.int32)
        dst = jax.random.randint(jax.random.fold_in(_gk, 3), (20000,), 0, 1250, jnp.int32)
        _o = jnp.argsort(dst, stable=True)
        src = src[_o]
        dst = dst[_o]
        edge_type_2 = jax.random.randint(jax.random.fold_in(_gk, 12), (20000,), 0, 2, jnp.int32)
        return (x, src, dst, edge_type_2)
    x, src, dst, edge_type_2 = _rec_inputs()

    def _L0_gnn_setup():
        import jax, jax.numpy as jnp
        import numpy as np
        NUM_RELATIONS = 2
        NUM_BASES = 30
        HIDDEN = 512
        N_NODES = 1250
        N_EDGES = 20000

        def rgcn_gate_layer(x, row, col, edge_type, basis, att, gate_w, root, bias):
            H = x.shape[1]
            w = jnp.einsum('rb,bio->rio', att, basis)
            x_j = x[col]
            msgs = []
            for r in range(NUM_RELATIONS):
                gate = jax.nn.sigmoid(x_j @ gate_w[r, :, 0])
                msgs.append(gate[:, None] * x_j @ w[r])
            msg = jnp.where((edge_type == 0)[:, None], msgs[0], msgs[1])
            agg = jax.ops.segment_sum(msg, row, num_segments=x.shape[0])
            return agg + x @ root + bias
        key = jax.random.key(seed)
        ks = jax.random.split(key, 16)
        H, R, B = (HIDDEN, NUM_RELATIONS, NUM_BASES)
        bound = 1.0 / np.sqrt(B * H)
        u = lambda k, shape: jax.random.uniform(k, shape, jnp.float32, -bound, bound)
        inp = {'x': jax.random.normal(ks[0], (N_NODES, H), jnp.float32), 'edge_index': jax.random.randint(ks[1], (2, N_EDGES), 0, N_NODES, jnp.int32), 'edge_type': jax.random.randint(ks[2], (N_EDGES,), 0, R, jnp.int32), 'basis1': u(ks[3], (B, H, H)), 'att1': u(ks[4], (R, B)), 'gate_w1': u(ks[5], (R, H, 1)), 'root1': u(ks[6], (H, H)), 'bias1': u(ks[7], (H,)), 'basis2': u(ks[8], (B, H, H)), 'att2': u(ks[9], (R, B)), 'gate_w2': u(ks[10], (R, H, 1)), 'root2': u(ks[11], (H, H)), 'bias2': u(ks[12], (H,))}
        return inp
    _L0_gnn_all = _L0_gnn_setup()
    _L0_gnn_in = {k: v for k, v in _L0_gnn_all.items() if k in ('basis1', 'att1', 'gate_w1', 'root1', 'bias1', 'basis2', 'att2', 'gate_w2', 'root2', 'bias2')}
    del _L0_gnn_all

    def _L0_mix_setup():
        import jax, jax.numpy as jnp
        import numpy as np
        DEPTH, DIM, HEADS, DIM_HEAD, NBF, MULT = (2, 512, 8, 64, 256, 4)
        INNER = HEADS * DIM_HEAD

        def layernorm(x, g, b, eps=1e-05):
            mu = jnp.mean(x, axis=-1, keepdims=True)
            var = jnp.mean((x - mu) ** 2, axis=-1, keepdims=True)
            return (x - mu) * jax.lax.rsqrt(var + eps) * g + b

        def softmax_kernel(data, proj, is_query, eps=0.0001):
            d = data.shape[-1]
            normalizer = d ** (-0.25)
            ratio = proj.shape[0] ** (-0.5)
            data_dash = jnp.einsum('bhnd,md->bhnm', data * normalizer, proj)
            diag = jnp.sum(data ** 2, axis=-1, keepdims=True) * 0.5 * normalizer ** 2
            if is_query:
                m = jnp.max(data_dash, axis=-1, keepdims=True)
            else:
                m = jnp.max(data_dash, axis=(-2, -1), keepdims=True)
            m = jax.lax.stop_gradient(m)
            return ratio * (jnp.exp(data_dash - diag - m) + eps)
        key = jax.random.key(seed)
        ks = jax.random.split(key, 16)
        s = 0.02
        B, N = (4, 1024)
        inp = {'x': jax.random.normal(ks[0], (B, N, DIM), jnp.float32), 'ln1_g': jnp.ones((DEPTH, DIM), jnp.float32), 'ln1_b': jnp.zeros((DEPTH, DIM), jnp.float32), 'ln2_g': jnp.ones((DEPTH, DIM), jnp.float32), 'ln2_b': jnp.zeros((DEPTH, DIM), jnp.float32), 'Wq': jax.random.normal(ks[1], (DEPTH, DIM, INNER), jnp.float32) * s, 'bq': jnp.zeros((DEPTH, INNER), jnp.float32), 'Wk': jax.random.normal(ks[2], (DEPTH, DIM, INNER), jnp.float32) * s, 'bk': jnp.zeros((DEPTH, INNER), jnp.float32), 'Wv': jax.random.normal(ks[3], (DEPTH, DIM, INNER), jnp.float32) * s, 'bv': jnp.zeros((DEPTH, INNER), jnp.float32), 'Wo': jax.random.normal(ks[4], (DEPTH, INNER, DIM), jnp.float32) * s, 'bo': jnp.zeros((DEPTH, DIM), jnp.float32), 'proj': jax.random.normal(ks[5], (DEPTH, NBF, DIM_HEAD), jnp.float32), 'W1': jax.random.normal(ks[6], (DEPTH, DIM, DIM * MULT), jnp.float32) * s, 'b1': jnp.zeros((DEPTH, DIM * MULT), jnp.float32), 'W2': jax.random.normal(ks[7], (DEPTH, DIM * MULT, DIM), jnp.float32) * s, 'b2': jnp.zeros((DEPTH, DIM), jnp.float32)}
        return inp
    _L0_mix_all = _L0_mix_setup()
    _L0_mix_in = {k: v for k, v in _L0_mix_all.items() if k in ('ln1_g', 'ln1_b', 'ln2_g', 'ln2_b', 'Wq', 'bq', 'Wk', 'bk', 'Wv', 'bv', 'Wo', 'bo', 'proj', 'W1', 'b1', 'W2', 'b2')}
    del _L0_mix_all

    def _L0_ffn_setup():
        import jax, jax.numpy as jnp
        import numpy as np
        from jax import lax
        N_HEADS = 8
        D_KEYS = 128
        HALF = D_KEYS // 2
        N_KEYS = 256
        TOP_K = 8
        D_MODEL = 512

        def _forward(queries, Wq, bq, keys, w_down, w_up):
            N, T, D = queries.shape
            x = queries.reshape(-1, D)
            q = (x @ Wq + bq).reshape(-1, N_HEADS, D_KEYS)
            q1, q2 = (q[..., :HALF], q[..., HALF:])
            s1 = jnp.einsum('bhc,hnc->bhn', q1, keys[:, 0])
            s2 = jnp.einsum('bhc,hnc->bhn', q2, keys[:, 1])
            s1t, i1 = lax.top_k(s1, TOP_K)
            s2t, i2 = lax.top_k(s2, TOP_K)
            all_scores = (s1t[..., :, None] + s2t[..., None, :]).reshape(-1, N_HEADS, TOP_K * TOP_K)
            all_idx = (i1[..., :, None] * N_KEYS + i2[..., None, :]).reshape(-1, N_HEADS, TOP_K * TOP_K)
            scores, best = lax.top_k(all_scores, TOP_K)
            indices = jnp.take_along_axis(all_idx, best, axis=-1)
            w_d = w_down[indices]
            w_u = w_up[indices]
            inner = jnp.einsum('bd,bhkd->bhk', x, w_d)
            vals = jax.nn.relu(inner) * jax.nn.softmax(scores, axis=-1)
            out = jnp.einsum('bhk,bhkd->bd', vals, w_u)
            return out.reshape(N, T, D)
        key = jax.random.key(seed)
        ks = jax.random.split(key, 6)
        N, T = (2, 1024)
        queries = jax.random.normal(ks[0], (N, T, D_MODEL), dtype=jnp.float32)
        Wq = jax.random.normal(ks[1], (D_MODEL, N_HEADS * D_KEYS), dtype=jnp.float32) / np.sqrt(D_MODEL)
        bq = jnp.zeros((N_HEADS * D_KEYS,), dtype=jnp.float32)
        bound = 1.0 / np.sqrt(HALF)
        keys = jax.random.uniform(ks[2], (N_HEADS, 2, N_KEYS, HALF), dtype=jnp.float32, minval=-bound, maxval=bound)
        w_down = jax.random.normal(ks[3], (N_KEYS * N_KEYS, D_MODEL), dtype=jnp.float32) * 0.02
        w_up = jax.random.normal(ks[4], (N_KEYS * N_KEYS, D_MODEL), dtype=jnp.float32) * 0.02
        return {'queries': queries, 'Wq': Wq, 'bq': bq, 'keys': keys, 'w_down': w_down, 'w_up': w_up}
    _L0_ffn_all = _L0_ffn_setup()
    _L0_ffn_in = {k: v for k, v in _L0_ffn_all.items() if k in ('Wq', 'bq', 'keys', 'w_down', 'w_up')}
    del _L0_ffn_all
    return {'x': x, 'src': src, 'dst': dst, 'edge_type_2': edge_type_2, 'L0_gnn_basis1': _L0_gnn_in['basis1'], 'L0_gnn_att1': _L0_gnn_in['att1'], 'L0_gnn_gate_w1': _L0_gnn_in['gate_w1'], 'L0_gnn_root1': _L0_gnn_in['root1'], 'L0_gnn_bias1': _L0_gnn_in['bias1'], 'L0_gnn_basis2': _L0_gnn_in['basis2'], 'L0_gnn_att2': _L0_gnn_in['att2'], 'L0_gnn_gate_w2': _L0_gnn_in['gate_w2'], 'L0_gnn_root2': _L0_gnn_in['root2'], 'L0_gnn_bias2': _L0_gnn_in['bias2'], 'L0_mix_ln1_g': _L0_mix_in['ln1_g'], 'L0_mix_ln1_b': _L0_mix_in['ln1_b'], 'L0_mix_ln2_g': _L0_mix_in['ln2_g'], 'L0_mix_ln2_b': _L0_mix_in['ln2_b'], 'L0_mix_Wq': _L0_mix_in['Wq'], 'L0_mix_bq': _L0_mix_in['bq'], 'L0_mix_Wk': _L0_mix_in['Wk'], 'L0_mix_bk': _L0_mix_in['bk'], 'L0_mix_Wv': _L0_mix_in['Wv'], 'L0_mix_bv': _L0_mix_in['bv'], 'L0_mix_Wo': _L0_mix_in['Wo'], 'L0_mix_bo': _L0_mix_in['bo'], 'L0_mix_proj': _L0_mix_in['proj'], 'L0_mix_W1': _L0_mix_in['W1'], 'L0_mix_b1': _L0_mix_in['b1'], 'L0_mix_W2': _L0_mix_in['W2'], 'L0_mix_b2': _L0_mix_in['b2'], 'L0_ffn_Wq': _L0_ffn_in['Wq'], 'L0_ffn_bq': _L0_ffn_in['bq'], 'L0_ffn_keys': _L0_ffn_in['keys'], 'L0_ffn_w_down': _L0_ffn_in['w_down'], 'L0_ffn_w_up': _L0_ffn_in['w_up']}

def reference(x, src, dst, edge_type_2, L0_gnn_basis1, L0_gnn_att1, L0_gnn_gate_w1, L0_gnn_root1, L0_gnn_bias1, L0_gnn_basis2, L0_gnn_att2, L0_gnn_gate_w2, L0_gnn_root2, L0_gnn_bias2, L0_mix_ln1_g, L0_mix_ln1_b, L0_mix_ln2_g, L0_mix_ln2_b, L0_mix_Wq, L0_mix_bq, L0_mix_Wk, L0_mix_bk, L0_mix_Wv, L0_mix_bv, L0_mix_Wo, L0_mix_bo, L0_mix_proj, L0_mix_W1, L0_mix_b1, L0_mix_W2, L0_mix_b2, L0_ffn_Wq, L0_ffn_bq, L0_ffn_keys, L0_ffn_w_down, L0_ffn_w_up):
    import jax
    import jax.numpy as jnp

    def _L0_gnn_ref(x, edge_index, edge_type, basis1, att1, gate_w1, root1, bias1, basis2, att2, gate_w2, root2, bias2):
        import jax, jax.numpy as jnp
        import numpy as np
        NUM_RELATIONS = 2
        NUM_BASES = 30
        HIDDEN = 512
        N_NODES = 1250
        N_EDGES = 20000

        def rgcn_gate_layer(x, row, col, edge_type, basis, att, gate_w, root, bias):
            H = x.shape[1]
            w = jnp.einsum('rb,bio->rio', att, basis)
            x_j = x[col]
            msgs = []
            for r in range(NUM_RELATIONS):
                gate = jax.nn.sigmoid(x_j @ gate_w[r, :, 0])
                msgs.append(gate[:, None] * x_j @ w[r])
            msg = jnp.where((edge_type == 0)[:, None], msgs[0], msgs[1])
            agg = jax.ops.segment_sum(msg, row, num_segments=x.shape[0])
            return agg + x @ root + bias
        row, col = (edge_index[0], edge_index[1])
        h = jax.nn.relu(rgcn_gate_layer(x, row, col, edge_type, basis1, att1, gate_w1, root1, bias1))
        out = rgcn_gate_layer(h, row, col, edge_type, basis2, att2, gate_w2, root2, bias2)
        return out

    def _L0_mix_ref(x, ln1_g, ln1_b, ln2_g, ln2_b, Wq, bq, Wk, bk, Wv, bv, Wo, bo, proj, W1, b1, W2, b2):
        import jax, jax.numpy as jnp
        import numpy as np
        DEPTH, DIM, HEADS, DIM_HEAD, NBF, MULT = (2, 512, 8, 64, 256, 4)
        INNER = HEADS * DIM_HEAD

        def layernorm(x, g, b, eps=1e-05):
            mu = jnp.mean(x, axis=-1, keepdims=True)
            var = jnp.mean((x - mu) ** 2, axis=-1, keepdims=True)
            return (x - mu) * jax.lax.rsqrt(var + eps) * g + b

        def softmax_kernel(data, proj, is_query, eps=0.0001):
            d = data.shape[-1]
            normalizer = d ** (-0.25)
            ratio = proj.shape[0] ** (-0.5)
            data_dash = jnp.einsum('bhnd,md->bhnm', data * normalizer, proj)
            diag = jnp.sum(data ** 2, axis=-1, keepdims=True) * 0.5 * normalizer ** 2
            if is_query:
                m = jnp.max(data_dash, axis=-1, keepdims=True)
            else:
                m = jnp.max(data_dash, axis=(-2, -1), keepdims=True)
            m = jax.lax.stop_gradient(m)
            return ratio * (jnp.exp(data_dash - diag - m) + eps)
        B, N, D = x.shape
        for i in range(DEPTH):
            y = layernorm(x, ln1_g[i], ln1_b[i])
            q = (y @ Wq[i] + bq[i]).reshape(B, N, HEADS, DIM_HEAD).transpose(0, 2, 1, 3)
            k = (y @ Wk[i] + bk[i]).reshape(B, N, HEADS, DIM_HEAD).transpose(0, 2, 1, 3)
            v = (y @ Wv[i] + bv[i]).reshape(B, N, HEADS, DIM_HEAD).transpose(0, 2, 1, 3)
            qp = softmax_kernel(q, proj[i], True)
            kp = softmax_kernel(k, proj[i], False)
            k_sum = kp.sum(axis=2)
            d_inv = 1.0 / jnp.einsum('bhnm,bhm->bhn', qp, k_sum)
            ctx = jnp.einsum('bhnm,bhnd->bhmd', kp, v)
            o = jnp.einsum('bhmd,bhnm,bhn->bhnd', ctx, qp, d_inv)
            o = o.transpose(0, 2, 1, 3).reshape(B, N, INNER)
            x = x + o @ Wo[i] + bo[i]
            y = layernorm(x, ln2_g[i], ln2_b[i])
            h = jax.nn.gelu(y @ W1[i] + b1[i], approximate=False)
            x = x + h @ W2[i] + b2[i]
        return x

    def _L0_ffn_ref(queries, Wq, bq, keys, w_down, w_up):
        import jax, jax.numpy as jnp
        import numpy as np
        from jax import lax
        N_HEADS = 8
        D_KEYS = 128
        HALF = D_KEYS // 2
        N_KEYS = 256
        TOP_K = 8
        D_MODEL = 512

        def _forward(queries, Wq, bq, keys, w_down, w_up):
            N, T, D = queries.shape
            x = queries.reshape(-1, D)
            q = (x @ Wq + bq).reshape(-1, N_HEADS, D_KEYS)
            q1, q2 = (q[..., :HALF], q[..., HALF:])
            s1 = jnp.einsum('bhc,hnc->bhn', q1, keys[:, 0])
            s2 = jnp.einsum('bhc,hnc->bhn', q2, keys[:, 1])
            s1t, i1 = lax.top_k(s1, TOP_K)
            s2t, i2 = lax.top_k(s2, TOP_K)
            all_scores = (s1t[..., :, None] + s2t[..., None, :]).reshape(-1, N_HEADS, TOP_K * TOP_K)
            all_idx = (i1[..., :, None] * N_KEYS + i2[..., None, :]).reshape(-1, N_HEADS, TOP_K * TOP_K)
            scores, best = lax.top_k(all_scores, TOP_K)
            indices = jnp.take_along_axis(all_idx, best, axis=-1)
            w_d = w_down[indices]
            w_u = w_up[indices]
            inner = jnp.einsum('bd,bhkd->bhk', x, w_d)
            vals = jax.nn.relu(inner) * jax.nn.softmax(scores, axis=-1)
            out = jnp.einsum('bhk,bhkd->bd', vals, w_u)
            return out.reshape(N, T, D)
        return _forward(queries, Wq, bq, keys, w_down, w_up)
    edge_index = jnp.stack([src, dst])
    xn = _layernorm(x, axis=-1)
    x = x + _L0_gnn_ref(xn, edge_index, edge_type_2, L0_gnn_basis1, L0_gnn_att1, L0_gnn_gate_w1, L0_gnn_root1, L0_gnn_bias1, L0_gnn_basis2, L0_gnn_att2, L0_gnn_gate_w2, L0_gnn_root2, L0_gnn_bias2) + _L0_mix_ref(xn[None], L0_mix_ln1_g, L0_mix_ln1_b, L0_mix_ln2_g, L0_mix_ln2_b, L0_mix_Wq, L0_mix_bq, L0_mix_Wk, L0_mix_bk, L0_mix_Wv, L0_mix_bv, L0_mix_Wo, L0_mix_bo, L0_mix_proj, L0_mix_W1, L0_mix_b1, L0_mix_W2, L0_mix_b2)[0]
    x = x + _L0_ffn_ref(_layernorm(x, axis=-1)[None], L0_ffn_Wq, L0_ffn_bq, L0_ffn_keys, L0_ffn_w_down, L0_ffn_w_up)[0]
    return x

_drawn_inputs = setup_inputs


def setup_inputs(seed=0):
    import zlib

    import numpy as np

    out = dict(_drawn_inputs(seed))
    spreads = {'L0_mix_ln1_g': (1.0, 0.6),
     'L0_mix_ln1_b': (0.0, 0.57),
     'L0_mix_ln2_g': (1.0, 0.2),
     'L0_mix_ln2_b': (0.0, 0.48),
     'L0_mix_bq': (0.0, 0.8),
     'L0_mix_bk': (0.0, 0.8),
     'L0_mix_bv': (0.0, 0.1),
     'L0_mix_bo': (0.0, 0.1),
     'L0_mix_b1': (0.0, 0.1),
     'L0_mix_b2': (0.0, 0.1),
     'L0_ffn_bq': (0.0, 0.8)}
    factors = {'L0_gnn_basis1': 8.0,
     'L0_gnn_att1': 8.0,
     'L0_gnn_gate_w1': 8.0,
     'L0_gnn_root1': 8.0,
     'L0_gnn_bias1': 8.0,
     'L0_gnn_basis2': 8.0,
     'L0_gnn_att2': 8.0,
     'L0_gnn_gate_w2': 8.0,
     'L0_gnn_root2': 8.0,
     'L0_gnn_bias2': 8.0,
     'L0_mix_Wq': 8.0,
     'L0_mix_Wk': 8.0,
     'L0_mix_proj': 8.0,
     'L0_ffn_Wq': 8.0,
     'L0_ffn_keys': 8.0,
     'L0_ffn_w_down': 8.0,
     'L0_ffn_w_up': 8.0}
    for name, (base, spread) in spreads.items():
        noise = np.random.default_rng([zlib.crc32(name.encode()), seed]).standard_normal(out[name].shape)
        drawn = base * np.exp(spread * noise) if base else spread * noise
        out[name] = jnp.asarray(drawn.astype(out[name].dtype))
    for name, factor in factors.items():
        out[name] = (out[name] * factor).astype(out[name].dtype)
    return out
```

```python
from contextlib import ExitStack

import concourse.bass as bass
from concourse import mybir

F32 = mybir.dt.float32
I32 = mybir.dt.int32
U32 = mybir.dt.uint32
ALU = mybir.AluOpType
ACT = mybir.ActivationFunctionType
AX = mybir.AxisListType.X
ds = bass.ds

NODES, DIM, EDGES = 1250, 512, 20000
P = 125
TILES = NODES // P
PAIRS = TILES // 2
PT = 2 * P
KC = DIM // 128
BASES, RELS = 30, 2
HEADS, HD, FEATS = 8, 64, 256
HID = 4 * DIM
HC = HID // 128
GROUPS = EDGES // P
CELLS = RELS * NODES * NODES
COLT = RELS * TILES
NORM = HD ** -0.25
EPS_K = 1e-4
EPS_LN = 1e-5
PKH, NKEYS, TOPK, HALF = 8, 256, 8, 64
SLOTS = PKH * TOPK
RING = 16
ROUNDS = SLOTS // RING
HOLD = 8
MAGIC = float(0x5F3759DF)


def build(nc, a, out):
    with ExitStack() as ctx:
        def sb(name, shape, dt=F32):
            return ctx.enter_context(nc.sbuf_tensor(name, shape, dt))

        def sem(name):
            return ctx.enter_context(nc.semaphore(name))

        def dram(name, shape, dt=F32):
            return nc.dram_tensor(name, shape, dt, kind="Internal").ap()

        adj = dram("adj", [CELLS + 128, 1])
        cells_t = dram("cells_t", [GROUPS, P])
        xn_d = dram("xn_d", [NODES, DIM])
        res_d = dram("res_d", [NODES, DIM])
        adj_zero = adj[0:CELLS, :].rearrange("(z p w) o -> z p (w o)", z=5, p=P)
        adj_2d = adj[0:CELLS, :].rearrange("(k r) o -> k (r o)", r=NODES)

        def tok(ap):
            return ap.rearrange("(t p) d -> p t d", p=P)

        h = sb("h", [P, TILES, DIM])
        ident = sb("ident", [128, 128])
        ones = sb("ones", [HEADS, P])
        zeros = sb("zeros", [128, 128])
        headsel = sb("headsel", [128, KC, HEADS])
        att_b = sb("att_b", [128, 2, RELS * BASES])
        wreg = sb("wreg", [128, 4, 4 * DIM])
        projbd = sb("projbd", [128, 2 * FEATS])
        biasb = sb("biasb", [P, 2, DIM])
        cols = sb("cols", [128, 64])
        big = sb("big", [128, 20480])
        qv = sb("qv", [128, 10200])
        stage = sb("stage", [128, 5120])
        ctx_flat = sb("ctx_flat", [128, 2 * HEADS * (HD + 1)])
        ctx_sb = ctx_flat[:, :].rearrange("p (u d) -> p u d", u=2 * HEADS)
        st6 = sb("st6", [P, TILES, 6])
        mv = sb("mv", [P, TILES, 2])
        rs = sb("rs", [P, 4, TILES])
        small = sb("small", [P, 408])
        psum = [ctx.enter_context(nc.psum_tensor(f"bank{i}", [128, 512], F32)) for i in range(8)]

        def view(region, at, shape, parts=128):
            n = 1
            for s in shape:
                n *= s
            v = region[0:parts, at:at + n]
            if len(shape) == 2:
                v = v.rearrange("p (a b) -> p a b", a=shape[0])
            if len(shape) == 3:
                v = v.rearrange("p (a b c) -> p a b c", a=shape[0], b=shape[1])
            return v

        c_g1, c_b1, c_g2, c_b2, c_bq, c_bk = (cols[:, 4 * i:4 * i + 4] for i in range(6))
        c_h1 = cols[:, 24:24 + HC]
        c_gate = cols[:, 40:48].rearrange("p (k r) -> p k r", k=KC)
        c_bqf = cols[:, 48:56]
        b_v, b_o = (biasb[:, i, :] for i in range(2))
        b_2 = b_v

        zst = view(stage, 0, [2, DIM], P)
        y_t = view(stage, 1024, [KC, PT])
        k_t = view(stage, 2024, [KC, PT])
        sq = view(stage, 3024, [2, KC, PT])
        kfeat = view(stage, 0, [2, HEADS * FEATS], P)
        q_st = view(stage, 0, [KC, PT])
        qfeat = view(stage, 1000, [2, DIM], P)
        qfeat_t = view(stage, 2024, [2, 4 * P])
        o_sb = view(stage, 3024, [2, DIM], P)
        o_t = view(stage, 4048, [2, 4 * P])
        kdash = view(big, 0, [TILES, HEADS * FEATS], P)
        q_t = view(qv, 0, [KC, NODES])
        v_aug = qv[0:P, 5000:10200].rearrange("p (t h d) -> p t h d", t=TILES, h=HEADS)
        diag = small[:, 0:160].rearrange("p (t s h) -> p t s h", t=TILES, s=2)
        kmax = small[:, 160:240].rearrange("p (t h) -> p t h", t=TILES)
        kmax_all = small[:, 240:248]
        kneg = small[:, 250:330].rearrange("p (t h) -> p t h", t=TILES)
        qmax = small[:, 330:334].rearrange("p (j s) -> p j s", j=2)
        qneg = small[:, 334:338].rearrange("p (j s) -> p j s", j=2)
        rden = small[:, 340:356].rearrange("p (j h) -> p j h", j=2)
        kmax_t = small[0:8, 360:361]
        kmax_d = small[0:8, 364:372]
        w1_sb = view(big, 0, [KC, HID])
        w2_sb = view(big, 8192, [HC, DIM])
        act_t = view(big, 16384, [HC, PT])
        wrel = qv[:, 0:8192].rearrange("p (l r k) -> p l r k", l=2, r=2)
        zrel = view(big, 0, [COLT, DIM], P)
        xroot = view(big, 10240, [TILES, DIM], P)
        x1 = view(big, 15360, [TILES, DIM], P)
        wflat = wreg[:, :, :].rearrange("p a b -> p (a b)")
        slab = wflat[0:P, 0:5000].rearrange("p (s c r) -> p s c r", s=2, c=COLT)
        root_sb = wflat[:, 5120:7168].rearrange("p (k n) -> p k n", k=KC)
        gx = view(stage, 0, [2, DIM], P)
        gx_t = view(stage, 1024, [2, 4 * P])
        gate = small[:, 400:404].rearrange("p (j r) -> p j r", j=2)
        wqf = view(big, 0, [KC, PKH * 128])
        ring_dn = view(big, 4096, [RING, DIM], P)
        ring_up = view(big, 12288, [RING, DIM], P)
        keybd = wflat[:, 0:4096].rearrange("p (h n) -> p h n", h=PKH)
        xl = view(qv, 0, [DIM], P)
        dot_scr = view(qv, 512, [DIM], P)
        acc = view(qv, 1024, [DIM], P)
        xl_t = view(qv, 1536, [4 * P])
        pq_t = view(qv, 2048, [PKH, P])
        top_v = view(qv, 3072, [PKH, 2, TOPK], P)
        top_i = qv[0:P, 3200:3328].bitcast(U32).rearrange("p (h s k) -> p h s k", h=PKH, s=2)
        top_f = view(qv, 3328, [PKH, 2, TOPK], P)
        sums = view(qv, 3456, [PKH, TOPK * TOPK], P)
        best_v = view(qv, 3968, [PKH, TOPK], P)
        best_i = qv[0:P, 4032:4096].bitcast(U32).rearrange("p (h k) -> p h k", h=PKH)
        best_hi = qv[0:P, 4096:4160].bitcast(U32)
        best_lo = qv[0:P, 4160:4224].bitcast(U32)
        hi_f = view(qv, 4224, [PKH * TOPK], P)
        lo_f = view(qv, 4288, [PKH * TOPK], P)
        pick = view(qv, 4352, [PKH, TOPK, TOPK], P)
        pick_a = view(qv, 4864, [SLOTS], P)
        pick_b = view(qv, 4928, [SLOTS], P)
        slot_f = view(qv, 4992, [SLOTS], P)
        slots = qv[0:P, 5056:5120].bitcast(I32)
        probs = view(qv, 5120, [PKH, TOPK], P)
        prob_s = view(qv, 5184, [PKH], P)
        inner = view(qv, 5192, [SLOTS], P)
        vals = view(qv, 5256, [SLOTS], P)
        idx_dn = qv[0:P, 5320:5336].bitcast(I32)
        idx_up = qv[0:P, 5336:5352].bitcast(I32)
        dots = view(qv, 5352, [RING], P)
        wts = view(qv, 5368, [RING], P)
        iota8 = view(qv, 5384, [TOPK], P)
        iota8_u = qv[0:P, 5392:5400].bitcast(I32)

        s_xin = sem("x_loaded")
        s_const = sem("constants_made")
        s_edge = sem("edges_loaded")
        s_cell = sem("cells_step")
        s_cellp = sem("cells_transposed")
        s_cellsb = sem("cells_t_copied")
        s_cellw = sem("cells_t_written")
        s_cellb = sem("cells_broadcast")
        s_code = sem("edge_code_made")
        s_idx = sem("edge_index_made")
        s_zbuf = sem("zeros_made")
        s_adjz = sem("adjacency_zeroed")
        s_stg = sem("group_index_staged")
        s_adj = sem("group_added")
        s_ln = sem("ln0_step")
        s_xnw = sem("xn_written")
        s_att = sem("att_loaded")

        block = ctx.enter_context(nc.Block())

        cellb = view(big, 0, [GROUPS, P], P)
        e_raw = qv[0:P, 0:480].bitcast(I32).rearrange("p (s g) -> p s g", s=3)
        e_f = view(qv, 480, [3, GROUPS], P)
        cell = view(qv, 960, [GROUPS], P)
        code = view(qv, 1120, [GROUPS], P)
        flag = view(qv, 1280, [GROUPS], P)
        trash = view(qv, 1440, [GROUPS], P)
        wmask = view(qv, 1600, [P], P)
        cell_ts = view(qv, 1856, [2, P])
        zbuf = view(qv, 2200, [5000], P)
        e_idx = sb("e_idx", [P, GROUPS], I32)
        e_cnt = sb("e_cnt", [P, GROUPS])
        g_idx = sb("g_idx", [P, 1], I32)
        g_cnt = sb("g_cnt", [P, 1])

        tick = sb("tick", [1, 12 + 2 + 4 * SLOTS // HOLD])
        holds = [0, 0]

        def hold_dve():
            holds[0] = (holds[0] + 1) % 12
            nc.vector.memset(tick[:, holds[0]:holds[0] + 1], 0.0)

        def hold_pool():
            holds[1] += 1
            return nc.gpsimd.tensor_tensor(tick[:, 11 + holds[1]:12 + holds[1]], ones[0:1, 0:1], ones[0:1, 0:1], ALU.add)

        def rsqrt(dve, s, n, src, c0, w):
            v, y, t = (rs[:, k, c0:c0 + w] for k in (1, 0, 2))
            yi, vi = y.bitcast(I32), v.bitcast(I32)
            nc.vector.tensor_scalar(v, src, EPS_LN, None, ALU.add).then_inc(s, 1)
            dve.wait_ge(s, n + 1)
            nc.vector.tensor_scalar(yi, vi, -0.5, MAGIC, ALU.mult, ALU.add).then_inc(s, 1)
            n += 2
            for _ in range(4):
                dve.wait_ge(s, n)
                nc.vector.tensor_tensor(t, y, y, ALU.mult).then_inc(s, 1)
                dve.wait_ge(s, n + 1)
                nc.vector.tensor_tensor(t, t, v, ALU.mult).then_inc(s, 1)
                dve.wait_ge(s, n + 2)
                nc.vector.tensor_scalar(t, t, -0.5, 1.5, ALU.mult, ALU.add).then_inc(s, 1)
                dve.wait_ge(s, n + 3)
                nc.vector.tensor_tensor(y, y, t, ALU.mult).then_inc(s, 1)
                n += 4
            return n
        RSQ = 18
        LN0_DONE = 3 * TILES + RSQ

        def setup_pool():
            nc.gpsimd.memset(ident[:, :], 0.0).then_inc(s_const, 1)
            nc.gpsimd.memset(ones[:, :], 1.0).then_inc(s_const, 1)
            nc.gpsimd.memset(zeros[:, :], 0.0).then_inc(s_const, 1)
            nc.gpsimd.memset(headsel[:, :, :], 0.0).then_inc(s_const, 1)
            nc.gpsimd.memset(wmask, 257.0).then_inc(s_const, 1)
            nc.gpsimd.memset(zbuf, 0.0).then_inc(s_zbuf, 1)
            nc.gpsimd.iota(trash.bitcast(I32), pattern=[[0, GROUPS]], base=CELLS, channel_multiplier=1).then_inc(s_const, 1)
            nc.gpsimd.wait_ge(s_const, 6)
            nc.gpsimd.affine_select(out=ident[:, :], in_=ident[:, :], compare_op=ALU.not_equal, fill=1.0, base=0,
                                    pattern=[[-1, 128]], channel_multiplier=1).then_inc(s_const, 1)
            nc.gpsimd.affine_select(out=wmask, in_=wmask, compare_op=ALU.is_gt, fill=1.0, base=0,
                                    pattern=[[-1, P]], channel_multiplier=1).then_inc(s_const, 1)
            nc.gpsimd.wait_ge(s_const, 8)
            for c in range(KC):
                for s in range(2):
                    nc.gpsimd.memset(headsel[64 * s:64 * s + 64, c, 2 * c + s:2 * c + s + 1], 1.0).then_inc(s_const, 1)
        CONSTS = 8 + 2 * KC

        def adjacency_pool(pool):
            pool.wait_ge(s_idx, 4)
            pool.wait_ge(s_adjz, 5 * 16)

            def add_group(g):
                nc.gpsimd.tensor_copy(g_idx[:, :], e_idx[:, ds(g, 1)]).then_inc(s_stg, 1)
                nc.gpsimd.tensor_copy(g_cnt[:, :], e_cnt[:, ds(g, 1)]).then_inc(s_stg, 1)
                pool.wait_ge(s_stg, g * 2 + 2)
                hold_pool()
                nc.gpsimd.indirect_dma_start(
                    out=adj, out_offset=bass.IndirectOffsetOnAxis(ap=g_idx[:, :], axis=0), in_=g_cnt[:, :],
                    in_offset=None, bounds_check=CELLS + 127, oob_is_err=True, compute_op=ALU.add).then_inc(s_adj, 16)

            add_group(0)
            with pool.Fori(1, GROUPS) as g:
                pool.wait_ge(s_adj, g * 16)
                add_group(g)

        def setup_sp(sp):
            sp.dma_start(h[:, :, :], tok(a["x"])).then_inc(s_xin, 16)
            for n, name in enumerate(("src", "dst", "edge_type_2")):
                sp.dma_start(e_raw[:, n, :], a[name].rearrange("(p g) -> p g", p=P)).then_inc(s_edge, 16)
            sp.dma_start(att_b[:, 0, :], a["L0_gnn_att1"].rearrange("r b -> (r b)").partition_broadcast(128)).then_inc(s_att, 16)
            sp.dma_start(att_b[:, 1, :], a["L0_gnn_att2"].rearrange("r b -> (r b)").partition_broadcast(128)).then_inc(s_att, 16)
            sp.wait_ge(s_zbuf, 1)
            for n in range(5):
                sp.dma_start(adj_zero[n], zbuf).then_inc(s_adjz, 16)
            sp.wait_ge(s_cellsb, 2)
            sp.dma_start(cells_t[0:128, :], cell_ts[:, 0, :]).then_inc(s_cellw, 16)
            sp.dma_start(cells_t[128:GROUPS, :], cell_ts[0:GROUPS - 128, 1, :]).then_inc(s_cellw, 16)
            sp.wait_ge(s_cellw, 32)
            sp.dma_start(cellb, cells_t.rearrange("g p -> (g p)").partition_broadcast(P).rearrange("q (g p) -> q g p", g=GROUPS)).then_inc(s_cellb, 16)
            sp.wait_ge(s_ln, LN0_DONE)
            sp.dma_start(tok(xn_d), h[:, :, :]).then_inc(s_xnw, 16)

        def setup_dve(dve):
            dve.wait_ge(s_edge, 48)
            nc.vector.tensor_copy(e_f, e_raw).then_inc(s_cell, 1)
            dve.wait_ge(s_cell, 1)
            nc.vector.tensor_scalar(e_f[:, 2, :], e_f[:, 2, :], 0.0, float(NODES), ALU.not_equal, ALU.mult).then_inc(s_cell, 1)
            dve.wait_ge(s_cell, 2)
            nc.vector.tensor_tensor(e_f[:, 2, :], e_f[:, 2, :], e_f[:, 1, :], ALU.add).then_inc(s_cell, 1)
            dve.wait_ge(s_cell, 3)
            nc.vector.scalar_tensor_tensor(cell, e_f[:, 2, :], float(NODES), e_f[:, 0, :], ALU.mult, ALU.add).then_inc(s_cell, 1)
            dve.wait_ge(s_cellp, 1)
            nc.vector.tensor_copy(cell_ts[:, 0, :], psum[0][:, 0:P]).then_inc(s_cellsb, 1)
            nc.vector.tensor_copy(cell_ts[0:GROUPS - 128, 1, :], psum[0][0:GROUPS - 128, 128:128 + P]).then_inc(s_cellsb, 1)
            dve.wait_ge(s_xin, 16)
            for t in range(TILES):
                nc.vector.bn_stats(st6[:, t, :], h[:, t, :]).then_inc(s_ln, 1)
            dve.wait_ge(s_ln, TILES)
            for t in range(TILES):
                nc.vector.bn_aggr(mv[:, t, :], st6[:, t, :]).then_inc(s_ln, 1)
            dve.wait_ge(s_ln, 2 * TILES)
            rsqrt(dve, s_ln, 2 * TILES, mv[:, :, 1], 0, TILES)
            dve.wait_ge(s_ln, 2 * TILES + RSQ)
            for t in range(TILES):
                nc.vector.tensor_scalar(h[:, t, :], h[:, t, :], mv[:, t, 0:1], rs[:, 0, t:t + 1], ALU.subtract, ALU.mult).then_inc(s_ln, 1)
            dve.wait_ge(s_const, CONSTS)
            dve.wait_ge(s_cellb, 16)
            with dve.Fori(0, GROUPS) as g:
                nc.vector.scalar_tensor_tensor(cellb[:, ds(g, 1), :].rearrange("p a b -> p (a b)"), cellb[:, ds(g, 1), :].rearrange("p a b -> p (a b)"), cell[:, ds(g, 1)], wmask,
                                               ALU.is_equal, ALU.mult, accum_out=code[:, ds(g, 1)]).then_inc(s_code, 1)
            dve.wait_ge(s_code, GROUPS)
            nc.vector.tensor_copy(e_cnt[:, :], code).then_inc(s_idx, 1)
            nc.vector.tensor_scalar(flag, code, 256.0, None, ALU.is_ge).then_inc(s_cell, 1)
            nc.vector.tensor_copy(trash, trash.bitcast(I32)).then_inc(s_cell, 1)
            dve.wait_ge(s_cell, 6)
            nc.vector.tensor_tensor(trash, trash, cell, ALU.subtract).then_inc(s_idx, 1)
            dve.wait_ge(s_idx, 2)
            nc.vector.tensor_tensor(trash, trash, flag, ALU.mult).then_inc(s_idx, 1)
            dve.wait_ge(s_idx, 3)
            nc.vector.tensor_tensor(e_idx[:, :], trash, cell, ALU.add).then_inc(s_idx, 1)

        def setup_pe(pe):
            pe.wait_ge(s_const, CONSTS)
            pe.wait_ge(s_cell, 4)
            nc.tensor.transpose(psum[0][:, 0:P], cell[:, 0:128], ident[0:P, 0:P])
            nc.tensor.transpose(psum[0][0:GROUPS - 128, 128:128 + P], cell[:, 128:GROUPS], ident[0:P, 0:P]).then_inc(s_cellp, 1)

        ADDS = dict(w=13 * 16, pj=32, pjT=1, pjS=4, stat=1 + 2 * TILES + RSQ, z=TILES, yT_pe=KC * PAIRS, yT=KC * PAIRS, q_pe=KC * PAIRS,
                    q=KC * PAIRS, sq=2 * KC * PAIRS, k=KC * PAIRS, k_pe=KC * PAIRS, v_pe=TILES, v=TILES, dg_pe=PAIRS, dg=PAIRS,
                    kd_pe=4 * TILES, kmx=4 * TILES, kd=4 * TILES, gmx=5, gmx_pe=2, kneg=1, kx=TILES, kf=TILES, ctx_pe=TILES, ctx=4,
                    qs=PAIRS, qd_pe=4 * TILES, qm=4 * TILES, qn=4 * TILES, qx=4 * TILES, qT_pe=4 * TILES, qT=4 * TILES, o_pe=TILES,
                    rd=2 * TILES, o=2 * TILES, oT_pe=TILES, oT=TILES, at_pe=TILES, hat=2 * TILES, mw=48, ln2=(4 + RSQ) * PAIRS,
                    z2=TILES, y2_pe=KC * PAIRS, y2=KC * PAIRS, f1_pe=HC * PAIRS, f1=HC * PAIRS, f2_pe=TILES, hf=2 * TILES)
        m = {name: sem("mix_" + name) for name in ADDS}
        s_comb = sem("bases_added")
        s_comb0 = sem("relation_sums_zeroed")
        s_basis = [sem(f"basis_ring_{n}") for n in range(4)]
        proj_st = ctx_flat[:, 0:256].rearrange("p (k d) -> p k d", k=2)
        W_LOADS = 13 * 16
        BLOCKS = 2 * BASES // PAIRS
        BRING = 4

        def sq1(ap):
            return ap.rearrange("p a b -> p (a b)")

        def mix_loads_sp(sp, l):
            if l == 1:
                sp.wait_ge(g_sem[1]["out"], OUT_DONE)
                sp.wait_ge(m["hf"], 2 + 2 * TILES)
            for n, name in enumerate(("Wq", "Wk", "Wv", "Wo")):
                sp.dma_start(wreg[:, n, :].rearrange("p (k n) -> p k n", k=KC),
                             a["L0_mix_" + name][l].rearrange("(k p) n -> p k n", p=128)).then_inc(m["w"], 16)
            for c, name in ((c_g1, "ln1_g"), (c_b1, "ln1_b"), (c_g2, "ln2_g"), (c_b2, "ln2_b"), (c_bq, "bq"), (c_bk, "bk"), (c_h1, "b1")):
                sp.dma_start(c, a["L0_mix_" + name][l].rearrange("(k p) -> p k", p=128), allow_slow_non_contiguous=True).then_inc(m["w"], 16)
            for b, name in ((b_v, "bv"), (b_o, "bo")):
                sp.dma_start(b, a["L0_mix_" + name][l].partition_broadcast(P)).then_inc(m["w"], 16)
            if l == 1:
                sp.wait_ge(m["pjT"], 1)
            for s in range(2):
                sp.dma_start(proj_st[:, :, 64 * s:64 * s + 64], a["L0_mix_proj"][l].rearrange("(k p) d -> p k d", p=128)).then_inc(m["pj"], 16)

        def mlp_loads_sp(sp, l):
            sp.wait_ge(m["ctx"], l * ADDS["ctx"] + 4)
            sp.dma_start(w1_sb, a["L0_mix_W1"][l].rearrange("(k p) n -> p k n", p=128)).then_inc(m["mw"], 16)
            sp.dma_start(w2_sb, a["L0_mix_W2"][l].rearrange("(k p) n -> p k n", p=128)).then_inc(m["mw"], 16)
            sp.dma_start(b_2, a["L0_mix_b2"][l].partition_broadcast(P)).then_inc(m["mw"], 16)

        def bases_sp(sp, l=0):
            sp.wait_ge(m["hat"], 2 + 2 * TILES)
            sp.sem_inc(s_comb, 2 * BRING)
            with sp.Fori(0, PAIRS) as i:
                for n in range(BLOCKS):
                    gl, b = n // (BLOCKS // 2), n % (BLOCKS // 2)
                    sp.wait_ge(s_comb, i * (2 * BLOCKS) + 2 * n + 2)
                    sp.dma_start(wreg[:, n % BRING, :].rearrange("p (k n) -> p k n", k=KC),
                                 a[f"L0_gnn_basis{gl + 1}"][ds(i * (BLOCKS // 2) + b, 1), :, :].rearrange("o (k p) n -> p (o k) n", p=128)
                                 ).then_inc(s_basis[n % BRING], 16)

        def attn1_dve(dve, l):
            dve.wait_ge(m["pjT"], l * ADDS["pjT"] + 1)
            for s in range(2):
                rows = slice(64 * s, 64 * s + 64)
                nc.vector.memset(projbd[rows, FEATS * (1 - s):FEATS * (2 - s)], 0.0).then_inc(m["pjS"], 1)
                nc.vector.tensor_scalar(projbd[rows, FEATS * s:FEATS * s + FEATS], psum[7][rows, 0:FEATS], NORM, None,
                                        ALU.mult).then_inc(m["pjS"], 1)
            if l == 1:
                dve.wait_ge(g_sem[1]["z"], 4 + 2 * TILES)
                dve.wait_ge(g_sem[1]["st"], 16 + 16 * PAIRS)
            else:
                dve.wait_ge(s_adjz, 5 * 16)
            nc.vector.memset(v_aug[:, :, :, HD:HD + 1].rearrange("p t h o -> p (t h) o"), 1.0).then_inc(m["stat"], 1)
            for t in range(TILES):
                nc.vector.bn_stats(st6[:, t, :], h[:, t, :]).then_inc(m["stat"], 1)
            dve.wait_ge(m["stat"], l * ADDS["stat"] + 1 + TILES)
            for t in range(TILES):
                nc.vector.bn_aggr(mv[:, t, :], st6[:, t, :]).then_inc(m["stat"], 1)
            dve.wait_ge(m["stat"], l * ADDS["stat"] + 1 + 2 * TILES)
            n = rsqrt(dve, m["stat"], l * ADDS["stat"] + 1 + 2 * TILES, mv[:, :, 1], 0, TILES)
            dve.wait_ge(m["stat"], n)
            dve.wait_ge(m["w"], l * ADDS["w"] + W_LOADS)
            if l == 0:
                dve.sem_inc(m["yT_pe"], KC)
            with dve.Fori(0, PAIRS) as i:
                dve.wait_ge(m["yT_pe"], l * ADDS["yT_pe"] + i * KC + KC)
                for j in range(2):
                    nc.vector.tensor_scalar(zst[:, j, :], sq1(h[:, ds(i * 2 + j, 1), :]), mv[:, ds(i * 2 + j, 1), 0:1].rearrange("p a b -> p (a b)"),
                                            rs[:, 0, ds(i * 2 + j, 1)], ALU.subtract, ALU.mult).then_inc(m["z"], 1)
                for c in range(KC):
                    dve.wait_ge(m["k_pe"], l * ADDS["k_pe"] + i * KC + c + 1)
                    nc.vector.tensor_scalar(k_t[:, c, :], psum[4 + c % 2][:, 0:PT], c_bk[:, c:c + 1], None, ALU.add).then_inc(m["k"], 1)
                for j in range(2):
                    dve.wait_ge(m["v_pe"], l * ADDS["v_pe"] + i * 2 + j + 1)
                    nc.vector.tensor_tensor(v_aug[:, ds(i * 2 + j, 1), :, 0:HD].rearrange("p o h d -> p (o h) d"),
                                            psum[6 + j][0:P, :].rearrange("p (h d) -> p h d", h=HEADS),
                                            b_v.rearrange("p (h d) -> p h d", h=HEADS), ALU.add).then_inc(m["v"], 1)
                dve.wait_ge(m["dg_pe"], l * ADDS["dg_pe"] + i + 1)
                nc.vector.tensor_scalar(diag[:, ds(i * 2, 2), :, :].rearrange("p t s h -> p (t s h)"), psum[0][0:P, 0:32],
                                        0.5 * NORM * NORM, None, ALU.mult).then_inc(m["dg"], 1)
                for n in range(8):
                    j, c = n // 4, n % 4
                    dve.wait_ge(m["kd_pe"], l * ADDS["kd_pe"] + i * 8 + n + 1)
                    nc.vector.tensor_reduce(sq1(kmax[:, ds(i * 2 + j, 1), 2 * c:2 * c + 2]),
                                            psum[6 + n % 2][0:P, :].rearrange("p (s m) -> p s m", s=2), AX, ALU.max).then_inc(m["kmx"], 1)
            dve.wait_ge(m["kmx"], l * ADDS["kmx"] + 4 * TILES)
            nc.vector.tensor_reduce(kmax_all, kmax.rearrange("p t h -> p h t"), AX, ALU.max).then_inc(m["gmx"], 1)
            dve.wait_ge(m["gmx_pe"], l * ADDS["gmx_pe"] + 1)
            nc.vector.tensor_reduce(kmax_t, psum[0][0:HEADS, 0:P], AX, ALU.max).then_inc(m["gmx"], 1)
            dve.wait_ge(m["gmx"], l * ADDS["gmx"] + 2)
            nc.vector.tensor_scalar(kmax_d, ident[0:HEADS, 0:HEADS], kmax_t, None, ALU.mult).then_inc(m["gmx"], 1)
            dve.wait_ge(m["gmx_pe"], l * ADDS["gmx_pe"] + 2)
            nc.vector.tensor_copy(kmax_all, psum[1][0:P, 0:HEADS]).then_inc(m["gmx"], 1)
            dve.wait_ge(m["gmx"], l * ADDS["gmx"] + 4)
            dve.wait_ge(m["dg"], l * ADDS["dg"] + PAIRS)
            nc.vector.tensor_tensor(kneg, diag[:, :, 1, :], kmax_all.unsqueeze(1).to_broadcast([P, TILES, HEADS]), ALU.add).then_inc(m["gmx"], 1)
            dve.wait_ge(m["gmx"], l * ADDS["gmx"] + 5)
            nc.vector.tensor_scalar(kneg, kneg, -1.0, None, ALU.mult).then_inc(m["kneg"], 1)

        def attn1_pe(pe, l):
            pe.wait_ge(m["pj"], l * ADDS["pj"] + 32)
            if l == 0:
                pe.wait_ge(s_const, CONSTS)
            else:
                pe.wait_ge(g_sem[1]["out"], OUT_DONE)
            for k in range(2):
                mm = nc.tensor.transpose(psum[7][:, 128 * k:128 * k + 128], proj_st[:, k, :], ident[:, :])
            mm.then_inc(m["pjT"], 1)
            pe.wait_ge(m["w"], l * ADDS["w"] + W_LOADS)
            pe.wait_ge(m["pjS"], l * ADDS["pjS"] + 4)
            if l == 0:
                pe.sem_inc(m["dg"], 1)
            if l == 0:
                pe.sem_inc(m["sq"], 4)
            if l == 0:
                pe.sem_inc(m["k"], 2)
            if l == 0:
                pe.sem_inc(m["kd"], 2)
            with pe.Fori(0, PAIRS) as i:
                pe.wait_ge(m["z"], l * ADDS["z"] + i * 2 + 2)
                pe.wait_ge(m["dg"], l * ADDS["dg"] + i + 1)
                for c in range(KC):
                    for j in range(2):
                        mm = nc.tensor.transpose(psum[c // 2][:, 256 * (c % 2) + P * j:256 * (c % 2) + P * j + P],
                                                 zst[:, j, 128 * c:128 * c + 128], ident[0:P, 0:P])
                    mm.then_inc(m["yT_pe"], 1)
                pe.wait_ge(m["yT"], l * ADDS["yT"] + i * KC + KC)
                for c in range(KC):
                    pe.wait_ge(m["sq"], l * ADDS["sq"] + i * KC * 2 + 2 * c + 1)
                    for k in range(KC):
                        mm = nc.tensor.matmul(psum[2 + c % 2][:, 0:PT], wreg[:, 0, 512 * k + 128 * c:512 * k + 128 * c + 128],
                                              y_t[:, k, :], start=(k == 0), stop=(k == KC - 1))
                    mm.then_inc(m["q_pe"], 1)
                    pe.wait_ge(m["k"], l * ADDS["k"] + i * KC + c + 1)
                    for k in range(KC):
                        mm = nc.tensor.matmul(psum[4 + c % 2][:, 0:PT], wreg[:, 1, 512 * k + 128 * c:512 * k + 128 * c + 128],
                                              y_t[:, k, :], start=(k == 0), stop=(k == KC - 1))
                    mm.then_inc(m["k_pe"], 1)
                for j in range(2):
                    pe.wait_ge(m["kd"], l * ADDS["kd"] + i * 8 + j + 1)
                    for k in range(KC):
                        mm = nc.tensor.matmul(psum[6 + j][0:P, :], y_t[:, k, P * j:P * j + P], wreg[:, 2, 512 * k:512 * k + 512],
                                              start=(k == 0), stop=(k == KC - 1))
                    mm.then_inc(m["v_pe"], 1)
                pe.wait_ge(m["sq"], l * ADDS["sq"] + i * KC * 2 + 2 * KC + 4)
                for j in range(2):
                    for s in range(2):
                        for c in range(KC):
                            mm = nc.tensor.matmul(psum[0][0:P, 16 * j + 8 * s:16 * j + 8 * s + 8], sq[:, s, c, P * j:P * j + P],
                                                  headsel[:, c, :], start=(c == 0), stop=(c == KC - 1), skip_group_check=True)
                mm.then_inc(m["dg_pe"], 1)
                pe.wait_ge(m["v"], l * ADDS["v"] + i * 2 + 2)
                for n in range(8):
                    j, c = n // 4, n % 4
                    if n >= 2:
                        pe.wait_ge(m["kd"], l * ADDS["kd"] + i * 8 + n + 1)
                    nc.tensor.matmul(psum[6 + n % 2][0:P, :], k_t[:, c, P * j:P * j + P], projbd[:, :], start=True, stop=True).then_inc(m["kd_pe"], 1)
            pe.wait_ge(m["gmx"], l * ADDS["gmx"] + 1)
            pe.wait_ge(m["dg"], l * ADDS["dg"] + 1 + PAIRS)
            nc.tensor.transpose(psum[0][0:HEADS, 0:P], kmax_all, ident[0:P, 0:P]).then_inc(m["gmx_pe"], 1)
            pe.wait_ge(m["gmx"], l * ADDS["gmx"] + 3)
            nc.tensor.matmul(psum[1][0:P, 0:HEADS], ones[:, :], kmax_d, start=True, stop=True).then_inc(m["gmx_pe"], 1)

        def attn1_act(act, l):
            act.wait_ge(m["w"], l * ADDS["w"] + W_LOADS)
            if l == 0:
                act.wait_ge(s_idx, 4)
                act.wait_ge(s_adjz, 5 * 16)
            with act.Fori(0, PAIRS) as i:
                for c in range(KC):
                    act.wait_ge(m["yT_pe"], l * ADDS["yT_pe"] + i * KC + 2 * (c // 2) + 2 + KC)
                    nc.scalar.activation(y_t[:, c, :], psum[c // 2][:, 256 * (c % 2):256 * (c % 2) + PT], ACT.Identity,
                                         bias=c_b1[:, c:c + 1], scale=c_g1[:, c:c + 1]).then_inc(m["yT"], 1)
                for c in range(KC):
                    act.wait_ge(m["q_pe"], l * ADDS["q_pe"] + i * KC + c + 1)
                    nc.scalar.activation(q_t[:, c, ds(i * PT, PT)], psum[2 + c % 2][:, 0:PT], ACT.Identity,
                                         bias=c_bq[:, c:c + 1]).then_inc(m["q"], 1)
                    nc.scalar.activation(sq[:, 0, c, :], psum[2 + c % 2][:, 0:PT], ACT.Square, bias=c_bq[:, c:c + 1]).then_inc(m["sq"], 1)
                    act.wait_ge(m["k"], l * ADDS["k"] + i * KC + c + 3)
                    nc.scalar.activation(sq[:, 1, c, :], k_t[:, c, :], ACT.Square).then_inc(m["sq"], 1)
                for n in range(8):
                    j, c = n // 4, n % 4
                    act.wait_ge(m["kmx"], l * ADDS["kmx"] + i * 8 + n + 1)
                    nc.scalar.activation(sq1(kdash[:, ds(i * 2 + j, 1), 512 * c:512 * c + 512]), psum[6 + n % 2][0:P, :],
                                         ACT.Copy).then_inc(m["kd"], 1)

        def attn2_act(act, l):
            act.wait_ge(m["kneg"], l * ADDS["kneg"] + 1)
            act.wait_ge(m["kd"], l * ADDS["kd"] + 2 + 4 * TILES)
            if l == 0:
                act.sem_inc(m["ctx_pe"], 2)
            with act.Fori(0, PAIRS) as i:
                for j in range(2):
                    act.wait_ge(m["ctx_pe"], l * ADDS["ctx_pe"] + i * 2 + j + 1)
                    for hh in range(HEADS):
                        op = nc.scalar.activation(kfeat[:, j, FEATS * hh:FEATS * hh + FEATS],
                                                  sq1(kdash[:, ds(i * 2 + j, 1), FEATS * hh:FEATS * hh + FEATS]), ACT.Exp,
                                                  bias=sq1(kneg[:, ds(i * 2 + j, 1), hh:hh + 1]))
                    op.then_inc(m["kx"], 1)

        def attn2_dve(dve, l):
            with dve.Fori(0, PAIRS) as i:
                for j in range(2):
                    dve.wait_ge(m["kx"], l * ADDS["kx"] + i * 2 + j + 1)
                    nc.vector.tensor_scalar(kfeat[:, j, :], kfeat[:, j, :], EPS_K, None, ALU.add).then_inc(m["kf"], 1)
            dve.wait_ge(m["ctx_pe"], l * ADDS["ctx_pe"] + 2 + TILES)
            for b in range(4):
                nc.vector.tensor_copy(ctx_sb[:, 4 * b:4 * b + 4, :].rearrange("p u d -> p (u d)"), psum[b][:, 0:4 * (HD + 1)]).then_inc(m["ctx"], 1)

        def attn2_pe(pe, l):
            pe.wait_ge(m["gmx"], l * ADDS["gmx"] + 4)
            pe.wait_ge(m["sq"], l * ADDS["sq"] + 4 + 2 * KC * PAIRS)
            for b in range(4):
                nc.tensor.matmul(psum[b][:, 0:4 * (HD + 1)], zeros[:, :], wreg[:, 0, 0:4 * (HD + 1)], start=True, stop=False, skip_group_check=True)
            with pe.Fori(0, PAIRS) as i:
                for j in range(2):
                    pe.wait_ge(m["kf"], l * ADDS["kf"] + i * 2 + j + 1)
                    for u in range(2 * HEADS):
                        mm = nc.tensor.matmul(psum[u // 4][:, (HD + 1) * (u % 4):(HD + 1) * (u % 4 + 1)], kfeat[:, j, 128 * u:128 * u + 128],
                                              v_aug[:, ds(i * 2 + j, 1), u // 2, :].rearrange("p o d -> p (o d)"),
                                              start=False, stop=True, skip_group_check=True)
                    mm.then_inc(m["ctx_pe"], 1)

        STEPS = 2 * KC

        def attn3_dve(dve, l):
            dve.wait_ge(m["ctx_pe"], l * ADDS["ctx_pe"] + 2 + TILES)
            with dve.Fori(0, PAIRS) as i:
                nc.vector.tensor_copy(q_st, q_t[:, :, ds(i * PT, PT)]).then_inc(m["qs"], 1)

                def normalize(j):
                    dve.wait_ge(m["o_pe"], l * ADDS["o_pe"] + i * 2 + j + 1)
                    for b in range(2):
                        nc.vector.reciprocal(rden[:, j, 4 * b:4 * b + 4].unsqueeze(2),
                                             psum[4 + b][0:P, 0:4 * (HD + 1)].rearrange("p (h d) -> p h d", h=4)[:, :, HD:HD + 1]).then_inc(m["rd"], 1)
                    dve.wait_ge(m["rd"], l * ADDS["rd"] + i * 4 + 2 * j + 2)
                    for b in range(2):
                        nc.vector.tensor_tensor(o_sb[:, j, 256 * b:256 * b + 256].rearrange("p (h d) -> p h d", h=4),
                                                psum[4 + b][0:P, 0:4 * (HD + 1)].rearrange("p (h d) -> p h d", h=4)[:, :, 0:HD],
                                                rden[:, j, 4 * b:4 * b + 4].unsqueeze(2).to_broadcast([P, 4, HD]), ALU.mult).then_inc(m["o"], 1)

                def residual(j):
                    ht = sq1(h[:, ds(i * 2 + j, 1), :])
                    dve.wait_ge(m["at_pe"], l * ADDS["at_pe"] + i * 2 + j + 1)
                    nc.vector.tensor_tensor(ht, psum[7][0:P, :], ht, ALU.add).then_inc(m["hat"], 1)
                    dve.wait_ge(m["hat"], l * ADDS["hat"] + i * 4 + 2 * j + 3)
                    nc.vector.tensor_tensor(ht, ht, b_o, ALU.add).then_inc(m["hat"], 1)

                for n in range(STEPS + 1):
                    if n < STEPS:
                        j, c = n // KC, n % KC
                        dve.wait_ge(m["qd_pe"], l * ADDS["qd_pe"] + i * STEPS + n + 1)
                        nc.vector.tensor_reduce(qmax[:, n % 2, :], psum[n % 2][0:P, :].rearrange("p (s m) -> p s m", s=2), AX, ALU.max).then_inc(m["qm"], 1)
                        dve.wait_ge(m["qm"], l * ADDS["qm"] + i * STEPS + n + 1)
                        nc.vector.scalar_tensor_tensor(qneg[:, n % 2, :], qmax[:, n % 2, :], -1.0,
                                                       diag[:, ds(i * 2 + j, 1), 0, 2 * c:2 * c + 2].rearrange("p o s -> p (o s)"),
                                                       ALU.mult, ALU.subtract).then_inc(m["qn"], 1)
                    if n >= 1:
                        dve.wait_ge(m["qT_pe"], l * ADDS["qT_pe"] + i * STEPS + n + 2)
                        nc.vector.tensor_scalar(qfeat_t[:, (n - 1) % 2, :], psum[2 + (n - 1) % 2][:, 0:4 * P], EPS_K, None, ALU.add).then_inc(m["qT"], 1)
                    if n == 6:
                        normalize(0)
                residual(0)
                normalize(1)
                residual(1)

        def attn3_act(act, l):
            if l == 0:
                act.sem_inc(m["qT_pe"], 2)
            with act.Fori(0, PAIRS) as i:
                def turn(j):
                    act.wait_ge(m["oT_pe"], l * ADDS["oT_pe"] + i * 2 + j + 1)
                    nc.scalar.activation(o_t[:, j, :], psum[6][:, 0:4 * P], ACT.Copy).then_inc(m["oT"], 1)
                for n in range(STEPS):
                    act.wait_ge(m["qn"], l * ADDS["qn"] + i * STEPS + n + 1)
                    act.wait_ge(m["qT_pe"], l * ADDS["qT_pe"] + i * STEPS + n + 1)
                    for s in range(2):
                        op = nc.scalar.activation(qfeat[:, n % 2, FEATS * s:FEATS * s + FEATS], psum[n % 2][0:P, FEATS * s:FEATS * s + FEATS],
                                                  ACT.Exp, bias=qneg[:, n % 2, s:s + 1])
                    op.then_inc(m["qx"], 1)
                turn(0)
                turn(1)

        def attn3_pe(pe, l):
            pe.wait_ge(m["ctx"], l * ADDS["ctx"] + 4)
            if l == 0:
                pe.sem_inc(m["qx"], 2)
            if l == 0:
                pe.sem_inc(m["qT"], 2)
            if l == 0:
                pe.sem_inc(m["o"], 2)
            if l == 0:
                pe.sem_inc(m["oT"], 1)
            if l == 0:
                pe.sem_inc(m["hat"], 2)
            with pe.Fori(0, PAIRS) as i:
                pe.wait_ge(m["qs"], l * ADDS["qs"] + i + 1)

                def out_proj(j):
                    pe.wait_ge(m["o"], l * ADDS["o"] + i * 4 + 2 * j + 4)
                    pe.wait_ge(m["oT"], l * ADDS["oT"] + i * 2 + j + 1)
                    for k in range(KC):
                        mm = nc.tensor.transpose(psum[6][:, P * k:P * k + P], o_sb[:, j, 128 * k:128 * k + 128], ident[0:P, 0:P])
                    mm.then_inc(m["oT_pe"], 1)

                def out_mm(j):
                    pe.wait_ge(m["oT"], l * ADDS["oT"] + i * 2 + j + 2)
                    pe.wait_ge(m["hat"], l * ADDS["hat"] + i * 4 + 2 * j + 1)
                    for k in range(KC):
                        mm = nc.tensor.matmul(psum[7][0:P, :], o_t[:, j, P * k:P * k + P], wreg[:, 3, 512 * k:512 * k + 512],
                                              start=(k == 0), stop=(k == KC - 1))
                    mm.then_inc(m["at_pe"], 1)

                for n in range(STEPS + 2):
                    if n < STEPS:
                        j, c = n // KC, n % KC
                        pe.wait_ge(m["qx"], l * ADDS["qx"] + i * STEPS + n + 1)
                        nc.tensor.matmul(psum[n % 2][0:P, :], q_st[:, c, P * j:P * j + P], projbd[:, :], start=True, stop=True).then_inc(m["qd_pe"], 1)
                    if 1 <= n <= STEPS:
                        pe.wait_ge(m["qx"], l * ADDS["qx"] + i * STEPS + n + 2)
                        pe.wait_ge(m["qT"], l * ADDS["qT"] + i * STEPS + n)
                        for q in range(4):
                            mm = nc.tensor.transpose(psum[2 + (n - 1) % 2][:, P * q:P * q + P], qfeat[:, (n - 1) % 2, 128 * q:128 * q + 128], ident[0:P, 0:P])
                        mm.then_inc(m["qT_pe"], 1)
                    if n >= 2:
                        j, c = (n - 2) // KC, (n - 2) % KC
                        pe.wait_ge(m["qT"], l * ADDS["qT"] + i * STEPS + n + 1)
                        if c == 0:
                            pe.wait_ge(m["o"], l * ADDS["o"] + i * 4 + 2 * j + 2)
                        for s in range(2):
                            hh = 2 * c + s
                            for q in range(2):
                                mm = nc.tensor.matmul(psum[4 + hh // 4][0:P, (HD + 1) * (hh % 4):(HD + 1) * (hh % 4 + 1)],
                                                      qfeat_t[:, n % 2, P * (2 * s + q):P * (2 * s + q) + P], ctx_sb[:, 2 * hh + q, :],
                                                      start=(q == 0), stop=(q == 1), skip_group_check=True)
                        if c == KC - 1:
                            mm.then_inc(m["o_pe"], 1)
                out_proj(0)
                out_mm(0)
                out_proj(1)
                out_mm(1)

        LN2 = 4 + RSQ

        def mlp_dve(dve, l):
            if l == 0:
                dve.wait_ge(m["qs"], l * ADDS["qs"] + PAIRS)
                nc.vector.memset(qv[:, 0:8192], 0.0).then_inc(s_comb0, 1)
                dve.wait_ge(s_comb0, 1)
                dve.wait_ge(s_att, 32)
            dve.wait_ge(m["hat"], l * ADDS["hat"] + 2 + 2 * TILES)
            dve.wait_ge(m["mw"], l * ADDS["mw"] + 48)
            if l == 0:
                dve.sem_inc(m["y2_pe"], KC)
            with dve.Fori(0, PAIRS) as i:
                for j in range(2):
                    nc.vector.bn_stats(st6[:, j, :], sq1(h[:, ds(i * 2 + j, 1), :])).then_inc(m["ln2"], 1)
                dve.wait_ge(m["ln2"], l * ADDS["ln2"] + i * LN2 + 2)
                hold_dve()
                for j in range(2):
                    nc.vector.bn_aggr(mv[:, j, :], st6[:, j, :]).then_inc(m["ln2"], 1)
                dve.wait_ge(m["ln2"], l * ADDS["ln2"] + i * LN2 + 4)
                rsqrt(dve, m["ln2"], l * ADDS["ln2"] + i * LN2 + 4, mv[:, 0:2, 1], 0, 2)
                dve.wait_ge(m["ln2"], l * ADDS["ln2"] + i * LN2 + LN2)
                dve.wait_ge(m["y2_pe"], l * ADDS["y2_pe"] + i * KC + KC)
                for j in range(2):
                    nc.vector.tensor_scalar(zst[:, j, :], sq1(h[:, ds(i * 2 + j, 1), :]), mv[:, j, 0:1], rs[:, 0, j:j + 1],
                                            ALU.subtract, ALU.mult).then_inc(m["z2"], 1)
                if l == 0:
                    for n in range(BLOCKS):
                        gl, b = n // (BLOCKS // 2), n % (BLOCKS // 2)
                        dve.wait_ge(s_basis[n % BRING], i * (16 * BLOCKS // BRING) + 16 * (n // BRING) + 16)
                        dve.wait_ge(s_comb, i * (2 * BLOCKS) + 2 * n + 2 * BRING)
                        for r in range(RELS):
                            nc.vector.scalar_tensor_tensor(wrel[:, gl, r, :], wreg[:, n % BRING, :], att_b[:, gl, ds(i * (BLOCKS // 2) + (r * BASES + b), 1)],
                                                           wrel[:, gl, r, :], ALU.mult, ALU.add).then_inc(s_comb, 1)
                for j in range(2):
                    ht = sq1(h[:, ds(i * 2 + j, 1), :])
                    dve.wait_ge(m["f2_pe"], l * ADDS["f2_pe"] + i * 2 + j + 1)
                    nc.vector.tensor_tensor(ht, psum[6 + j][0:P, :], ht, ALU.add).then_inc(m["hf"], 1)
                    dve.wait_ge(m["hf"], l * ADDS["hf"] + i * 4 + 2 * j + 3)
                    nc.vector.tensor_tensor(ht, ht, b_2, ALU.add).then_inc(m["hf"], 1)
            dve.wait_ge(m["hf"], l * ADDS["hf"] + 2 + 2 * TILES)

        def mlp_pe(pe, l):
            pe.wait_ge(m["mw"], l * ADDS["mw"] + 48)
            pe.wait_ge(m["hat"], l * ADDS["hat"] + 2 + 2 * TILES)
            if l == 0:
                pe.sem_inc(m["f1"], 4)
            if l == 0:
                pe.sem_inc(m["hf"], 2)
            with pe.Fori(0, PAIRS) as i:
                pe.wait_ge(m["z2"], l * ADDS["z2"] + i * 2 + 2)
                for c in range(KC):
                    for j in range(2):
                        mm = nc.tensor.transpose(psum[c // 2][:, 256 * (c % 2) + P * j:256 * (c % 2) + P * j + P],
                                                 zst[:, j, 128 * c:128 * c + 128], ident[0:P, 0:P])
                    mm.then_inc(m["y2_pe"], 1)
                pe.wait_ge(m["y2"], l * ADDS["y2"] + i * KC + KC)
                for n in range(HC):
                    pe.wait_ge(m["f1"], l * ADDS["f1"] + i * HC + n + 1)
                    for k in range(KC):
                        mm = nc.tensor.matmul(psum[2 + n % 4][:, 0:PT], w1_sb[:, k, 128 * n:128 * n + 128], y_t[:, k, :],
                                              start=(k == 0), stop=(k == KC - 1))
                    mm.then_inc(m["f1_pe"], 1)
                pe.wait_ge(m["f1"], l * ADDS["f1"] + i * HC + HC + 4)
                pe.wait_ge(m["hf"], l * ADDS["hf"] + i * 4 + 2)
                for j in range(2):
                    for k in range(HC):
                        mm = nc.tensor.matmul(psum[6 + j][0:P, :], act_t[:, k, P * j:P * j + P], w2_sb[:, k, :],
                                              start=(k == 0), stop=(k == HC - 1))
                    mm.then_inc(m["f2_pe"], 1)

        def mlp_act(act, l):
            with act.Fori(0, PAIRS) as i:
                for c in range(KC):
                    act.wait_ge(m["y2_pe"], l * ADDS["y2_pe"] + i * KC + 2 * (c // 2) + 2 + KC)
                    nc.scalar.activation(y_t[:, c, :], psum[c // 2][:, 256 * (c % 2):256 * (c % 2) + PT], ACT.Identity,
                                         bias=c_b2[:, c:c + 1], scale=c_g2[:, c:c + 1]).then_inc(m["y2"], 1)
                for n in range(HC):
                    act.wait_ge(m["f1_pe"], l * ADDS["f1_pe"] + i * HC + n + 1)
                    nc.scalar.activation(act_t[:, n, :], psum[2 + n % 4][:, 0:PT], ACT.Gelu, bias=c_h1[:, n:n + 1]).then_inc(m["f1"], 1)

        g_names = "w x xT_pe xT gt_pe gt z_pe z r agg out xin st".split()
        g_sem = [{n: sem(f"gcn{gl}_{n}") for n in g_names} for gl in range(2)]
        s_slab = [[sem(f"gcn{gl}_slab_{j}") for j in range(2)] for gl in range(2)]
        OUT_DONE = 4 + 2 * TILES
        COMB_DONE = 2 * BRING + 2 * 2 * BASES
        b_g = b_v
        xin = view(stage, 2024, [2, DIM], P)

        def gcn_sp(sp, gl):
            g = g_sem[gl]
            if gl == 0:
                sp.wait_ge(s_comb, COMB_DONE)
                sp.wait_ge(s_adj, 16 * GROUPS)
                sp.wait_ge(m["hf"], 2 + 2 * TILES)
                sp.wait_ge(s_xnw, 16)
            else:
                sp.wait_ge(g_sem[0]["r"], 2 + TILES)
                sp.wait_ge(g_sem[0]["agg"], 2 + TILES)
            sp.dma_start(root_sb, a[f"L0_gnn_root{gl + 1}"].rearrange("(k p) n -> p k n", p=128)).then_inc(g["w"], 16)
            for r in range(RELS):
                sp.dma_start(c_gate[:, :, r], a[f"L0_gnn_gate_w{gl + 1}"][r].rearrange("(k p) o -> p (k o)", p=128), allow_slow_non_contiguous=True).then_inc(g["w"], 16)
            sp.dma_start(b_g, a[f"L0_gnn_bias{gl + 1}"].partition_broadcast(P)).then_inc(g["w"], 16)
            if gl == 0:
                with sp.Fori(0, PAIRS) as i:
                    sp.wait_ge(g["xT_pe"], i * 2 + 2)
                    sp.dma_start(gx, tok(xn_d)[:, ds(i * 2, 2), :]).then_inc(g["x"], 16)
            sp.sem_inc(g["agg"], 2)
            with sp.Fori(0, PAIRS) as i:
                for j in range(2):
                    sp.wait_ge(g["agg"], i * 2 + j + 1)
                    sp.dma_start(slab[:, j, :, :], adj_2d[:, ds(i * PT + j * P, P)].rearrange("(c p) r -> p c r", p=P)).then_inc(s_slab[gl][j], 16)
                if gl == 1:
                    sp.wait_ge(g["out"], i * 4 + 8)
                    sp.dma_start(tok(res_d)[:, ds(i * 2, 2), :], gx).then_inc(g["st"], 16)

        def gcn_x_act(act, gl):
            g = g_sem[gl]
            with act.Fori(0, PAIRS) as i:
                act.wait_ge(g["out"], i * 4 + 4)
                act.dma_start(xin, tok(a["x"])[:, ds(i * 2, 2), :]).then_inc(g["xin"], 16)

        def gcn_pe(pe, gl):
            g = g_sem[gl]
            pe.wait_ge(g["w"], 64)
            pe.wait_ge(m["hf"], 2 + 2 * TILES)
            pe.sem_inc(g["z"], 4)
            pe.sem_inc(g["r"], 2)
            with pe.Fori(0, PAIRS) as i:
                pe.wait_ge(g["x"], (i + 1) * (16 if gl == 0 else 1))
                for j in range(2):
                    pe.wait_ge(g["gt"], i * 2 + j + 1)
                    for k in range(KC):
                        mm = nc.tensor.transpose(psum[j][:, P * k:P * k + P], gx[:, j, 128 * k:128 * k + 128], ident[0:P, 0:P])
                    mm.then_inc(g["xT_pe"], 1)
                for j in range(2):
                    pe.wait_ge(g["xT"], i * 2 + j + 1)
                    for k in range(KC):
                        mm = nc.tensor.matmul(psum[j][0:P, 500:502], gx_t[:, j, P * k:P * k + P], c_gate[:, k, :], start=(k == 0), stop=(k == KC - 1))
                    mm.then_inc(g["gt_pe"], 1)
                    for r in range(RELS):
                        pe.wait_ge(g["z"], i * 4 + 2 * j + r + 1)
                        for k in range(KC):
                            mm = nc.tensor.matmul(psum[2 + 3 * j + r][0:P, :], gx_t[:, j, P * k:P * k + P], wrel[:, gl, r, 512 * k:512 * k + 512],
                                                  start=(k == 0), stop=(k == KC - 1))
                        mm.then_inc(g["z_pe"], 1)
                    pe.wait_ge(g["r"], i * 2 + j + 1)
                    for k in range(KC):
                        mm = nc.tensor.matmul(psum[4 + 3 * j][0:P, :], gx_t[:, j, P * k:P * k + P], root_sb[:, k, :], start=(k == 0), stop=(k == KC - 1))
                    mm.then_inc(g["z_pe"], 1)
            pe.wait_ge(g["z"], 4 + 2 * TILES)
            pe.wait_ge(g["gt"], 2 + TILES)
            pe.sem_inc(g["out"], 4)
            with pe.Fori(0, PAIRS) as i:
                for j in range(2):
                    pe.wait_ge(s_slab[gl][j], i * 16 + 16)
                    pe.wait_ge(g["out"], i * 4 + 2 * j + 1)
                    for c in range(COLT):
                        mm = nc.tensor.matmul(psum[j][0:P, :], slab[:, j, c, :], zrel[:, c, :], start=(c == 0), stop=(c == COLT - 1))
                    mm.then_inc(g["agg"], 1)

        def gcn_act(act, gl):
            g = g_sem[gl]
            act.sem_inc(g["gt"], 2)
            act.sem_inc(g["xT_pe"], 2)
            with act.Fori(0, PAIRS) as i:
                for j in range(2):
                    act.wait_ge(g["xT_pe"], i * 2 + j + 3)
                    nc.scalar.activation(gx_t[:, j, :], psum[j][:, 0:4 * P], ACT.Copy).then_inc(g["xT"], 1)
                for j in range(2):
                    act.wait_ge(g["gt_pe"], i * 2 + j + 1)
                    nc.scalar.activation(gate[:, j, :], psum[j][0:P, 500:502], ACT.Sigmoid).then_inc(g["gt"], 1)
                    act.wait_ge(g["gt"], i * 2 + j + 3)
                    for r in range(RELS):
                        act.wait_ge(g["z_pe"], i * 6 + 3 * j + r + 1)
                        nc.scalar.activation(sq1(zrel[:, ds(i * 2 + (j + r * TILES), 1), :]), psum[2 + 3 * j + r][0:P, :], ACT.Identity,
                                             scale=gate[:, j, r:r + 1]).then_inc(g["z"], 1)

        def gcn_dve(dve, gl):
            g = g_sem[gl]
            dve.wait_ge(g["w"], 64)
            dve.sem_inc(g["st"], 16)
            if gl == 1:
                dve.wait_ge(g_sem[0]["out"], OUT_DONE)
            with dve.Fori(0, PAIRS) as i:
                if gl == 1:
                    dve.wait_ge(g["xT_pe"], i * 2 + 2)
                    nc.vector.tensor_copy(gx, x1[:, ds(i * 2, 2), :]).then_inc(g["x"], 1)
                for j in range(2):
                    dve.wait_ge(g["z_pe"], i * 6 + 3 * j + 3)
                    nc.vector.tensor_tensor(sq1(xroot[:, ds(i * 2 + j, 1), :]), psum[4 + 3 * j][0:P, :], b_g, ALU.add).then_inc(g["r"], 1)
            with dve.Fori(0, PAIRS) as i:
                if gl == 1:
                    dve.wait_ge(g["st"], i * 16 + 16)
                for j in range(2):
                    dve.wait_ge(g["agg"], i * 2 + j + 3)
                    t = i * 2 + j
                    dst = sq1(x1[:, ds(t, 1), :]) if gl == 0 else gx[:, j, :]
                    nc.vector.tensor_tensor(dst, psum[j][0:P, :], sq1(xroot[:, ds(t, 1), :]), ALU.add).then_inc(g["out"], 1)
                    dve.wait_ge(g["out"], i * 4 + 2 * j + 5)
                    if gl == 0:
                        nc.vector.tensor_scalar(dst, dst, 0.0, None, ALU.max).then_inc(g["out"], 1)
                    else:
                        dve.wait_ge(g["xin"], i * 16 + 16)
                        nc.vector.tensor_tensor(dst, dst, xin[:, j, :], ALU.add).then_inc(g["out"], 1)

        p_w, p_keys, p_keysT, p_keysS, p_res, p_h, p_ln, p_x, p_xT_pe, p_xT, p_q_pe, p_q, p_s_pe, p_top, p_exp, p_slots, p_vals, p_dn, p_up = (
            sem("mem_" + n) for n in ("weights keys keysT_pe keys_placed residual_in h ln x xT_pe xT q_pe q s_pe top exp slots vals dots_done "
                                      "rows_added").split())
        s_dn = [sem(f"mem_down_{n}") for n in range(RING)]
        s_up = [sem(f"mem_up_{n}") for n in range(RING)]
        s_hold = sem("mem_holds")
        s_out = [sem(f"out_{j}") for j in range(2)]
        res_all = view(stage, 0, [TILES, DIM], P)
        keys_st = view(big, 16384, [2 * PKH, 128])
        slots_of = [slots, biasb[:, 1, 0:SLOTS].bitcast(I32)]
        acc_of = [acc, projbd[0:P, :]]
        QB = 4

        def mem_sp(sp):
            sp.wait_ge(m["f2_pe"], ADDS["f2_pe"] + TILES)
            sp.wait_ge(g_sem[1]["st"], 16 + 16 * PAIRS)
            for half in range(2):
                for hh in range(PKH):
                    sp.dma_start(keys_st[:, 2 * hh:2 * hh + 2, HALF * half:HALF * half + HALF],
                                 a["L0_ffn_keys"][hh, half].rearrange("(n p) d -> p n d", p=128)).then_inc(p_keys, 16)
            sp.dma_start(wqf, a["L0_ffn_Wq"].rearrange("(k p) n -> p k n", p=128)).then_inc(p_w, 16)
            sp.dma_start(c_bqf, a["L0_ffn_bq"].rearrange("(h p) -> p h", p=128), allow_slow_non_contiguous=True).then_inc(p_w, 16)
            sp.dma_start(res_all, tok(res_d)).then_inc(p_res, 16)

            def store(i, j):
                sp.wait_ge(p_up, i * (2 * SLOTS) + (RING + (j + 1) * SLOTS))
                sp.dma_start(tok(out)[:, ds(i * 2 + j, 1), :], acc_of[j].unsqueeze(1)).then_inc(s_out[j], 16)

            with sp.Fori(0, PAIRS) as i:
                store(i, 0)
                store(i, 1)
            for j in range(2):
                sp.wait_ge(s_out[j], 16 + 16 * PAIRS)

        def mem_pool(pool):
            pool.sem_inc(p_dn, RING)
            pool.sem_inc(p_up, RING)
            pool.sem_inc(s_hold, 1)

            def tile(i, j):
                if j == 0:
                    pool.wait_ge(s_hold, i * (4 * SLOTS // HOLD) + 1)
                pool.wait_ge(p_slots, i * 2 + (j + 1))
                for used, landed, ring, table in ((p_dn, s_dn, ring_dn, "L0_ffn_w_down"), (p_up, s_up, ring_up, "L0_ffn_w_up")):
                    for s in range(SLOTS):
                        if s % HOLD == 0:
                            pool.wait_ge(used, i * (2 * SLOTS) + (j * SLOTS + s + HOLD))
                            hold_pool().then_inc(s_hold, 1)
                        nc.gpsimd.indirect_dma_start(
                            out=ring[:, s % RING, :], out_offset=None, in_=a[table],
                            in_offset=bass.IndirectOffsetOnAxis(ap=slots_of[j][:, s:s + 1], axis=0)).then_inc(landed[s % RING], 16)

            with pool.Fori(0, PAIRS) as i:
                tile(i, 0)
                tile(i, 1)

        def mem_pe(pe):
            pe.wait_ge(p_keys, 16 * 2 * PKH)
            pe.wait_ge(m["hf"], ADDS["hf"] + 2 + 2 * TILES)
            for u in range(2 * PKH):
                mm = nc.tensor.transpose(psum[u // 4][:, 128 * (u % 4):128 * (u % 4) + 128], keys_st[:, u, :], ident[:, :])
            mm.then_inc(p_keysT, 1)
            pe.wait_ge(p_keysS, 2 * PKH)
            pe.wait_ge(p_w, 32)
            pe.sem_inc(p_top, 4 * 4)
            with pe.Fori(0, TILES) as t:
                pe.wait_ge(p_x, t + 1)
                for k in range(KC):
                    mm = nc.tensor.transpose(psum[0][:, P * k:P * k + P], xl[:, 128 * k:128 * k + 128], ident[0:P, 0:P])
                mm.then_inc(p_xT_pe, 1)
                pe.wait_ge(p_xT, t + 1)
                for hh in range(PKH):
                    for k in range(KC):
                        mm = nc.tensor.matmul(psum[1 + hh // QB][:, P * (hh % QB):P * (hh % QB) + P], wqf[:, k, 128 * hh:128 * hh + 128],
                                              xl_t[:, P * k:P * k + P], start=(k == 0), stop=(k == KC - 1), skip_group_check=True)
                    if hh % QB == QB - 1:
                        mm.then_inc(p_q_pe, 1)
                for hh in range(PKH):
                    pe.wait_ge(p_q, t * PKH + (hh + 1))
                    if hh < 4:
                        pe.wait_ge(p_top, t * TOPN + 16)
                    else:
                        pe.wait_ge(p_top, t * TOPN + (4 * (hh - 3) + 16))
                    nc.tensor.matmul(psum[3 + hh % 4][0:P, :], pq_t[:, hh, :], keybd[:, hh, :], start=True, stop=True).then_inc(p_s_pe, 1)

        def mem_act(act):
            with act.Fori(0, TILES) as t:
                act.wait_ge(p_xT_pe, t + 1)
                nc.scalar.activation(xl_t, psum[0][:, 0:4 * P], ACT.Copy).then_inc(p_xT, 1)
                for hh in range(PKH):
                    act.wait_ge(p_q_pe, t * 2 + (hh // QB + 1))
                    nc.scalar.activation(pq_t[:, hh, :], psum[1 + hh // QB][:, P * (hh % QB):P * (hh % QB) + P], ACT.Identity,
                                         bias=c_bqf[:, hh:hh + 1]).then_inc(p_q, 1)
                act.wait_ge(p_exp, t * 2 + 1)
                nc.scalar.activation(probs.rearrange("p h k -> p (h k)"), probs.rearrange("p h k -> p (h k)"), ACT.Exp).then_inc(p_exp, 1)

        def top_steps(dve, t, par, emit=True):
            n = 16

            def step(ins, sync=True):
                nonlocal n
                ins.then_inc(p_top, 1)
                n += 1
                if sync:
                    dve.wait_ge(p_top, t * TOPN + n)
                    hold_dve()

            for hh in range(PKH):
                dve.wait_ge(p_s_pe, t * PKH + (hh + 1))
                hold_dve()
                for s in range(2):
                    step(nc.vector.max(top_v[:, hh, s, :], psum[3 + hh % 4][0:P, NKEYS * s:NKEYS * s + NKEYS]), sync=(s == 1))
                for s in range(2):
                    step(nc.vector.max_index(top_i[:, hh, s, :], top_v[:, hh, s, :], psum[3 + hh % 4][0:P, NKEYS * s:NKEYS * s + NKEYS]), sync=False)
            dve.wait_ge(p_top, t * TOPN + n)
            step(nc.vector.tensor_copy(top_f, top_i), sync=False)
            step(nc.vector.tensor_tensor(sums.rearrange("p h (i j) -> p h i j", i=TOPK), top_v[:, :, 0, :].unsqueeze(3).to_broadcast([P, PKH, TOPK, TOPK]),
                                         top_v[:, :, 1, :].unsqueeze(2).to_broadcast([P, PKH, TOPK, TOPK]), ALU.add))
            for hh in range(PKH):
                step(nc.vector.max(best_v[:, hh, :], sums[:, hh, :]), sync=(hh == PKH - 1))
            for hh in range(PKH):
                step(nc.vector.max_index(best_i[:, hh, :], best_v[:, hh, :], sums[:, hh, :]), sync=(hh == PKH - 1))
            bi = best_i.rearrange("p h k -> p (h k)")
            step(nc.vector.tensor_scalar(best_hi, bi, 3, None, ALU.logical_shift_right), sync=False)
            step(nc.vector.tensor_scalar(best_lo, bi, 7, None, ALU.bitwise_and))
            step(nc.vector.tensor_copy(hi_f, best_hi), sync=False)
            step(nc.vector.tensor_copy(lo_f, best_lo))
            for s, (where, got) in enumerate(((hi_f, pick_a), (lo_f, pick_b))):
                step(nc.vector.tensor_tensor(pick.rearrange("p h k j -> p (h k) j"), where.unsqueeze(2).to_broadcast([P, SLOTS, TOPK]),
                                             iota8.unsqueeze(1).to_broadcast([P, SLOTS, TOPK]), ALU.is_equal))
                step(nc.vector.tensor_tensor(pick, pick, top_f[:, :, s, :].unsqueeze(2).to_broadcast([P, PKH, TOPK, TOPK]), ALU.mult))
                step(nc.vector.tensor_reduce(got, pick.rearrange("p h k j -> p (h k) j"), AX, ALU.add))
            step(nc.vector.scalar_tensor_tensor(slot_f, pick_a, float(NKEYS), pick_b, ALU.mult, ALU.add))
            nc.vector.tensor_copy(slots_of[par], slot_f).then_inc(p_slots, 1)
            nc.vector.tensor_tensor(probs, best_v, best_v[:, :, 0:1].to_broadcast([P, PKH, TOPK]), ALU.subtract).then_inc(p_exp, 1)
            dve.wait_ge(p_exp, t * 2 + 2)
            step(nc.vector.tensor_reduce(prob_s, probs, AX, ALU.add))
            step(nc.vector.reciprocal(prob_s, prob_s))
            step(nc.vector.tensor_tensor(probs, probs, prob_s.unsqueeze(2).to_broadcast([P, PKH, TOPK]), ALU.mult))

        TOPN = 4 * PKH + 2 + 2 * PKH + 4 + 6 + 1 + 3

        def mem_dve(dve):
            for s in range(2):
                for b in range(4):
                    rows = slice(64 * s, 64 * s + 64)
                    if s == 0 and b == 0:
                        dve.wait_ge(p_keysT, 1)
                    nc.vector.tensor_copy(keybd[rows, 2 * b:2 * b + 2, NKEYS * s:NKEYS * s + NKEYS],
                                          psum[b][rows, :].rearrange("p (h m) -> p h m", h=2)).then_inc(p_keysS, 1)
                    nc.vector.memset(keybd[rows, 2 * b:2 * b + 2, NKEYS * (1 - s):NKEYS * (2 - s)], 0.0).then_inc(p_keysS, 1)
            dve.wait_ge(p_res, 16)
            for t in range(TILES):
                nc.vector.tensor_tensor(h[:, t, :], h[:, t, :], res_all[:, t, :], ALU.add).then_inc(p_h, 1)
            dve.wait_ge(p_h, TILES)
            for t in range(TILES):
                nc.vector.bn_stats(st6[:, t, :], h[:, t, :]).then_inc(p_ln, 1)
            dve.wait_ge(p_ln, TILES)
            for t in range(TILES):
                nc.vector.bn_aggr(mv[:, t, :], st6[:, t, :]).then_inc(p_ln, 1)
            dve.wait_ge(p_ln, 2 * TILES)
            rsqrt(dve, p_ln, 2 * TILES, mv[:, :, 1], 0, TILES)
            dve.wait_ge(p_ln, 2 * TILES + RSQ)
            for n in range(TOPK):
                nc.vector.memset(iota8[:, n:n + 1], float(n)).then_inc(p_ln, 1)
            dve.wait_ge(p_ln, 2 * TILES + RSQ + TOPK)
            dve.sem_inc(s_out[0], 16)
            dve.sem_inc(s_out[1], 16)

            def prepare(t, par):
                nc.vector.tensor_scalar(xl, sq1(h[:, ds(t, 1), :]), sq1(mv[:, ds(t, 1), 0:1]), rs[:, 0, ds(t, 1)],
                                        ALU.subtract, ALU.mult).then_inc(p_x, 1)
                top_steps(dve, t, par)

            def dots(i, j):
                for s in range(SLOTS):
                    dve.wait_ge(s_dn[s % RING], i * (2 * 16 * ROUNDS) + 16 * (j * ROUNDS + s // RING + 1))
                    nc.vector.tensor_tensor_reduce(out=ring_dn[:, s % RING, :], in0=ring_dn[:, s % RING, :], in1=xl, scale=1.0, scalar=0.0,
                                                   op0=ALU.mult, op1=ALU.add, accum_out=inner[:, s:s + 1]).then_inc(p_dn, 1)
                dve.wait_ge(p_dn, i * (2 * SLOTS) + (RING + (j + 1) * SLOTS))
                nc.vector.scalar_tensor_tensor(vals, inner, 0.0, probs.rearrange("p h k -> p (h k)"), ALU.max, ALU.mult).then_inc(p_vals, 1)

            def rows(i, j):
                dve.wait_ge(s_out[j], i * 16 + 16)
                dve.wait_ge(p_vals, i * 2 + (j + 1))
                for s in range(SLOTS):
                    dve.wait_ge(s_up[s % RING], i * (2 * 16 * ROUNDS) + 16 * (j * ROUNDS + s // RING + 1))
                    if s:
                        dve.wait_ge(p_up, i * (2 * SLOTS) + (RING + j * SLOTS + s))
                    nc.vector.scalar_tensor_tensor(acc_of[j], ring_up[:, s % RING, :], vals[:, s:s + 1],
                                                   acc_of[j] if s else sq1(h[:, ds(i * 2 + j, 1), :]), ALU.mult, ALU.add).then_inc(p_up, 1)

            prepare(0, 0)
            with dve.Fori(0, PAIRS - 1) as i:
                for j in range(2):
                    dots(i, j)
                    prepare(i * 2 + (j + 1), 1 - j)
                    rows(i, j)
            dots(PAIRS - 1, 0)
            prepare(TILES - 1, 1)
            rows(PAIRS - 1, 0)
            dots(PAIRS - 1, 1)
            rows(PAIRS - 1, 1)

        @block.sync
        def _(sp):
            setup_sp(sp)
            mix_loads_sp(sp, 0)
            mlp_loads_sp(sp, 0)
            bases_sp(sp)
            gcn_sp(sp, 0)
            gcn_sp(sp, 1)
            mix_loads_sp(sp, 1)
            mlp_loads_sp(sp, 1)
            mem_sp(sp)

        @block.gpsimd
        def _(pool):
            setup_pool()
            adjacency_pool(pool)
            mem_pool(pool)

        @block.tensor
        def _(pe):
            setup_pe(pe)
            for l in range(2):
                attn1_pe(pe, l)
                attn2_pe(pe, l)
                attn3_pe(pe, l)
                mlp_pe(pe, l)
                if l == 0:
                    gcn_pe(pe, 0)
                    gcn_pe(pe, 1)
            mem_pe(pe)

        @block.scalar
        def _(act):
            for l in range(2):
                attn1_act(act, l)
                attn2_act(act, l)
                attn3_act(act, l)
                mlp_act(act, l)
                if l == 0:
                    gcn_act(act, 0)
                    gcn_act(act, 1)
                    gcn_x_act(act, 1)
            mem_act(act)

        @block.vector
        def _(dve):
            setup_dve(dve)
            for l in range(2):
                attn1_dve(dve, l)
                attn2_dve(dve, l)
                attn3_dve(dve, l)
                mlp_dve(dve, l)
                if l == 0:
                    gcn_dve(dve, 0)
                    gcn_dve(dve, 1)
            mem_dve(dve)


def kernel(**inputs):
    import numpy as np
    import concourse.bacc as bacc
    from concourse.bass_utils import run_bass_kernel_spmd

    nc = bacc.Bacc("TRN2", target_bir_lowering=False, num_devices=1)
    arrays, aps = {}, {}
    for name, value in inputs.items():
        v = np.ascontiguousarray(value)
        arrays["in_" + name] = v
        aps[name] = nc.dram_tensor("in_" + name, v.shape, mybir.dt.from_np(v.dtype), kind="ExternalInput").ap()
    out = nc.dram_tensor("out", (NODES, DIM), F32, kind="ExternalOutput").ap()
    build(nc, aps, out)
    r = run_bass_kernel_spmd(nc, [arrays], core_ids=[0])
    return r.results[0]["out"]
```

```python
from contextlib import ExitStack

import concourse.bass as bass
from concourse import mybir

F32 = mybir.dt.float32
I32 = mybir.dt.int32
U32 = mybir.dt.uint32
ALU = mybir.AluOpType
ACT = mybir.ActivationFunctionType
AX = mybir.AxisListType.X
ds = bass.ds

NODES, DIM, EDGES = 1250, 512, 20000
P = 125
TILES = NODES // P
PAIRS = TILES // 2
PT = 2 * P
KC = DIM // 128
BASES, RELS = 30, 2
HEADS, HD, FEATS = 8, 64, 256
HID = 4 * DIM
HC = HID // 128
HH = HC // 2
GROUPS = EDGES // P
CELLS = RELS * NODES * NODES
COLT = RELS * TILES
NORM = HD ** -0.25
EPS_K = 1e-4
EPS_LN = 1e-5
PKH, NKEYS, TOPK, HALF = 8, 256, 8, 64
SLOTS = PKH * TOPK
RING = 16
ROUNDS = SLOTS // RING
DRING = 8
HOLD = 8
MAGIC = float(0x5F3759DF)


def build(nc, a, out):
    with ExitStack() as ctx:
        def sb(name, shape, dt=F32):
            return ctx.enter_context(nc.sbuf_tensor(name, shape, dt))

        def sem(name):
            return ctx.enter_context(nc.semaphore(name))

        def dram(name, shape, dt=F32):
            return nc.dram_tensor(name, shape, dt, kind="Internal").ap()

        adj = dram("adj", [CELLS + 128, 1])
        cells_t = dram("cells_t", [GROUPS, P])
        xn_d = dram("xn_d", [NODES, DIM])
        res_d = dram("res_d", [NODES, DIM])
        adj_zero = adj[0:CELLS, :].rearrange("(z p f w) o -> z p f (w o)", z=5, p=P, f=4)
        adj_2d = adj[0:CELLS, :].rearrange("(k r) o -> k (r o)", r=NODES)

        def tok(ap):
            return ap.rearrange("(t p) d -> p t d", p=P)

        h = sb("h", [P, TILES, DIM])
        ident = sb("ident", [128, 128])
        ones = sb("ones", [HEADS, P])
        zeros = sb("zeros", [128, 128])
        headsel = sb("headsel", [128, KC, HEADS])
        att_b = sb("att_b", [128, 2, RELS * BASES])
        wreg = sb("wreg", [128, 4, 4 * DIM])
        projbd = sb("projbd", [128, 2 * FEATS])
        biasb = sb("biasb", [P, 2, DIM])
        cols = sb("cols", [128, 64])
        big = sb("big", [128, 20480])
        qv = sb("qv", [128, 10200])
        stage = sb("stage", [128, 5120])
        ctx_flat = sb("ctx_flat", [128, 2 * HEADS * (HD + 1)])
        ctx_sb = ctx_flat[:, :].rearrange("p (u d) -> p u d", u=2 * HEADS)
        st6 = sb("st6", [P, TILES, 6])
        mv = sb("mv", [P, TILES, 2])
        rs = sb("rs", [P, 4, TILES])
        small = sb("small", [P, 408])
        psum = [ctx.enter_context(nc.psum_tensor(f"bank{i}", [128, 512], F32)) for i in range(8)]

        def view(region, at, shape, parts=128):
            n = 1
            for s in shape:
                n *= s
            v = region[0:parts, at:at + n]
            if len(shape) == 2:
                v = v.rearrange("p (a b) -> p a b", a=shape[0])
            if len(shape) == 3:
                v = v.rearrange("p (a b c) -> p a b c", a=shape[0], b=shape[1])
            return v

        c_g1, c_b1, c_g2, c_b2, c_bq, c_bk = (cols[:, 4 * i:4 * i + 4] for i in range(6))
        c_h1 = cols[:, 24:24 + HC]
        c_gate = cols[:, 40:48].rearrange("p (k r) -> p k r", k=KC)
        c_bqf = cols[:, 48:56]
        b_v, b_o = (biasb[:, i, :] for i in range(2))
        b_2 = b_v

        zst = view(stage, 0, [2, DIM], P)
        y_t = view(stage, 1024, [KC, PT])
        k_t = view(stage, 2024, [KC, PT])
        sq = view(stage, 3024, [2, KC, PT])
        kfeat = view(stage, 0, [2, HEADS * FEATS], P)
        q_st = view(stage, 0, [KC, PT])
        qfeat = view(stage, 1000, [2, DIM], P)
        qfeat_t = view(stage, 2024, [2, 4 * P])
        o_sb = view(stage, 3024, [2, DIM], P)
        o_t = view(stage, 4048, [2, 4 * P])
        kdash = view(big, 0, [TILES, HEADS * FEATS], P)
        q_t = view(qv, 0, [KC, NODES])
        v_aug = qv[0:P, 5000:10200].rearrange("p (t h d) -> p t h d", t=TILES, h=HEADS)
        diag = small[:, 0:160].rearrange("p (t s h) -> p t s h", t=TILES, s=2)
        kmax = small[:, 160:240].rearrange("p (t h) -> p t h", t=TILES)
        kmax_all = small[:, 240:248]
        kneg = small[:, 250:330].rearrange("p (t h) -> p t h", t=TILES)
        qmax = small[:, 330:334].rearrange("p (j s) -> p j s", j=2)
        qneg = small[:, 334:338].rearrange("p (j s) -> p j s", j=2)
        rden = small[:, 340:356].rearrange("p (j h) -> p j h", j=2)
        kmax_t = small[0:8, 360:361]
        kmax_d = small[0:8, 364:372]
        w1_sb = view(big, 0, [KC, HID])
        w2_sb = view(big, 8192, [HC, DIM])
        act_t = view(big, 16384, [HH, PT])
        wrel = qv[:, 0:8192].rearrange("p (l r k) -> p l r k", l=2, r=2)
        zrel = view(big, 0, [COLT, DIM], P)
        xroot = view(big, 10240, [TILES, DIM], P)
        x1 = view(big, 15360, [TILES, DIM], P)
        wflat = wreg[:, :, :].rearrange("p a b -> p (a b)")
        slab = wflat[0:P, 0:5000].rearrange("p (s c r) -> p s c r", s=2, c=COLT)
        root_sb = wflat[:, 5120:7168].rearrange("p (k n) -> p k n", k=KC)
        gx = view(stage, 0, [2, DIM], P)
        gx_t = view(stage, 1024, [2, 4 * P])
        gate = small[:, 400:404].rearrange("p (j r) -> p j r", j=2)
        keybd = wflat[:, 4096:8192].rearrange("p (h n) -> p h n", h=PKH)
        wqf = wflat[:, 0:4096].rearrange("p (k n) -> p k n", k=KC)
        diags = view(stage, 2024, [DRING, P], P)
        res_p = view(stage, 3024, [2, DIM], P)
        ring = [region[0:P, at + DIM * n:at + DIM * n + DIM] for region, at, count in ((qv, 5592, 9), (ctx_flat, 0, 2), (stage, 4048, 2), (big, 18384, 3))
                for n in range(count)]
        mvm = small[:, 0:4].rearrange("p (j s) -> p j s", j=2)
        xl = view(qv, 0, [DIM], P)
        dot_scr = view(qv, 512, [DIM], P)
        acc = view(qv, 1024, [DIM], P)
        xl_t = view(qv, 1536, [4 * P])
        pq_t = view(qv, 2048, [PKH, P])
        top_v = view(qv, 3072, [PKH, 2, TOPK], P)
        top_i = qv[0:P, 3200:3328].bitcast(U32).rearrange("p (h s k) -> p h s k", h=PKH, s=2)
        top_f = view(qv, 3328, [PKH, 2, TOPK], P)
        sums = view(qv, 3456, [PKH, TOPK * TOPK], P)
        best_v = view(qv, 3968, [PKH, TOPK], P)
        best_i = qv[0:P, 4032:4096].bitcast(U32).rearrange("p (h k) -> p h k", h=PKH)
        best_hi = qv[0:P, 4096:4160].bitcast(U32)
        best_lo = qv[0:P, 4160:4224].bitcast(U32)
        hi_f = view(qv, 4224, [PKH * TOPK], P)
        lo_f = view(qv, 4288, [PKH * TOPK], P)
        pick = view(qv, 4352, [PKH, TOPK, TOPK], P)
        pick_a = view(qv, 4864, [SLOTS], P)
        pick_b = view(qv, 4928, [SLOTS], P)
        slot_f = view(qv, 4992, [SLOTS], P)
        slots = qv[0:P, 5056:5120].bitcast(I32)
        probs = view(qv, 5120, [PKH, TOPK], P)
        prob_s = view(qv, 5184, [PKH], P)
        inner = view(qv, 5192, [SLOTS], P)
        vals = view(qv, 5256, [SLOTS], P)
        idx_dn = qv[0:P, 5320:5336].bitcast(I32)
        idx_up = qv[0:P, 5336:5352].bitcast(I32)
        dots = view(qv, 5352, [RING], P)
        wts = view(qv, 5368, [RING], P)
        iota8 = view(qv, 5384, [TOPK], P)
        iota8_u = qv[0:P, 5392:5400].bitcast(I32)

        s_xin = sem("x_loaded")
        s_const = sem("constants_made")
        s_edge = sem("edges_loaded")
        s_cell = sem("cells_step")
        s_cellp = sem("cells_transposed")
        s_cellsb = sem("cells_t_copied")
        s_cellw = sem("cells_t_written")
        s_cellb = sem("cells_broadcast")
        s_code = sem("edge_code_made")
        s_idx = sem("edge_index_made")
        s_adjz = sem("adjacency_zeroed")
        s_stg = sem("group_index_staged")
        s_adj = sem("group_added")
        s_ln = sem("ln0_step")
        s_xnw = sem("xn_written")
        s_att = sem("att_loaded")

        block = ctx.enter_context(nc.Block())

        cellb = big[0:P, :].rearrange("p (c w) -> p c w", c=PAIRS)
        CHUNK = GROUPS // PAIRS
        e_raw = qv[0:P, 5000:5480].bitcast(I32).rearrange("p (s g) -> p s g", s=3)
        e_f = view(qv, 5480, [3, GROUPS], P)
        cell_ts = view(qv, 5960, [2, P])
        cell, code, flag, trash = (view(ctx_flat, 256 + GROUPS * n, [GROUPS], P) for n in range(4))
        wmask = view(ctx_flat, 256 + 4 * GROUPS, [P], P)
        zbuf = wflat[0:P, 6144:6144 + CELLS // (20 * P)]
        e_idx = sb("e_idx", [P, GROUPS], I32)
        e_cnt = sb("e_cnt", [P, GROUPS])
        g_idx = sb("g_idx", [P, 1], I32)
        g_cnt = sb("g_cnt", [P, 1])

        tick = sb("tick", [1, 12 + 2 + 4 * SLOTS // HOLD])
        holds = [0, 0]

        def hold_dve():
            holds[0] = (holds[0] + 1) % 12
            nc.vector.memset(tick[:, holds[0]:holds[0] + 1], 0.0)

        def hold_pool():
            holds[1] += 1
            return nc.gpsimd.tensor_tensor(tick[:, 11 + holds[1]:12 + holds[1]], ones[0:1, 0:1], ones[0:1, 0:1], ALU.add)

        def rsqrt(dve, s, n, src, c0, w, row=0):
            v, y, t = (rs[:, k, c0:c0 + w] for k in (1, row, 2))
            yi, vi = y.bitcast(I32), v.bitcast(I32)
            nc.vector.tensor_scalar(v, src, EPS_LN, None, ALU.add).then_inc(s, 1)
            dve.wait_ge(s, n + 1)
            nc.vector.tensor_scalar(yi, vi, -0.5, MAGIC, ALU.mult, ALU.add).then_inc(s, 1)
            n += 2
            for _ in range(4):
                dve.wait_ge(s, n)
                nc.vector.tensor_tensor(t, y, y, ALU.mult).then_inc(s, 1)
                dve.wait_ge(s, n + 1)
                nc.vector.tensor_tensor(t, t, v, ALU.mult).then_inc(s, 1)
                dve.wait_ge(s, n + 2)
                nc.vector.tensor_scalar(t, t, -0.5, 1.5, ALU.mult, ALU.add).then_inc(s, 1)
                dve.wait_ge(s, n + 3)
                nc.vector.tensor_tensor(y, y, t, ALU.mult).then_inc(s, 1)
                n += 4
            return n
        RSQ = 18
        LN0_DONE = 3 * TILES + RSQ

        def setup_pool():
            nc.gpsimd.memset(ident[:, :], 0.0).then_inc(s_const, 1)
            nc.gpsimd.memset(ones[:, :], 1.0).then_inc(s_const, 1)
            nc.gpsimd.memset(zeros[:, :], 0.0).then_inc(s_const, 1)
            nc.gpsimd.memset(headsel[:, :, :], 0.0).then_inc(s_const, 1)
            nc.gpsimd.memset(wmask, 257.0).then_inc(s_const, 1)
            nc.gpsimd.memset(zbuf, 0.0).then_inc(s_const, 1)
            nc.gpsimd.iota(trash.bitcast(I32), pattern=[[0, GROUPS]], base=CELLS, channel_multiplier=1).then_inc(s_const, 1)
            nc.gpsimd.wait_ge(s_const, 7)
            nc.gpsimd.affine_select(out=ident[:, :], in_=ident[:, :], compare_op=ALU.not_equal, fill=1.0, base=0,
                                    pattern=[[-1, 128]], channel_multiplier=1).then_inc(s_const, 1)
            nc.gpsimd.affine_select(out=wmask, in_=wmask, compare_op=ALU.is_gt, fill=1.0, base=0,
                                    pattern=[[-1, P]], channel_multiplier=1).then_inc(s_const, 1)
            nc.gpsimd.wait_ge(s_const, 9)
            for c in range(KC):
                for s in range(2):
                    nc.gpsimd.memset(headsel[64 * s:64 * s + 64, c, 2 * c + s:2 * c + s + 1], 1.0).then_inc(s_const, 1)
        CONSTS = 9 + 2 * KC

        def adjacency_pool(pool):
            pool.wait_ge(s_idx, 4)
            pool.wait_ge(s_adjz, 5 * 16)

            def add_group(g):
                nc.gpsimd.tensor_copy(g_idx[:, :], e_idx[:, ds(g, 1)]).then_inc(s_stg, 1)
                nc.gpsimd.tensor_copy(g_cnt[:, :], e_cnt[:, ds(g, 1)]).then_inc(s_stg, 1)
                pool.wait_ge(s_stg, g * 2 + 2)
                hold_pool()
                nc.gpsimd.indirect_dma_start(
                    out=adj, out_offset=bass.IndirectOffsetOnAxis(ap=g_idx[:, :], axis=0), in_=g_cnt[:, :],
                    in_offset=None, bounds_check=CELLS + 127, oob_is_err=True, compute_op=ALU.add).then_inc(s_adj, 16)

            add_group(0)
            with pool.Fori(1, GROUPS) as g:
                pool.wait_ge(s_adj, g * 16)
                add_group(g)

        def setup_sp(sp):
            sp.dma_start(h[:, :, :], tok(a["x"])).then_inc(s_xin, 16)
            for n, name in enumerate(("src", "dst", "edge_type_2")):
                sp.dma_start(e_raw[:, n, :], a[name].rearrange("(p g) -> p g", p=P)).then_inc(s_edge, 16)
            sp.dma_start(att_b[:, 0, :], a["L0_gnn_att1"].rearrange("r b -> (r b)").partition_broadcast(128)).then_inc(s_att, 16)
            sp.dma_start(att_b[:, 1, :], a["L0_gnn_att2"].rearrange("r b -> (r b)").partition_broadcast(128)).then_inc(s_att, 16)
            attn_loads_sp(sp, 0)
            sp.wait_ge(s_cellsb, 2)
            sp.dma_start(cells_t[0:128, :], cell_ts[:, 0, :]).then_inc(s_cellw, 16)
            sp.dma_start(cells_t[128:GROUPS, :], cell_ts[0:GROUPS - 128, 1, :]).then_inc(s_cellw, 16)
            sp.wait_ge(s_cellw, 32)
            sp.dma_start(cellb[:, :, 0:CHUNK * P], cells_t.rearrange("g p -> (g p)").partition_broadcast(P).rearrange("q (c w) -> q c w", c=PAIRS)).then_inc(s_cellb, 16)
            sp.wait_ge(s_ln, LN0_DONE)
            sp.dma_start(tok(xn_d), h[:, :, :]).then_inc(s_xnw, 16)
            sp.wait_ge(s_const, 7)
            for n in range(5):
                sp.dma_start(adj_zero[n], zbuf.unsqueeze(1).to_broadcast([P, 4, CELLS // (20 * P)])).then_inc(s_adjz, 16)
            sp.wait_ge(s_adjz, 5 * 16)
            wo_load_sp(sp, 0)

        def setup_dve(dve):
            dve.wait_ge(s_edge, 48)
            nc.vector.tensor_copy(e_f, e_raw).then_inc(s_cell, 1)
            dve.wait_ge(s_cell, 1)
            nc.vector.tensor_scalar(e_f[:, 2, :], e_f[:, 2, :], 0.0, float(NODES), ALU.not_equal, ALU.mult).then_inc(s_cell, 1)
            dve.wait_ge(s_cell, 2)
            nc.vector.tensor_tensor(e_f[:, 2, :], e_f[:, 2, :], e_f[:, 1, :], ALU.add).then_inc(s_cell, 1)
            dve.wait_ge(s_cell, 3)
            nc.vector.scalar_tensor_tensor(cell, e_f[:, 2, :], float(NODES), e_f[:, 0, :], ALU.mult, ALU.add).then_inc(s_cell, 1)
            dve.wait_ge(s_cellp, 1)
            nc.vector.tensor_copy(cell_ts[:, 0, :], psum[0][:, 0:P]).then_inc(s_cellsb, 1)
            nc.vector.tensor_copy(cell_ts[0:GROUPS - 128, 1, :], psum[0][0:GROUPS - 128, 128:128 + P]).then_inc(s_cellsb, 1)
            dve.wait_ge(s_xin, 16)
            for t in range(TILES):
                nc.vector.bn_stats(st6[:, t, :], h[:, t, :]).then_inc(s_ln, 1)
            dve.wait_ge(s_ln, TILES)
            for t in range(TILES):
                nc.vector.bn_aggr(mv[:, t, :], st6[:, t, :]).then_inc(s_ln, 1)
            dve.wait_ge(s_ln, 2 * TILES)
            rsqrt(dve, s_ln, 2 * TILES, mv[:, :, 1], 0, TILES)
            dve.wait_ge(s_ln, 2 * TILES + RSQ)
            for t in range(TILES):
                nc.vector.tensor_scalar(h[:, t, :], h[:, t, :], mv[:, t, 0:1], rs[:, 0, t:t + 1], ALU.subtract, ALU.mult).then_inc(s_ln, 1)

        def merge_dve(dve, i):
            dve.wait_ge(s_cellb, 16)
            for n in range(CHUNK):
                part = big[0:P, ds(i * 4096 + P * n, P)]
                nc.vector.scalar_tensor_tensor(part, part, cell[:, ds(i * CHUNK + n, 1)], wmask,
                                               ALU.is_equal, ALU.mult, accum_out=code[:, ds(i * CHUNK + n, 1)]).then_inc(s_code, 1)

        def edge_index_dve(dve):
            dve.wait_ge(s_code, GROUPS)
            nc.vector.tensor_copy(e_cnt[:, :], code).then_inc(s_idx, 1)
            nc.vector.tensor_scalar(flag, code, 256.0, None, ALU.is_ge).then_inc(s_cell, 1)
            nc.vector.tensor_copy(trash, trash.bitcast(I32)).then_inc(s_cell, 1)
            dve.wait_ge(s_cell, 6)
            nc.vector.tensor_tensor(trash, trash, cell, ALU.subtract).then_inc(s_idx, 1)
            dve.wait_ge(s_idx, 2)
            nc.vector.tensor_tensor(trash, trash, flag, ALU.mult).then_inc(s_idx, 1)
            dve.wait_ge(s_idx, 3)
            nc.vector.tensor_tensor(e_idx[:, :], trash, cell, ALU.add).then_inc(s_idx, 1)

        def setup_pe(pe):
            pe.wait_ge(s_const, CONSTS)
            pe.wait_ge(s_cell, 4)
            nc.tensor.transpose(psum[0][:, 0:P], cell[:, 0:128], ident[0:P, 0:P])
            nc.tensor.transpose(psum[0][0:GROUPS - 128, 128:128 + P], cell[:, 128:GROUPS], ident[0:P, 0:P]).then_inc(s_cellp, 1)

        ADDS = dict(w=13 * 16, pj=32, pjT=1, pjS=4, stat=1 + 2 * TILES + RSQ, z=TILES, yT_pe=KC * PAIRS, yT=KC * PAIRS, q_pe=KC * PAIRS,
                    sq=2 * KC * PAIRS, k=KC * PAIRS, k_pe=KC * PAIRS, v_pe=TILES, v=TILES, dg_pe=PAIRS, dg=PAIRS,
                    kd_pe=4 * TILES, kmx=4 * TILES, kd=4 * TILES, gmx=5, gmx_pe=2, kneg=1, kx=TILES, kf=TILES, ctx_pe=TILES, ctx=4,
                    qs=PAIRS, qd_pe=4 * TILES, qm=4 * TILES, qn=4 * TILES, qx=4 * TILES, qT_pe=4 * TILES, qT=4 * TILES, o_pe=TILES,
                    rd=2 * TILES, o=2 * TILES, oT_pe=TILES, oT=TILES, at_pe=TILES, hat=2 * TILES, mw=48, ln2=(4 + RSQ) * PAIRS,
                    z2=TILES, y2_pe=KC * PAIRS, y2=KC * PAIRS, f1_pe=HC * PAIRS, f1=HC * PAIRS, f2_pe=TILES, hf=2 * TILES)
        m = {name: sem("mix_" + name) for name in ADDS}
        s_comb = sem("bases_added")
        s_comb0 = sem("relation_sums_zeroed")
        s_basis = [sem(f"basis_ring_{n}") for n in range(4)]
        proj_st = ctx_flat[:, 0:256].rearrange("p (k d) -> p k d", k=2)
        W_LOADS = 12 * 16
        BLOCKS = 2 * BASES // PAIRS
        BRING = 4

        def sq1(ap):
            return ap.rearrange("p a b -> p (a b)")

        def wo_load_sp(sp, l):
            sp.wait_ge(m["w"], l * ADDS["w"] + W_LOADS)
            sp.dma_start(wreg[:, 3, :].rearrange("p (k n) -> p k n", k=KC), a["L0_mix_Wo"][l].rearrange("(k p) n -> p k n", p=128)).then_inc(m["w"], 16)

        def attn_loads_sp(sp, l):
            for n, name in enumerate(("Wq", "Wk", "Wv")):
                sp.dma_start(wreg[:, n, :].rearrange("p (k n) -> p k n", k=KC),
                             a["L0_mix_" + name][l].rearrange("(k p) n -> p k n", p=128)).then_inc(m["w"], 16)
            for c, name in ((c_g1, "ln1_g"), (c_b1, "ln1_b"), (c_g2, "ln2_g"), (c_b2, "ln2_b"), (c_bq, "bq"), (c_bk, "bk"), (c_h1, "b1")):
                sp.dma_start(c, a["L0_mix_" + name][l].rearrange("(k p) -> p k", p=128), allow_slow_non_contiguous=True).then_inc(m["w"], 16)
            for b, name in ((b_v, "bv"), (b_o, "bo")):
                sp.dma_start(b, a["L0_mix_" + name][l].partition_broadcast(P)).then_inc(m["w"], 16)
            for s in range(2):
                sp.dma_start(proj_st[:, :, 64 * s:64 * s + 64], a["L0_mix_proj"][l].rearrange("(k p) d -> p k d", p=128)).then_inc(m["pj"], 16)

        def mlp_loads_sp(sp, l):
            sp.wait_ge(m["ctx"], l * ADDS["ctx"] + 4)
            sp.dma_start(w1_sb, a["L0_mix_W1"][l].rearrange("(k p) n -> p k n", p=128)).then_inc(m["mw"], 16)
            sp.dma_start(w2_sb, a["L0_mix_W2"][l].rearrange("(k p) n -> p k n", p=128)).then_inc(m["mw"], 16)
            sp.dma_start(b_2, a["L0_mix_b2"][l].partition_broadcast(P)).then_inc(m["mw"], 16)

        def bases_sp(sp, l=0):
            sp.wait_ge(m["hat"], 2 + 2 * TILES)
            sp.sem_inc(s_comb, 2 * BRING)
            with sp.Fori(0, PAIRS) as i:
                for n in range(BLOCKS):
                    gl, b = n // (BLOCKS // 2), n % (BLOCKS // 2)
                    sp.wait_ge(s_comb, i * (2 * BLOCKS) + 2 * n + 2)
                    sp.dma_start(wreg[:, n % BRING, :].rearrange("p (k n) -> p k n", k=KC),
                                 a[f"L0_gnn_basis{gl + 1}"][ds(i * (BLOCKS // 2) + b, 1), :, :].rearrange("o (k p) n -> p (o k) n", p=128)
                                 ).then_inc(s_basis[n % BRING], 16)

        def attn1_dve(dve, l):
            dve.wait_ge(m["pjT"], l * ADDS["pjT"] + 1)
            for s in range(2):
                rows = slice(64 * s, 64 * s + 64)
                nc.vector.memset(projbd[rows, FEATS * (1 - s):FEATS * (2 - s)], 0.0).then_inc(m["pjS"], 1)
                nc.vector.tensor_scalar(projbd[rows, FEATS * s:FEATS * s + FEATS], psum[7][rows, 0:FEATS], NORM, None,
                                        ALU.mult).then_inc(m["pjS"], 1)
            if l == 1:
                dve.wait_ge(g_sem[1]["z"], 4 + 2 * TILES)
                dve.wait_ge(g_sem[1]["st"], 16 + 16 * PAIRS)
            else:
                dve.wait_ge(s_cellw, 32)
                dve.wait_ge(s_const, CONSTS)
                dve.wait_ge(s_ln, LN0_DONE)
            nc.vector.memset(v_aug[:, :, :, HD:HD + 1].rearrange("p t h o -> p (t h) o"), 1.0).then_inc(m["stat"], 1)
            for t in range(TILES):
                nc.vector.bn_stats(st6[:, t, :], h[:, t, :]).then_inc(m["stat"], 1)
            dve.wait_ge(m["stat"], l * ADDS["stat"] + 1 + TILES)
            for t in range(TILES):
                nc.vector.bn_aggr(mv[:, t, :], st6[:, t, :]).then_inc(m["stat"], 1)
            dve.wait_ge(m["stat"], l * ADDS["stat"] + 1 + 2 * TILES)
            n = rsqrt(dve, m["stat"], l * ADDS["stat"] + 1 + 2 * TILES, mv[:, :, 1], 0, TILES)
            dve.wait_ge(m["stat"], n)
            dve.wait_ge(m["w"], l * ADDS["w"] + W_LOADS)
            if l == 0:
                dve.sem_inc(m["yT_pe"], KC)
            with dve.Fori(0, PAIRS) as i:
                dve.wait_ge(m["yT_pe"], l * ADDS["yT_pe"] + i * KC + KC)
                for j in range(2):
                    nc.vector.tensor_scalar(zst[:, j, :], sq1(h[:, ds(i * 2 + j, 1), :]), mv[:, ds(i * 2 + j, 1), 0:1].rearrange("p a b -> p (a b)"),
                                            rs[:, 0, ds(i * 2 + j, 1)], ALU.subtract, ALU.mult).then_inc(m["z"], 1)
                for c in range(KC):
                    dve.wait_ge(m["k_pe"], l * ADDS["k_pe"] + i * KC + c + 1)
                    nc.vector.tensor_scalar(k_t[:, c, :], psum[4 + c % 2][:, 0:PT], c_bk[:, c:c + 1], None, ALU.add).then_inc(m["k"], 1)
                for j in range(2):
                    dve.wait_ge(m["v_pe"], l * ADDS["v_pe"] + i * 2 + j + 1)
                    nc.vector.tensor_tensor(v_aug[:, ds(i * 2 + j, 1), :, 0:HD].rearrange("p o h d -> p (o h) d"),
                                            psum[6 + j][0:P, :].rearrange("p (h d) -> p h d", h=HEADS),
                                            b_v.rearrange("p (h d) -> p h d", h=HEADS), ALU.add).then_inc(m["v"], 1)
                if l == 0:
                    merge_dve(dve, i)
                dve.wait_ge(m["dg_pe"], l * ADDS["dg_pe"] + i + 1)
                nc.vector.tensor_scalar(diag[:, ds(i * 2, 2), :, :].rearrange("p t s h -> p (t s h)"), psum[0][0:P, 0:32],
                                        0.5 * NORM * NORM, None, ALU.mult).then_inc(m["dg"], 1)
                for n in range(8):
                    j, c = n // 4, n % 4
                    dve.wait_ge(m["kd_pe"], l * ADDS["kd_pe"] + i * 8 + n + 1)
                    nc.vector.tensor_reduce(sq1(kmax[:, ds(i * 2 + j, 1), 2 * c:2 * c + 2]),
                                            psum[6 + n % 2][0:P, :].rearrange("p (s m) -> p s m", s=2), AX, ALU.max).then_inc(m["kmx"], 1)
            dve.wait_ge(m["kmx"], l * ADDS["kmx"] + 4 * TILES)
            nc.vector.tensor_reduce(kmax_all, kmax.rearrange("p t h -> p h t"), AX, ALU.max).then_inc(m["gmx"], 1)
            dve.wait_ge(m["gmx_pe"], l * ADDS["gmx_pe"] + 1)
            nc.vector.tensor_reduce(kmax_t, psum[0][0:HEADS, 0:P], AX, ALU.max).then_inc(m["gmx"], 1)
            dve.wait_ge(m["gmx"], l * ADDS["gmx"] + 2)
            nc.vector.tensor_scalar(kmax_d, ident[0:HEADS, 0:HEADS], kmax_t, None, ALU.mult).then_inc(m["gmx"], 1)
            dve.wait_ge(m["gmx_pe"], l * ADDS["gmx_pe"] + 2)
            nc.vector.tensor_copy(kmax_all, psum[1][0:P, 0:HEADS]).then_inc(m["gmx"], 1)
            dve.wait_ge(m["gmx"], l * ADDS["gmx"] + 4)
            dve.wait_ge(m["dg"], l * ADDS["dg"] + PAIRS)
            nc.vector.tensor_tensor(kneg, diag[:, :, 1, :], kmax_all.unsqueeze(1).to_broadcast([P, TILES, HEADS]), ALU.add).then_inc(m["gmx"], 1)
            dve.wait_ge(m["gmx"], l * ADDS["gmx"] + 5)
            nc.vector.tensor_scalar(kneg, kneg, -1.0, None, ALU.mult).then_inc(m["kneg"], 1)
            if l == 0:
                edge_index_dve(dve)

        def attn1_pe(pe, l):
            pe.wait_ge(m["pj"], l * ADDS["pj"] + 32)
            if l == 0:
                pe.wait_ge(s_const, CONSTS)
            else:
                pe.wait_ge(g_sem[1]["out"], OUT_DONE)
            for k in range(2):
                mm = nc.tensor.transpose(psum[7][:, 128 * k:128 * k + 128], proj_st[:, k, :], ident[:, :])
            mm.then_inc(m["pjT"], 1)
            pe.wait_ge(m["w"], l * ADDS["w"] + W_LOADS)
            pe.wait_ge(m["pjS"], l * ADDS["pjS"] + 4)
            if l == 0:
                pe.sem_inc(m["dg"], 1)
            if l == 0:
                pe.sem_inc(m["sq"], 4)
            if l == 0:
                pe.sem_inc(m["k"], 2)
            if l == 0:
                pe.sem_inc(m["kd"], 2)
            with pe.Fori(0, PAIRS) as i:
                pe.wait_ge(m["z"], l * ADDS["z"] + i * 2 + 2)
                pe.wait_ge(m["dg"], l * ADDS["dg"] + i + 1)
                for c in range(KC):
                    for j in range(2):
                        mm = nc.tensor.transpose(psum[c // 2][:, 256 * (c % 2) + P * j:256 * (c % 2) + P * j + P],
                                                 zst[:, j, 128 * c:128 * c + 128], ident[0:P, 0:P])
                    mm.then_inc(m["yT_pe"], 1)
                pe.wait_ge(m["yT"], l * ADDS["yT"] + i * KC + KC)
                for c in range(KC):
                    pe.wait_ge(m["sq"], l * ADDS["sq"] + i * KC * 2 + 2 * c + 1)
                    for k in range(KC):
                        mm = nc.tensor.matmul(psum[2 + c % 2][:, 0:PT], wreg[:, 0, 512 * k + 128 * c:512 * k + 128 * c + 128],
                                              y_t[:, k, :], start=(k == 0), stop=(k == KC - 1))
                    mm.then_inc(m["q_pe"], 1)
                    pe.wait_ge(m["k"], l * ADDS["k"] + i * KC + c + 1)
                    for k in range(KC):
                        mm = nc.tensor.matmul(psum[4 + c % 2][:, 0:PT], wreg[:, 1, 512 * k + 128 * c:512 * k + 128 * c + 128],
                                              y_t[:, k, :], start=(k == 0), stop=(k == KC - 1))
                    mm.then_inc(m["k_pe"], 1)
                for j in range(2):
                    pe.wait_ge(m["kd"], l * ADDS["kd"] + i * 8 + j + 1)
                    for k in range(KC):
                        mm = nc.tensor.matmul(psum[6 + j][0:P, :], y_t[:, k, P * j:P * j + P], wreg[:, 2, 512 * k:512 * k + 512],
                                              start=(k == 0), stop=(k == KC - 1))
                    mm.then_inc(m["v_pe"], 1)
                pe.wait_ge(m["sq"], l * ADDS["sq"] + i * KC * 2 + 2 * KC + 4)
                for j in range(2):
                    for s in range(2):
                        for c in range(KC):
                            mm = nc.tensor.matmul(psum[0][0:P, 16 * j + 8 * s:16 * j + 8 * s + 8], sq[:, s, c, P * j:P * j + P],
                                                  headsel[:, c, :], start=(c == 0), stop=(c == KC - 1), skip_group_check=True)
                mm.then_inc(m["dg_pe"], 1)
                pe.wait_ge(m["v"], l * ADDS["v"] + i * 2 + 2)
                for n in range(8):
                    j, c = n // 4, n % 4
                    if n >= 2:
                        pe.wait_ge(m["kd"], l * ADDS["kd"] + i * 8 + n + 1)
                    nc.tensor.matmul(psum[6 + n % 2][0:P, :], k_t[:, c, P * j:P * j + P], projbd[:, :], start=True, stop=True).then_inc(m["kd_pe"], 1)
            pe.wait_ge(m["gmx"], l * ADDS["gmx"] + 1)
            pe.wait_ge(m["dg"], l * ADDS["dg"] + 1 + PAIRS)
            nc.tensor.transpose(psum[0][0:HEADS, 0:P], kmax_all, ident[0:P, 0:P]).then_inc(m["gmx_pe"], 1)
            pe.wait_ge(m["gmx"], l * ADDS["gmx"] + 3)
            nc.tensor.matmul(psum[1][0:P, 0:HEADS], ones[:, :], kmax_d, start=True, stop=True).then_inc(m["gmx_pe"], 1)

        def attn1_act(act, l):
            act.wait_ge(m["w"], l * ADDS["w"] + W_LOADS)
            with act.Fori(0, PAIRS) as i:
                for c in range(KC):
                    act.wait_ge(m["yT_pe"], l * ADDS["yT_pe"] + i * KC + 2 * (c // 2) + 2 + KC)
                    nc.scalar.activation(y_t[:, c, :], psum[c // 2][:, 256 * (c % 2):256 * (c % 2) + PT], ACT.Identity,
                                         bias=c_b1[:, c:c + 1], scale=c_g1[:, c:c + 1]).then_inc(m["yT"], 1)
                for c in range(KC):
                    act.wait_ge(m["q_pe"], l * ADDS["q_pe"] + i * KC + c + 1)
                    nc.scalar.activation(q_t[:, c, ds(i * PT, PT)], psum[2 + c % 2][:, 0:PT], ACT.Identity,
                                         bias=c_bq[:, c:c + 1])
                    nc.scalar.activation(sq[:, 0, c, :], psum[2 + c % 2][:, 0:PT], ACT.Square, bias=c_bq[:, c:c + 1]).then_inc(m["sq"], 1)
                    act.wait_ge(m["k"], l * ADDS["k"] + i * KC + c + 3)
                    nc.scalar.activation(sq[:, 1, c, :], k_t[:, c, :], ACT.Square).then_inc(m["sq"], 1)
                for n in range(8):
                    j, c = n // 4, n % 4
                    act.wait_ge(m["kmx"], l * ADDS["kmx"] + i * 8 + n + 1)
                    nc.scalar.activation(sq1(kdash[:, ds(i * 2 + j, 1), 512 * c:512 * c + 512]), psum[6 + n % 2][0:P, :],
                                         ACT.Copy).then_inc(m["kd"], 1)

        def attn2_act(act, l):
            act.wait_ge(m["kneg"], l * ADDS["kneg"] + 1)
            act.wait_ge(m["kd"], l * ADDS["kd"] + 2 + 4 * TILES)
            if l == 0:
                act.sem_inc(m["ctx_pe"], 2)
            with act.Fori(0, PAIRS) as i:
                for j in range(2):
                    act.wait_ge(m["ctx_pe"], l * ADDS["ctx_pe"] + i * 2 + j + 1)
                    for hh in range(HEADS):
                        op = nc.scalar.activation(kfeat[:, j, FEATS * hh:FEATS * hh + FEATS],
                                                  sq1(kdash[:, ds(i * 2 + j, 1), FEATS * hh:FEATS * hh + FEATS]), ACT.Exp,
                                                  bias=sq1(kneg[:, ds(i * 2 + j, 1), hh:hh + 1]))
                    op.then_inc(m["kx"], 1)

        def attn2_dve(dve, l):
            with dve.Fori(0, PAIRS) as i:
                for j in range(2):
                    dve.wait_ge(m["kx"], l * ADDS["kx"] + i * 2 + j + 1)
                    nc.vector.tensor_scalar(kfeat[:, j, :], kfeat[:, j, :], EPS_K, None, ALU.add).then_inc(m["kf"], 1)
            dve.wait_ge(m["ctx_pe"], l * ADDS["ctx_pe"] + 2 + TILES)
            for b in range(4):
                nc.vector.tensor_copy(ctx_sb[:, 4 * b:4 * b + 4, :].rearrange("p u d -> p (u d)"), psum[b][:, 0:4 * (HD + 1)]).then_inc(m["ctx"], 1)

        def attn2_pe(pe, l):
            pe.wait_ge(m["gmx"], l * ADDS["gmx"] + 4)
            pe.wait_ge(m["sq"], l * ADDS["sq"] + 4 + 2 * KC * PAIRS)
            for b in range(4):
                nc.tensor.matmul(psum[b][:, 0:4 * (HD + 1)], zeros[:, :], wreg[:, 0, 0:4 * (HD + 1)], start=True, stop=False, skip_group_check=True)
            with pe.Fori(0, PAIRS) as i:
                for j in range(2):
                    pe.wait_ge(m["kf"], l * ADDS["kf"] + i * 2 + j + 1)
                    for u in range(2 * HEADS):
                        mm = nc.tensor.matmul(psum[u // 4][:, (HD + 1) * (u % 4):(HD + 1) * (u % 4 + 1)], kfeat[:, j, 128 * u:128 * u + 128],
                                              v_aug[:, ds(i * 2 + j, 1), u // 2, :].rearrange("p o d -> p (o d)"),
                                              start=False, stop=True, skip_group_check=True)
                    mm.then_inc(m["ctx_pe"], 1)

        STEPS = 2 * KC

        def attn3_dve(dve, l):
            dve.wait_ge(m["ctx_pe"], l * ADDS["ctx_pe"] + 2 + TILES)
            with dve.Fori(0, PAIRS) as i:
                nc.vector.tensor_copy(q_st, q_t[:, :, ds(i * PT, PT)]).then_inc(m["qs"], 1)

                def normalize(j):
                    dve.wait_ge(m["o_pe"], l * ADDS["o_pe"] + i * 2 + j + 1)
                    for b in range(2):
                        nc.vector.reciprocal(rden[:, j, 4 * b:4 * b + 4].unsqueeze(2),
                                             psum[4 + b][0:P, 0:4 * (HD + 1)].rearrange("p (h d) -> p h d", h=4)[:, :, HD:HD + 1]).then_inc(m["rd"], 1)
                    dve.wait_ge(m["rd"], l * ADDS["rd"] + i * 4 + 2 * j + 2)
                    for b in range(2):
                        nc.vector.tensor_tensor(o_sb[:, j, 256 * b:256 * b + 256].rearrange("p (h d) -> p h d", h=4),
                                                psum[4 + b][0:P, 0:4 * (HD + 1)].rearrange("p (h d) -> p h d", h=4)[:, :, 0:HD],
                                                rden[:, j, 4 * b:4 * b + 4].unsqueeze(2).to_broadcast([P, 4, HD]), ALU.mult).then_inc(m["o"], 1)

                def residual(j):
                    ht = sq1(h[:, ds(i * 2 + j, 1), :])
                    dve.wait_ge(m["at_pe"], l * ADDS["at_pe"] + i * 2 + j + 1)
                    nc.vector.tensor_tensor(ht, psum[7][0:P, :], ht, ALU.add).then_inc(m["hat"], 1)
                    dve.wait_ge(m["hat"], l * ADDS["hat"] + i * 4 + 2 * j + 3)
                    nc.vector.tensor_tensor(ht, ht, b_o, ALU.add).then_inc(m["hat"], 1)

                for n in range(STEPS + 1):
                    if n < STEPS:
                        j, c = n // KC, n % KC
                        dve.wait_ge(m["qd_pe"], l * ADDS["qd_pe"] + i * STEPS + n + 1)
                        nc.vector.tensor_reduce(qmax[:, n % 2, :], psum[n % 2][0:P, :].rearrange("p (s m) -> p s m", s=2), AX, ALU.max).then_inc(m["qm"], 1)
                        dve.wait_ge(m["qm"], l * ADDS["qm"] + i * STEPS + n + 1)
                        nc.vector.scalar_tensor_tensor(qneg[:, n % 2, :], qmax[:, n % 2, :], -1.0,
                                                       diag[:, ds(i * 2 + j, 1), 0, 2 * c:2 * c + 2].rearrange("p o s -> p (o s)"),
                                                       ALU.mult, ALU.subtract).then_inc(m["qn"], 1)
                    if n >= 1:
                        dve.wait_ge(m["qT_pe"], l * ADDS["qT_pe"] + i * STEPS + n + 2)
                        nc.vector.tensor_scalar(qfeat_t[:, (n - 1) % 2, :], psum[2 + (n - 1) % 2][:, 0:4 * P], EPS_K, None, ALU.add).then_inc(m["qT"], 1)
                    if n == 6:
                        normalize(0)
                residual(0)
                normalize(1)
                residual(1)

        def attn3_act(act, l):
            if l == 0:
                act.sem_inc(m["qT_pe"], 2)
            with act.Fori(0, PAIRS) as i:
                def turn(j):
                    act.wait_ge(m["oT_pe"], l * ADDS["oT_pe"] + i * 2 + j + 1)
                    nc.scalar.activation(o_t[:, j, :], psum[6][:, 0:4 * P], ACT.Copy).then_inc(m["oT"], 1)
                for n in range(STEPS):
                    act.wait_ge(m["qn"], l * ADDS["qn"] + i * STEPS + n + 1)
                    act.wait_ge(m["qT_pe"], l * ADDS["qT_pe"] + i * STEPS + n + 1)
                    for s in range(2):
                        op = nc.scalar.activation(qfeat[:, n % 2, FEATS * s:FEATS * s + FEATS], psum[n % 2][0:P, FEATS * s:FEATS * s + FEATS],
                                                  ACT.Exp, bias=qneg[:, n % 2, s:s + 1])
                    op.then_inc(m["qx"], 1)
                turn(0)
                turn(1)

        def attn3_pe(pe, l):
            pe.wait_ge(m["ctx"], l * ADDS["ctx"] + 4)
            pe.wait_ge(m["w"], l * ADDS["w"] + W_LOADS + 16)
            if l == 0:
                pe.sem_inc(m["qx"], 2)
            if l == 0:
                pe.sem_inc(m["qT"], 2)
            if l == 0:
                pe.sem_inc(m["o"], 2)
            if l == 0:
                pe.sem_inc(m["oT"], 1)
            if l == 0:
                pe.sem_inc(m["hat"], 2)
            with pe.Fori(0, PAIRS) as i:
                pe.wait_ge(m["qs"], l * ADDS["qs"] + i + 1)

                def out_proj(j):
                    pe.wait_ge(m["o"], l * ADDS["o"] + i * 4 + 2 * j + 4)
                    pe.wait_ge(m["oT"], l * ADDS["oT"] + i * 2 + j + 1)
                    for k in range(KC):
                        mm = nc.tensor.transpose(psum[6][:, P * k:P * k + P], o_sb[:, j, 128 * k:128 * k + 128], ident[0:P, 0:P])
                    mm.then_inc(m["oT_pe"], 1)

                def out_mm(j):
                    pe.wait_ge(m["oT"], l * ADDS["oT"] + i * 2 + j + 2)
                    pe.wait_ge(m["hat"], l * ADDS["hat"] + i * 4 + 2 * j + 1)
                    for k in range(KC):
                        mm = nc.tensor.matmul(psum[7][0:P, :], o_t[:, j, P * k:P * k + P], wreg[:, 3, 512 * k:512 * k + 512],
                                              start=(k == 0), stop=(k == KC - 1))
                    mm.then_inc(m["at_pe"], 1)

                for n in range(STEPS + 2):
                    if n < STEPS:
                        j, c = n // KC, n % KC
                        pe.wait_ge(m["qx"], l * ADDS["qx"] + i * STEPS + n + 1)
                        nc.tensor.matmul(psum[n % 2][0:P, :], q_st[:, c, P * j:P * j + P], projbd[:, :], start=True, stop=True).then_inc(m["qd_pe"], 1)
                    if 1 <= n <= STEPS:
                        pe.wait_ge(m["qx"], l * ADDS["qx"] + i * STEPS + n + 2)
                        pe.wait_ge(m["qT"], l * ADDS["qT"] + i * STEPS + n)
                        for q in range(4):
                            mm = nc.tensor.transpose(psum[2 + (n - 1) % 2][:, P * q:P * q + P], qfeat[:, (n - 1) % 2, 128 * q:128 * q + 128], ident[0:P, 0:P])
                        mm.then_inc(m["qT_pe"], 1)
                    if n >= 2:
                        j, c = (n - 2) // KC, (n - 2) % KC
                        pe.wait_ge(m["qT"], l * ADDS["qT"] + i * STEPS + n + 1)
                        if c == 0:
                            pe.wait_ge(m["o"], l * ADDS["o"] + i * 4 + 2 * j + 2)
                        for s in range(2):
                            hh = 2 * c + s
                            for q in range(2):
                                mm = nc.tensor.matmul(psum[4 + hh // 4][0:P, (HD + 1) * (hh % 4):(HD + 1) * (hh % 4 + 1)],
                                                      qfeat_t[:, n % 2, P * (2 * s + q):P * (2 * s + q) + P], ctx_sb[:, 2 * hh + q, :],
                                                      start=(q == 0), stop=(q == 1), skip_group_check=True)
                        if c == KC - 1:
                            mm.then_inc(m["o_pe"], 1)
                out_proj(0)
                out_mm(0)
                out_proj(1)
                out_mm(1)

        LN2 = 4 + RSQ
        F1_BANKS = (2, 3, 4, 7)

        def ffn_z(dve, l, i, mean, rstd):
            dve.wait_ge(m["y2_pe"], l * ADDS["y2_pe"] + i * KC + KC)
            for j in range(2):
                nc.vector.tensor_scalar(zst[:, j, :], sq1(h[:, ds(i * 2 + j, 1), :]), mean[j], rstd[j],
                                        ALU.subtract, ALU.mult).then_inc(m["z2"], 1)

        def ffn_take(dve, l, i):
            for j in range(2):
                ht = sq1(h[:, ds(i * 2 + j, 1), :])
                dve.wait_ge(m["f2_pe"], l * ADDS["f2_pe"] + i * 2 + j + 1)
                nc.vector.tensor_tensor(ht, psum[5 + j][0:P, :], ht, ALU.add).then_inc(m["hf"], 1)
                dve.wait_ge(m["hf"], l * ADDS["hf"] + i * 4 + 2 * j + 3)
                nc.vector.tensor_tensor(ht, ht, b_2, ALU.add).then_inc(m["hf"], 1)

        def mlp_dve(dve):
            dve.wait_ge(m["qs"], PAIRS)
            nc.vector.memset(qv[:, 0:8192], 0.0).then_inc(s_comb0, 1)
            dve.wait_ge(s_comb0, 1)
            dve.wait_ge(s_att, 32)
            dve.wait_ge(m["hat"], 2 + 2 * TILES)
            dve.wait_ge(m["mw"], 48)
            dve.sem_inc(m["y2_pe"], KC)
            with dve.Fori(0, PAIRS) as i:
                for j in range(2):
                    nc.vector.bn_stats(st6[:, j, :], sq1(h[:, ds(i * 2 + j, 1), :])).then_inc(m["ln2"], 1)
                dve.wait_ge(m["ln2"], i * LN2 + 2)
                hold_dve()
                for j in range(2):
                    nc.vector.bn_aggr(mv[:, j, :], st6[:, j, :]).then_inc(m["ln2"], 1)
                dve.wait_ge(m["ln2"], i * LN2 + 4)
                rsqrt(dve, m["ln2"], i * LN2 + 4, mv[:, 0:2, 1], 0, 2)
                dve.wait_ge(m["ln2"], i * LN2 + LN2)
                ffn_z(dve, 0, i, [mv[:, j, 0:1] for j in range(2)], [rs[:, 0, j:j + 1] for j in range(2)])
                for n in range(BLOCKS):
                    gl, b = n // (BLOCKS // 2), n % (BLOCKS // 2)
                    dve.wait_ge(s_basis[n % BRING], i * (16 * BLOCKS // BRING) + 16 * (n // BRING) + 16)
                    dve.wait_ge(s_comb, i * (2 * BLOCKS) + 2 * n + 2 * BRING)
                    for r in range(RELS):
                        nc.vector.scalar_tensor_tensor(wrel[:, gl, r, :], wreg[:, n % BRING, :], att_b[:, gl, ds(i * (BLOCKS // 2) + (r * BASES + b), 1)],
                                                       wrel[:, gl, r, :], ALU.mult, ALU.add).then_inc(s_comb, 1)
                ffn_take(dve, 0, i)
            dve.wait_ge(m["hf"], 2 + 2 * TILES)

        def ffn_pe(pe, l, i):
            pe.wait_ge(m["z2"], l * ADDS["z2"] + i * 2 + 2)
            for c in range(KC):
                for j in range(2):
                    mm = nc.tensor.transpose(psum[c // 2][:, 256 * (c % 2) + P * j:256 * (c % 2) + P * j + P],
                                             zst[:, j, 128 * c:128 * c + 128], ident[0:P, 0:P])
                mm.then_inc(m["y2_pe"], 1)
            pe.wait_ge(m["y2"], l * ADDS["y2"] + i * KC + KC)
            pe.wait_ge(m["hf"], l * ADDS["hf"] + i * 4 + 2)
            for half in range(2):
                for n in range(HH * half, HH * half + HH):
                    pe.wait_ge(m["f1"], l * ADDS["f1"] + i * HC + n + 1)
                    for k in range(KC):
                        mm = nc.tensor.matmul(psum[F1_BANKS[n % 4]][:, 0:PT], w1_sb[:, k, 128 * n:128 * n + 128], y_t[:, k, :],
                                              start=(k == 0), stop=(k == KC - 1))
                    mm.then_inc(m["f1_pe"], 1)
                for j in range(2):
                    for k in range(HH * half, HH * half + HH):
                        if j == 0:
                            pe.wait_ge(m["f1"], l * ADDS["f1"] + i * HC + k + 5)
                        mm = nc.tensor.matmul(psum[5 + j][0:P, :], act_t[:, k % HH, P * j:P * j + P], w2_sb[:, k, :],
                                              start=(k == 0), stop=(k == HC - 1))
                    if half == 1:
                        mm.then_inc(m["f2_pe"], 1)

        def mlp_start_pe(pe, l):
            pe.wait_ge(m["mw"], l * ADDS["mw"] + 48)
            pe.wait_ge(m["hat"], l * ADDS["hat"] + 2 + 2 * TILES)

        def mlp_pe(pe):
            mlp_start_pe(pe, 0)
            pe.sem_inc(m["f1"], 4)
            pe.sem_inc(m["hf"], 2)
            with pe.Fori(0, PAIRS) as i:
                ffn_pe(pe, 0, i)

        def ffn_act(act, l, i):
            for c in range(KC):
                act.wait_ge(m["y2_pe"], l * ADDS["y2_pe"] + i * KC + 2 * (c // 2) + 2 + KC)
                nc.scalar.activation(y_t[:, c, :], psum[c // 2][:, 256 * (c % 2):256 * (c % 2) + PT], ACT.Identity,
                                     bias=c_b2[:, c:c + 1], scale=c_g2[:, c:c + 1]).then_inc(m["y2"], 1)
            for n in range(HC):
                act.wait_ge(m["f1_pe"], l * ADDS["f1_pe"] + i * HC + n + 1)
                nc.scalar.activation(act_t[:, n % HH, :], psum[F1_BANKS[n % 4]][:, 0:PT], ACT.Gelu, bias=c_h1[:, n:n + 1]).then_inc(m["f1"], 1)

        def mlp_act(act):
            with act.Fori(0, PAIRS) as i:
                ffn_act(act, 0, i)

        g_names = "w x xT_pe xT gt_pe gt z_pe z r agg out xin st".split()
        g_sem = [{n: sem(f"gcn{gl}_{n}") for n in g_names} for gl in range(2)]
        s_slab = [[sem(f"gcn{gl}_slab_{j}") for j in range(2)] for gl in range(2)]
        OUT_DONE = 4 + 2 * TILES
        COMB_DONE = 2 * BRING + 2 * 2 * BASES
        b_g = b_v
        xin = view(stage, 2024, [2, DIM], P)

        def gcn_sp(sp, gl):
            g = g_sem[gl]
            if gl == 0:
                sp.wait_ge(s_comb, COMB_DONE)
                sp.wait_ge(s_adj, 16 * GROUPS)
                sp.wait_ge(m["hf"], 2 + 2 * TILES)
                sp.wait_ge(s_xnw, 16)
            else:
                sp.wait_ge(g_sem[0]["r"], 2 + TILES)
                sp.wait_ge(g_sem[0]["agg"], 2 + TILES)
            sp.dma_start(root_sb, a[f"L0_gnn_root{gl + 1}"].rearrange("(k p) n -> p k n", p=128)).then_inc(g["w"], 16)
            for r in range(RELS):
                sp.dma_start(c_gate[:, :, r], a[f"L0_gnn_gate_w{gl + 1}"][r].rearrange("(k p) o -> p (k o)", p=128), allow_slow_non_contiguous=True).then_inc(g["w"], 16)
            sp.dma_start(b_g, a[f"L0_gnn_bias{gl + 1}"].partition_broadcast(P)).then_inc(g["w"], 16)
            if gl == 0:
                with sp.Fori(0, PAIRS) as i:
                    sp.wait_ge(g["xT_pe"], i * 2 + 2)
                    sp.dma_start(gx, tok(xn_d)[:, ds(i * 2, 2), :]).then_inc(g["x"], 16)
            sp.sem_inc(g["agg"], 2)
            with sp.Fori(0, PAIRS) as i:
                for j in range(2):
                    sp.wait_ge(g["agg"], i * 2 + j + 1)
                    sp.dma_start(slab[:, j, :, :], adj_2d[:, ds(i * PT + j * P, P)].rearrange("(c p) r -> p c r", p=P)).then_inc(s_slab[gl][j], 16)
                if gl == 1:
                    sp.wait_ge(g["out"], i * 4 + 8)
                    sp.dma_start(tok(res_d)[:, ds(i * 2, 2), :], gx).then_inc(g["st"], 16)

        def gcn_x_act(act, gl):
            g = g_sem[gl]
            with act.Fori(0, PAIRS) as i:
                act.wait_ge(g["out"], i * 4 + 4)
                act.dma_start(xin, tok(a["x"])[:, ds(i * 2, 2), :]).then_inc(g["xin"], 16)

        def gcn_pe(pe, gl):
            g = g_sem[gl]
            pe.wait_ge(g["w"], 64)
            pe.wait_ge(m["hf"], 2 + 2 * TILES)
            pe.sem_inc(g["z"], 4)
            pe.sem_inc(g["r"], 2)
            with pe.Fori(0, PAIRS) as i:
                pe.wait_ge(g["x"], (i + 1) * (16 if gl == 0 else 1))
                for j in range(2):
                    pe.wait_ge(g["gt"], i * 2 + j + 1)
                    for k in range(KC):
                        mm = nc.tensor.transpose(psum[j][:, P * k:P * k + P], gx[:, j, 128 * k:128 * k + 128], ident[0:P, 0:P])
                    mm.then_inc(g["xT_pe"], 1)
                for j in range(2):
                    pe.wait_ge(g["xT"], i * 2 + j + 1)
                    for k in range(KC):
                        mm = nc.tensor.matmul(psum[j][0:P, 500:502], gx_t[:, j, P * k:P * k + P], c_gate[:, k, :], start=(k == 0), stop=(k == KC - 1))
                    mm.then_inc(g["gt_pe"], 1)
                    for r in range(RELS):
                        pe.wait_ge(g["z"], i * 4 + 2 * j + r + 1)
                        for k in range(KC):
                            mm = nc.tensor.matmul(psum[2 + 3 * j + r][0:P, :], gx_t[:, j, P * k:P * k + P], wrel[:, gl, r, 512 * k:512 * k + 512],
                                                  start=(k == 0), stop=(k == KC - 1))
                        mm.then_inc(g["z_pe"], 1)
                    pe.wait_ge(g["r"], i * 2 + j + 1)
                    for k in range(KC):
                        mm = nc.tensor.matmul(psum[4 + 3 * j][0:P, :], gx_t[:, j, P * k:P * k + P], root_sb[:, k, :], start=(k == 0), stop=(k == KC - 1))
                    mm.then_inc(g["z_pe"], 1)
            pe.wait_ge(g["z"], 4 + 2 * TILES)
            pe.wait_ge(g["gt"], 2 + TILES)
            pe.sem_inc(g["out"], 4)
            with pe.Fori(0, PAIRS) as i:
                for j in range(2):
                    pe.wait_ge(s_slab[gl][j], i * 16 + 16)
                    pe.wait_ge(g["out"], i * 4 + 2 * j + 1)
                    for c in range(COLT):
                        mm = nc.tensor.matmul(psum[j][0:P, :], slab[:, j, c, :], zrel[:, c, :], start=(c == 0), stop=(c == COLT - 1))
                    mm.then_inc(g["agg"], 1)

        def gcn_act(act, gl):
            g = g_sem[gl]
            act.sem_inc(g["gt"], 2)
            act.sem_inc(g["xT_pe"], 2)
            with act.Fori(0, PAIRS) as i:
                for j in range(2):
                    act.wait_ge(g["xT_pe"], i * 2 + j + 3)
                    nc.scalar.activation(gx_t[:, j, :], psum[j][:, 0:4 * P], ACT.Copy).then_inc(g["xT"], 1)
                for j in range(2):
                    act.wait_ge(g["gt_pe"], i * 2 + j + 1)
                    nc.scalar.activation(gate[:, j, :], psum[j][0:P, 500:502], ACT.Sigmoid).then_inc(g["gt"], 1)
                    act.wait_ge(g["gt"], i * 2 + j + 3)
                    for r in range(RELS):
                        act.wait_ge(g["z_pe"], i * 6 + 3 * j + r + 1)
                        nc.scalar.activation(sq1(zrel[:, ds(i * 2 + (j + r * TILES), 1), :]), psum[2 + 3 * j + r][0:P, :], ACT.Identity,
                                             scale=gate[:, j, r:r + 1]).then_inc(g["z"], 1)

        def gcn_dve(dve, gl):
            g = g_sem[gl]
            dve.wait_ge(g["w"], 64)
            dve.sem_inc(g["st"], 16)
            if gl == 1:
                dve.wait_ge(g_sem[0]["out"], OUT_DONE)
            with dve.Fori(0, PAIRS) as i:
                if gl == 1:
                    dve.wait_ge(g["xT_pe"], i * 2 + 2)
                    nc.vector.tensor_copy(gx, x1[:, ds(i * 2, 2), :]).then_inc(g["x"], 1)
                for j in range(2):
                    dve.wait_ge(g["z_pe"], i * 6 + 3 * j + 3)
                    nc.vector.tensor_tensor(sq1(xroot[:, ds(i * 2 + j, 1), :]), psum[4 + 3 * j][0:P, :], b_g, ALU.add).then_inc(g["r"], 1)
            with dve.Fori(0, PAIRS) as i:
                if gl == 1:
                    dve.wait_ge(g["st"], i * 16 + 16)
                for j in range(2):
                    dve.wait_ge(g["agg"], i * 2 + j + 3)
                    t = i * 2 + j
                    dst = sq1(x1[:, ds(t, 1), :]) if gl == 0 else gx[:, j, :]
                    nc.vector.tensor_tensor(dst, psum[j][0:P, :], sq1(xroot[:, ds(t, 1), :]), ALU.add).then_inc(g["out"], 1)
                    dve.wait_ge(g["out"], i * 4 + 2 * j + 5)
                    if gl == 0:
                        nc.vector.tensor_scalar(dst, dst, 0.0, None, ALU.max).then_inc(g["out"], 1)
                    else:
                        dve.wait_ge(g["xin"], i * 16 + 16)
                        nc.vector.tensor_tensor(dst, dst, xin[:, j, :], ALU.add).then_inc(g["out"], 1)

        p_w, p_keys, p_keysT, p_keysS, p_res, p_h, p_ln, p_x, p_xT_pe, p_xT, p_q_pe, p_q, p_s_pe, p_top, p_exp, p_slots, p_vals, p_dn, p_up, p_diag, p_out = (
            sem("mem_" + n) for n in ("weights keys keysT_pe keys_placed residual_in h ln x xT_pe xT q_pe q s_pe top exp slots vals dots_done "
                                      "rows_added weights_placed taken").split())
        s_row = [sem(f"mem_row_{n}") for n in range(RING)]
        s_hold = sem("mem_holds")
        s_out = [sem(f"out_{j}") for j in range(2)]
        keys_st = view(qv, 5592, [2 * PKH, 128])
        slots_of = [slots, biasb[:, 1, 0:SLOTS].bitcast(I32)]
        acc_of = [acc, projbd[0:P, :]]
        QB = 4
        EXP_AT = 48
        TAKE_AT = 40
        LN3 = 4 + RSQ

        def landed(t, j, n):
            return t * (16 * 2 * ROUNDS) + 16 * (j * 2 * ROUNDS + n // RING + 1)

        def mem_sp(sp):
            sp.wait_ge(m["gmx"], ADDS["gmx"] + 5)
            for half in range(2):
                for hh in range(PKH):
                    sp.dma_start(keys_st[:, 2 * hh:2 * hh + 2, HALF * half:HALF * half + HALF],
                                 a["L0_ffn_keys"][hh, half].rearrange("(n p) d -> p n d", p=128)).then_inc(p_keys, 16)
            sp.dma_start(wqf, a["L0_ffn_Wq"].rearrange("(k p) n -> p k n", p=128)).then_inc(p_w, 16)
            sp.dma_start(c_bqf, a["L0_ffn_bq"].rearrange("(h p) -> p h", p=128), allow_slow_non_contiguous=True).then_inc(p_w, 16)
            sp.wait_ge(m["hat"], ADDS["hat"] + 2 + 2 * TILES)
            sp.wait_ge(g_sem[1]["st"], 16 + 16 * PAIRS)
            sp.dma_start(res_p, tok(res_d)[:, 0:2, :]).then_inc(p_res, 16)

            def store(i, j):
                sp.wait_ge(p_out, i * 2 + (j + 2))
                sp.dma_start(tok(out)[:, ds(i * 2 + j, 1), :], acc_of[j].unsqueeze(1)).then_inc(s_out[j], 16)

            with sp.Fori(0, PAIRS - 1) as i:
                sp.wait_ge(p_h, i * 2 + 2)
                sp.dma_start(res_p, tok(res_d)[:, ds(i * 2 + 2, 2), :]).then_inc(p_res, 16)
                store(i, 0)
                store(i, 1)
            store(PAIRS - 1, 0)
            store(PAIRS - 1, 1)
            for j in range(2):
                sp.wait_ge(s_out[j], 16 + 16 * PAIRS)

        def mem_pool(pool):
            pool.wait_ge(m["hat"], ADDS["hat"] + 2 + 2 * TILES)
            for s in range(2):
                nc.gpsimd.memset(keybd[64 * s:64 * s + 64, :, NKEYS * (1 - s):NKEYS * (2 - s)], 0.0).then_inc(p_keysS, 1)
            pool.sem_inc(p_up, RING)
            pool.sem_inc(s_hold, 1)
            pool.sem_inc(p_diag, 1)

            def tile(i, j):
                if j == 0:
                    pool.wait_ge(s_hold, i * (4 * SLOTS // HOLD) + 1)
                pool.wait_ge(p_slots, i * 2 + (j + 1))
                for n in range(2 * SLOTS):
                    s = n % SLOTS
                    if s % HOLD == 0:
                        if (s < RING) == (n < SLOTS):
                            pool.wait_ge(p_up, i * (2 * SLOTS) + (j * SLOTS + s + HOLD))
                        elif n < SLOTS:
                            pool.wait_ge(p_dn, i * (2 * SLOTS) + (j * SLOTS + s - RING + HOLD))
                        else:
                            pool.wait_ge(p_dn, i * (2 * SLOTS) + (j * SLOTS + SLOTS - RING + s + HOLD))
                        hold_pool().then_inc(s_hold, 1)
                    nc.gpsimd.indirect_dma_start(
                        out=ring[n % RING], out_offset=None, in_=a["L0_ffn_w_down" if n < SLOTS else "L0_ffn_w_up"],
                        in_offset=bass.IndirectOffsetOnAxis(ap=slots_of[j][:, s:s + 1], axis=0)).then_inc(s_row[n % RING], 16)

            with pool.Fori(0, PAIRS) as i:
                tile(i, 0)
                tile(i, 1)

        def mem_pe(pe):
            pe.wait_ge(p_keys, 16 * 2 * PKH)
            pe.wait_ge(m["hat"], ADDS["hat"] + 2 + 2 * TILES)
            for u in range(2 * PKH):
                mm = nc.tensor.transpose(psum[2 + u // 4][:, 128 * (u % 4):128 * (u % 4) + 128], keys_st[:, u, :], ident[:, :])
            mm.then_inc(p_keysT, 1)
            pe.wait_ge(p_keysS, 2 + 8)
            mlp_start_pe(pe, 1)
            ffn_pe(pe, 1, 0)
            pe.wait_ge(p_w, 32)
            pe.sem_inc(p_top, 4 * 4)
            pe.sem_inc(p_out, 1)

            def scores(t, j, hh):
                pe.wait_ge(p_q, t * PKH + (j * PKH + hh + 1))
                pe.wait_ge(p_top, t * TOPN + (j * TOPN + 4 * max(hh - 1, 0) + 16))
                nc.tensor.matmul(psum[3 + hh % 2][0:P, :], pq_t[:, hh, :], keybd[:, hh, :], start=True, stop=True).then_inc(p_s_pe, 1)

            def queries(b):
                for hh in range(QB * b, QB * b + QB):
                    for k in range(KC):
                        mm = nc.tensor.matmul(psum[1 + b][:, P * (hh % QB):P * (hh % QB) + P], wqf[:, k, 128 * hh:128 * hh + 128],
                                              xl_t[:, P * k:P * k + P], start=(k == 0), stop=(k == KC - 1), skip_group_check=True)
                mm.then_inc(p_q_pe, 1)

            def turn(t, j):
                pe.wait_ge(p_x, t + (j + 1))
                for k in range(KC):
                    mm = nc.tensor.transpose(psum[0][:, P * k:P * k + P], xl[:, 128 * k:128 * k + 128], ident[0:P, 0:P])
                mm.then_inc(p_xT_pe, 1)
                pe.wait_ge(p_xT, t + (j + 1))

            def rows(t, j, first, n):
                if first == 0:
                    pe.wait_ge(p_out, t + (j + 1))
                for s in range(first, first + n):
                    pe.wait_ge(p_diag, t * SLOTS + (j * SLOTS + s + 2))
                    pe.wait_ge(s_row[s % RING], landed(t, j, SLOTS + s))
                    nc.tensor.matmul(psum[7][0:P, :], diags[:, s % DRING, :], ring[s % RING], start=(s == 0), stop=(s == SLOTS - 1),
                                     skip_group_check=True).then_inc(p_up, 1)

            def tile(t, j):
                turn(t, j + 1)
                queries(0)
                rows(t, j, 0, 4)
                queries(1)
                rows(t, j, 4, 4)
                for hh in range(PKH):
                    scores(t, j + 1, hh)
                    rows(t, j, 8 + 2 * hh, 2)
                rows(t, j, 8 + 2 * PKH, SLOTS - 8 - 2 * PKH)

            turn(0, 0)
            queries(0)
            queries(1)
            for hh in range(PKH):
                scores(0, 0, hh)
            with pe.Fori(0, PAIRS - 1) as i:
                ffn_pe(pe, 1, i + 1)
                tile(i * 2, 0)
                tile(i * 2, 1)
            tile(TILES - 2, 0)
            rows(TILES - 1, 0, 0, SLOTS)

        def mem_act(act):
            act.wait_ge(p_keysT, 1)
            act.wait_ge(p_w, 32)
            for s in range(2):
                for b in range(4):
                    rows = slice(64 * s, 64 * s + 64)
                    nc.scalar.activation(keybd[rows, 2 * b:2 * b + 2, NKEYS * s:NKEYS * s + NKEYS],
                                         psum[2 + b][rows, :].rearrange("p (h m) -> p h m", h=2), ACT.Copy).then_inc(p_keysS, 1)
            ffn_act(act, 1, 0)

            def turn(t, j):
                act.wait_ge(p_xT_pe, t + (j + 1))
                nc.scalar.activation(xl_t, psum[0][:, 0:4 * P], ACT.Copy).then_inc(p_xT, 1)

            def queries(t, j, b):
                act.wait_ge(p_q_pe, t * 2 + (2 * j + b + 1))
                for hh in range(QB * b, QB * b + QB):
                    nc.scalar.activation(pq_t[:, hh, :], psum[1 + b][:, P * (hh % QB):P * (hh % QB) + P], ACT.Identity,
                                         bias=c_bqf[:, hh:hh + 1]).then_inc(p_q, 1)

            def exps(t, j):
                act.wait_ge(p_exp, t * 2 + (2 * j + 1))
                nc.scalar.activation(probs.rearrange("p h k -> p (h k)"), probs.rearrange("p h k -> p (h k)"), ACT.Exp).then_inc(p_exp, 1)

            def place(t, j, first, n):
                if first == 0:
                    act.wait_ge(p_vals, t + (j + 1))
                for s in range(first, first + n):
                    act.wait_ge(p_up, t * SLOTS + (j * SLOTS + s - DRING + 1 + RING))
                    nc.scalar.activation(diags[:, s % DRING, :], ident[0:P, 0:P], ACT.Copy, scale=vals[:, s:s + 1]).then_inc(p_diag, 1)

            def tile(t, j):
                turn(t, j + 1)
                place(t, j, 0, 4)
                queries(t, j + 1, 0)
                place(t, j, 4, 4)
                queries(t, j + 1, 1)
                place(t, j, 8, EXP_AT - 8)
                exps(t, j + 1)
                place(t, j, EXP_AT, SLOTS - EXP_AT)

            turn(0, 0)
            queries(0, 0, 0)
            queries(0, 0, 1)
            exps(0, 0)
            with act.Fori(0, PAIRS - 1) as i:
                ffn_act(act, 1, i + 1)
                tile(i * 2, 0)
                tile(i * 2, 1)
            tile(TILES - 2, 0)
            place(TILES - 1, 0, 0, SLOTS)

        def top_steps(dve, t, par, emit=True):
            n = 16

            def step(ins, sync=True):
                nonlocal n
                ins.then_inc(p_top, 1)
                n += 1
                if sync:
                    dve.wait_ge(p_top, t * TOPN + n)
                    hold_dve()

            for hh in range(PKH):
                dve.wait_ge(p_s_pe, t * PKH + (hh + 1))
                hold_dve()
                for s in range(2):
                    step(nc.vector.max(top_v[:, hh, s, :], psum[3 + hh % 2][0:P, NKEYS * s:NKEYS * s + NKEYS]), sync=(s == 1))
                for s in range(2):
                    step(nc.vector.max_index(top_i[:, hh, s, :], top_v[:, hh, s, :], psum[3 + hh % 2][0:P, NKEYS * s:NKEYS * s + NKEYS]), sync=False)
            dve.wait_ge(p_top, t * TOPN + n)
            step(nc.vector.tensor_copy(top_f, top_i), sync=False)
            step(nc.vector.tensor_tensor(sums.rearrange("p h (i j) -> p h i j", i=TOPK), top_v[:, :, 0, :].unsqueeze(3).to_broadcast([P, PKH, TOPK, TOPK]),
                                         top_v[:, :, 1, :].unsqueeze(2).to_broadcast([P, PKH, TOPK, TOPK]), ALU.add))
            for hh in range(PKH):
                step(nc.vector.max(best_v[:, hh, :], sums[:, hh, :]), sync=(hh == PKH - 1))
            for hh in range(PKH):
                step(nc.vector.max_index(best_i[:, hh, :], best_v[:, hh, :], sums[:, hh, :]), sync=(hh == PKH - 1))
            bi = best_i.rearrange("p h k -> p (h k)")
            step(nc.vector.tensor_scalar(best_hi, bi, 3, None, ALU.logical_shift_right), sync=False)
            step(nc.vector.tensor_scalar(best_lo, bi, 7, None, ALU.bitwise_and))
            step(nc.vector.tensor_copy(hi_f, best_hi), sync=False)
            step(nc.vector.tensor_copy(lo_f, best_lo))
            for s, (where, got) in enumerate(((hi_f, pick_a), (lo_f, pick_b))):
                step(nc.vector.tensor_tensor(pick.rearrange("p h k j -> p (h k) j"), where.unsqueeze(2).to_broadcast([P, SLOTS, TOPK]),
                                             iota8.unsqueeze(1).to_broadcast([P, SLOTS, TOPK]), ALU.is_equal))
                step(nc.vector.tensor_tensor(pick, pick, top_f[:, :, s, :].unsqueeze(2).to_broadcast([P, PKH, TOPK, TOPK]), ALU.mult))
                step(nc.vector.tensor_reduce(got, pick.rearrange("p h k j -> p (h k) j"), AX, ALU.add))
            step(nc.vector.scalar_tensor_tensor(slot_f, pick_a, float(NKEYS), pick_b, ALU.mult, ALU.add))
            nc.vector.tensor_copy(slots_of[par], slot_f).then_inc(p_slots, 1)
            nc.vector.tensor_tensor(probs, best_v, best_v[:, :, 0:1].to_broadcast([P, PKH, TOPK]), ALU.subtract).then_inc(p_exp, 1)
            dve.wait_ge(p_exp, t * 2 + 2)
            step(nc.vector.tensor_reduce(prob_s, probs, AX, ALU.add))
            step(nc.vector.reciprocal(prob_s, prob_s))
            step(nc.vector.tensor_tensor(probs, probs, prob_s.unsqueeze(2).to_broadcast([P, PKH, TOPK]), ALU.mult))

        TOPN = 4 * PKH + 2 + 2 * PKH + 4 + 6 + 1 + 3

        def mem_dve(dve):
            dve.wait_ge(m["hat"], ADDS["hat"] + 2 + 2 * TILES)
            n = ADDS["ln2"]
            for t in range(TILES):
                nc.vector.bn_stats(st6[:, t, :], h[:, t, :]).then_inc(m["ln2"], 1)
            dve.wait_ge(m["ln2"], n + TILES)
            for t in range(TILES):
                nc.vector.bn_aggr(mv[:, t, :], st6[:, t, :]).then_inc(m["ln2"], 1)
            dve.wait_ge(m["ln2"], n + 2 * TILES)
            rsqrt(dve, m["ln2"], n + 2 * TILES, mv[:, :, 1], 0, TILES, row=3)
            dve.wait_ge(m["ln2"], n + 2 * TILES + RSQ)

            def norm2(i):
                ffn_z(dve, 1, i, [mv[:, ds(i * 2 + j, 1), 0:1].rearrange("p a b -> p (a b)") for j in range(2)],
                      [rs[:, 3, ds(i * 2 + j, 1)] for j in range(2)])

            def finish(i):
                ffn_take(dve, 1, i)
                dve.wait_ge(p_res, i * 16 + 16)
                dve.wait_ge(m["hf"], ADDS["hf"] + i * 4 + 6)
                for j in range(2):
                    ht = sq1(h[:, ds(i * 2 + j, 1), :])
                    nc.vector.tensor_tensor(ht, ht, res_p[:, j, :], ALU.add).then_inc(p_h, 1)
                dve.wait_ge(p_h, i * 2 + 2)
                hold_dve()
                for j in range(2):
                    nc.vector.bn_stats(st6[:, j, :], sq1(h[:, ds(i * 2 + j, 1), :])).then_inc(p_ln, 1)
                dve.wait_ge(p_ln, i * LN3 + 2)
                hold_dve()
                for j in range(2):
                    nc.vector.bn_aggr(mvm[:, j, :], st6[:, j, :]).then_inc(p_ln, 1)
                dve.wait_ge(p_ln, i * LN3 + 4)
                rsqrt(dve, p_ln, i * LN3 + 4, mvm[:, :, 1], 0, 2)
                dve.wait_ge(p_ln, i * LN3 + LN3)

            def prepare(t, j):
                nc.vector.tensor_scalar(xl, sq1(h[:, ds(t, 1), :]), mvm[:, j, 0:1], rs[:, 0, j:j + 1], ALU.subtract, ALU.mult).then_inc(p_x, 1)
                top_steps(dve, t, j)

            def dots(i, j, first=0, n=SLOTS):
                for s in range(first, first + n):
                    dve.wait_ge(s_row[s % RING], landed(i * 2, j, s))
                    nc.vector.tensor_tensor_reduce(out=ring[s % RING], in0=ring[s % RING], in1=xl, scale=1.0, scalar=0.0,
                                                   op0=ALU.mult, op1=ALU.add, accum_out=inner[:, s:s + 1]).then_inc(p_dn, 1)

            def weigh(i, j):
                dve.wait_ge(p_dn, i * (2 * SLOTS) + ((j + 1) * SLOTS))
                dve.wait_ge(p_diag, i * (2 * SLOTS) + (j * SLOTS + 1))
                nc.vector.scalar_tensor_tensor(vals, inner, 0.0, probs.rearrange("p h k -> p (h k)"), ALU.max, ALU.mult).then_inc(p_vals, 1)

            def take(i, j):
                dve.wait_ge(s_out[j], i * 16 + 16)
                dve.wait_ge(p_up, i * (2 * SLOTS) + (RING + (j + 1) * SLOTS))
                nc.vector.tensor_tensor(acc_of[j], psum[7][0:P, :], sq1(h[:, ds(i * 2 + j, 1), :]), ALU.add).then_inc(p_out, 1)

            for n in range(TOPK):
                nc.vector.memset(iota8[:, n:n + 1], float(n)).then_inc(m["ln2"], 1)
            dve.wait_ge(m["ln2"], ADDS["ln2"] + 2 * TILES + RSQ + TOPK)
            dve.sem_inc(s_out[0], 16)
            dve.sem_inc(s_out[1], 16)
            norm2(0)
            finish(0)
            prepare(0, 0)
            with dve.Fori(0, PAIRS - 1) as i:
                norm2(i + 1)
                dots(i, 0)
                weigh(i, 0)
                prepare(i * 2 + 1, 1)
                take(i, 0)
                dots(i, 1, 0, TAKE_AT)
                finish(i + 1)
                dots(i, 1, TAKE_AT, SLOTS - TAKE_AT)
                weigh(i, 1)
                prepare(i * 2 + 2, 0)
                take(i, 1)
            dots(PAIRS - 1, 0)
            weigh(PAIRS - 1, 0)
            prepare(TILES - 1, 1)
            take(PAIRS - 1, 0)
            dots(PAIRS - 1, 1)
            weigh(PAIRS - 1, 1)
            take(PAIRS - 1, 1)

        @block.sync
        def _(sp):
            setup_sp(sp)
            mlp_loads_sp(sp, 0)
            bases_sp(sp)
            gcn_sp(sp, 0)
            gcn_sp(sp, 1)
            sp.wait_ge(g_sem[1]["out"], OUT_DONE)
            attn_loads_sp(sp, 1)
            wo_load_sp(sp, 1)
            mlp_loads_sp(sp, 1)
            mem_sp(sp)

        @block.gpsimd
        def _(pool):
            setup_pool()
            adjacency_pool(pool)
            mem_pool(pool)

        @block.tensor
        def _(pe):
            setup_pe(pe)
            for l in range(2):
                attn1_pe(pe, l)
                attn2_pe(pe, l)
                attn3_pe(pe, l)
                if l == 0:
                    mlp_pe(pe)
                    gcn_pe(pe, 0)
                    gcn_pe(pe, 1)
            mem_pe(pe)

        @block.scalar
        def _(act):
            for l in range(2):
                attn1_act(act, l)
                attn2_act(act, l)
                attn3_act(act, l)
                if l == 0:
                    mlp_act(act)
                    gcn_act(act, 0)
                    gcn_act(act, 1)
                    gcn_x_act(act, 1)
            mem_act(act)

        @block.vector
        def _(dve):
            setup_dve(dve)
            for l in range(2):
                attn1_dve(dve, l)
                attn2_dve(dve, l)
                attn3_dve(dve, l)
                if l == 0:
                    mlp_dve(dve)
                    gcn_dve(dve, 0)
                    gcn_dve(dve, 1)
            mem_dve(dve)


def kernel(**inputs):
    import numpy as np
    import concourse.bacc as bacc
    from concourse.bass_utils import run_bass_kernel_spmd

    nc = bacc.Bacc("TRN2", target_bir_lowering=False, num_devices=1)
    arrays, aps = {}, {}
    for name, value in inputs.items():
        v = np.ascontiguousarray(value)
        arrays["in_" + name] = v
        aps[name] = nc.dram_tensor("in_" + name, v.shape, mybir.dt.from_np(v.dtype), kind="ExternalInput").ap()
    out = nc.dram_tensor("out", (NODES, DIM), F32, kind="ExternalOutput").ap()
    build(nc, aps, out)
    r = run_bass_kernel_spmd(nc, [arrays], core_ids=[0])
    return r.results[0]["out"]
```

```python
from contextlib import ExitStack

import concourse.bass as bass
from concourse import mybir

F32 = mybir.dt.float32
I32 = mybir.dt.int32
U32 = mybir.dt.uint32
ALU = mybir.AluOpType
ACT = mybir.ActivationFunctionType
AX = mybir.AxisListType.X
ds = bass.ds

NODES, DIM, EDGES = 1250, 512, 20000
P = 125
TILES = NODES // P
PAIRS = TILES // 2
PT = 2 * P
KC = DIM // 128
BASES, RELS = 30, 2
HEADS, HD, FEATS = 8, 64, 256
HID = 4 * DIM
HC = HID // 128
HH = HC // 2
GROUPS = EDGES // P
CELLS = RELS * NODES * NODES
COLT = RELS * TILES
NORM = HD ** -0.25
EPS_K = 1e-4
EPS_LN = 1e-5
PKH, NKEYS, TOPK, HALF = 8, 256, 8, 64
SLOTS = PKH * TOPK
RING = 16
ROUNDS = SLOTS // RING
DRING = 8
HOLD = 8
MAGIC = float(0x5F3759DF)


def build(nc, a, out):
    with ExitStack() as ctx:
        def sb(name, shape, dt=F32):
            return ctx.enter_context(nc.sbuf_tensor(name, shape, dt))

        def sem(name):
            return ctx.enter_context(nc.semaphore(name))

        def dram(name, shape, dt=F32):
            return nc.dram_tensor(name, shape, dt, kind="Internal").ap()

        adj = dram("adj", [CELLS + 128, 1])
        cells_t = dram("cells_t", [GROUPS, P])
        xn_d = dram("xn_d", [NODES, DIM])
        res_d = dram("res_d", [NODES, DIM])
        adj_zero = adj[0:CELLS, :].rearrange("(z p f w) o -> z p f (w o)", z=5, p=P, f=4)
        adj_2d = adj[0:CELLS, :].rearrange("(k r) o -> k (r o)", r=NODES)

        def tok(ap):
            return ap.rearrange("(t p) d -> p t d", p=P)

        h = sb("h", [P, TILES, DIM])
        ident = sb("ident", [128, 128])
        ones = sb("ones", [HEADS, P])
        zeros = sb("zeros", [128, 128])
        headsel = sb("headsel", [128, KC, HEADS])
        att_b = sb("att_b", [128, 2, RELS * BASES])
        wreg = sb("wreg", [128, 4, 4 * DIM])
        projbd = sb("projbd", [128, 2 * FEATS])
        biasb = sb("biasb", [P, 2, DIM])
        cols = sb("cols", [128, 64])
        big = sb("big", [128, 20480])
        qv = sb("qv", [128, 10200])
        stage = sb("stage", [128, 5120])
        ctx_flat = sb("ctx_flat", [128, 2 * HEADS * (HD + 1)])
        ctx_sb = ctx_flat[:, :].rearrange("p (u d) -> p u d", u=2 * HEADS)
        st6 = sb("st6", [P, TILES, 6])
        mv = sb("mv", [P, TILES, 2])
        rs = sb("rs", [P, 4, TILES])
        small = sb("small", [P, 408])
        psum = [ctx.enter_context(nc.psum_tensor(f"bank{i}", [128, 512], F32)) for i in range(8)]

        def view(region, at, shape, parts=128):
            n = 1
            for s in shape:
                n *= s
            v = region[0:parts, at:at + n]
            if len(shape) == 2:
                v = v.rearrange("p (a b) -> p a b", a=shape[0])
            if len(shape) == 3:
                v = v.rearrange("p (a b c) -> p a b c", a=shape[0], b=shape[1])
            return v

        c_g1, c_b1, c_g2, c_b2, c_bq, c_bk = (cols[:, 4 * i:4 * i + 4] for i in range(6))
        c_h1 = cols[:, 24:24 + HC]
        c_gate = cols[:, 40:48].rearrange("p (k r) -> p k r", k=KC)
        c_bqf = cols[:, 48:56]
        b_v, b_o = (biasb[:, i, :] for i in range(2))
        b_2 = b_v

        zst = view(stage, 0, [2, DIM], P)
        y_t = view(stage, 1024, [KC, PT])
        k_t = view(stage, 2024, [KC, PT])
        sq = view(stage, 3024, [2, KC, PT])
        kfeat = view(stage, 0, [2, HEADS * FEATS], P)
        q_st = view(stage, 0, [KC, PT])
        qfeat = view(big, 16384, [4, DIM], P)
        qfeat_t = view(stage, 2024, [2, 4 * P])
        o_sb = view(stage, 3024, [2, DIM], P)
        o_t = view(stage, 4048, [2, 4 * P])
        kdash = view(big, 0, [TILES, HEADS * FEATS], P)
        q_t = view(qv, 0, [KC, NODES])
        v_aug = qv[0:P, 5000:10200].rearrange("p (t h d) -> p t h d", t=TILES, h=HEADS)
        diag = small[:, 0:160].rearrange("p (t s h) -> p t s h", t=TILES, s=2)
        kmax = small[:, 160:240].rearrange("p (t h) -> p t h", t=TILES)
        kmax_all = small[:, 240:248]
        kneg = small[:, 250:330].rearrange("p (t h) -> p t h", t=TILES)
        qmax = small[:, 372:380].rearrange("p (j s) -> p j s", j=4)
        qneg = small[:, 380:388].rearrange("p (j s) -> p j s", j=4)
        rden = small[:, 340:356].rearrange("p (j h) -> p j h", j=2)
        kmax_t = small[0:8, 360:361]
        kmax_d = small[0:8, 364:372]
        w1_sb = view(big, 0, [KC, HID])
        w2_sb = view(big, 8192, [HC, DIM])
        act_t = view(big, 16384, [HH, PT])
        wrel = qv[:, 0:8192].rearrange("p (l r k) -> p l r k", l=2, r=2)
        zrel = view(big, 0, [COLT, DIM], P)
        xroot = view(big, 10240, [TILES, DIM], P)
        x1 = view(big, 15360, [TILES, DIM], P)
        wflat = wreg[:, :, :].rearrange("p a b -> p (a b)")
        slab = wflat[0:P, 0:5000].rearrange("p (s c r) -> p s c r", s=2, c=COLT)
        root_sb = wflat[:, 5120:7168].rearrange("p (k n) -> p k n", k=KC)
        gx = view(stage, 0, [2, DIM], P)
        gx_t = view(stage, 1024, [2, 4 * P])
        gate = small[:, 400:404].rearrange("p (j r) -> p j r", j=2)
        keybd = wflat[:, 4096:8192].rearrange("p (h n) -> p h n", h=PKH)
        wqf = wflat[:, 0:4096].rearrange("p (k n) -> p k n", k=KC)
        diags = view(stage, 2024, [DRING, P], P)
        res_p = view(stage, 3024, [2, DIM], P)
        ring = [region[0:P, at + DIM * n:at + DIM * n + DIM] for region, at, count in ((qv, 5592, 9), (ctx_flat, 0, 2), (stage, 4048, 2), (big, 18384, 3))
                for n in range(count)]
        mvm = small[:, 0:4].rearrange("p (j s) -> p j s", j=2)
        xl = view(qv, 0, [2, DIM], P)
        acc = view(qv, 1024, [DIM], P)
        xl_t = view(qv, 1536, [4 * P])
        pq_t = view(qv, 2048, [PKH, P])
        top_v = view(qv, 3072, [PKH, 2, TOPK], P)
        top_i = qv[0:P, 3200:3328].bitcast(U32).rearrange("p (h s k) -> p h s k", h=PKH, s=2)
        top_f = view(qv, 3328, [PKH, 2, TOPK], P)
        sums = view(qv, 3456, [PKH, TOPK * TOPK], P)
        best_v = view(qv, 3968, [PKH, TOPK], P)
        best_i = qv[0:P, 4032:4096].bitcast(U32).rearrange("p (h k) -> p h k", h=PKH)
        best_hi = qv[0:P, 4096:4160].bitcast(U32)
        best_lo = qv[0:P, 4160:4224].bitcast(U32)
        hi_f = view(qv, 4224, [PKH * TOPK], P)
        lo_f = view(qv, 4288, [PKH * TOPK], P)
        pick = view(qv, 4352, [PKH, TOPK, TOPK], P)
        pick_a = view(qv, 4864, [SLOTS], P)
        pick_b = view(qv, 4928, [SLOTS], P)
        slot_f = view(qv, 4992, [SLOTS], P)
        slots = qv[0:P, 5056:5120].bitcast(I32)
        probs = view(qv, 5120, [PKH, TOPK], P)
        prob_s = view(qv, 5184, [PKH], P)
        inner = view(qv, 5192, [SLOTS], P)
        vals = view(qv, 5256, [SLOTS], P)
        idx_dn = qv[0:P, 5320:5336].bitcast(I32)
        idx_up = qv[0:P, 5336:5352].bitcast(I32)
        dots = view(qv, 5352, [RING], P)
        wts = view(qv, 5368, [RING], P)
        iota8 = view(qv, 5384, [TOPK], P)
        iota8_u = qv[0:P, 5392:5400].bitcast(I32)

        s_xin = sem("x_loaded")
        s_const = sem("constants_made")
        s_edge = sem("edges_loaded")
        s_cell = sem("cells_step")
        s_cellp = sem("cells_transposed")
        s_cellsb = sem("cells_t_copied")
        s_cellw = sem("cells_t_written")
        s_cellb = sem("cells_broadcast")
        s_code = sem("edge_code_made")
        s_idx = sem("edge_index_made")
        s_adjz = sem("adjacency_zeroed")
        s_stg = sem("group_index_staged")
        s_adj = sem("group_added")
        s_ln = sem("ln0_step")
        s_xnw = sem("xn_written")
        s_att = sem("att_loaded")

        block = ctx.enter_context(nc.Block())

        cellb = big[0:P, :].rearrange("p (c w) -> p c w", c=PAIRS)
        CHUNK = GROUPS // PAIRS
        e_raw = qv[0:P, 5000:5480].bitcast(I32).rearrange("p (s g) -> p s g", s=3)
        e_f = view(qv, 5480, [3, GROUPS], P)
        cell_ts = view(qv, 5960, [2, P])
        cell, code, flag, trash = (view(ctx_flat, 256 + GROUPS * n, [GROUPS], P) for n in range(4))
        wmask = view(ctx_flat, 256 + 4 * GROUPS, [P], P)
        zbuf = wflat[0:P, 6144:6144 + CELLS // (20 * P)]
        e_idx = sb("e_idx", [P, GROUPS], I32)
        e_cnt = sb("e_cnt", [P, GROUPS])
        g_idx = sb("g_idx", [P, 1], I32)
        g_cnt = sb("g_cnt", [P, 1])

        tick = sb("tick", [1, 12 + 2 + 4 * SLOTS // HOLD])
        holds = [0, 0]

        def hold_dve():
            holds[0] = (holds[0] + 1) % 12
            nc.vector.memset(tick[:, holds[0]:holds[0] + 1], 0.0)

        def hold_pool():
            holds[1] += 1
            return nc.gpsimd.tensor_tensor(tick[:, 11 + holds[1]:12 + holds[1]], ones[0:1, 0:1], ones[0:1, 0:1], ALU.add)

        def rsqrt(dve, s, n, src, c0, w, row=0):
            v, y, t = (rs[:, k, c0:c0 + w] for k in (1, row, 2))
            yi, vi = y.bitcast(I32), v.bitcast(I32)
            nc.vector.tensor_scalar(v, src, EPS_LN, None, ALU.add).then_inc(s, 1)
            dve.wait_ge(s, n + 1)
            nc.vector.tensor_scalar(yi, vi, -0.5, MAGIC, ALU.mult, ALU.add).then_inc(s, 1)
            n += 2
            for _ in range(4):
                dve.wait_ge(s, n)
                nc.vector.tensor_tensor(t, y, y, ALU.mult).then_inc(s, 1)
                dve.wait_ge(s, n + 1)
                nc.vector.tensor_tensor(t, t, v, ALU.mult).then_inc(s, 1)
                dve.wait_ge(s, n + 2)
                nc.vector.tensor_scalar(t, t, -0.5, 1.5, ALU.mult, ALU.add).then_inc(s, 1)
                dve.wait_ge(s, n + 3)
                nc.vector.tensor_tensor(y, y, t, ALU.mult).then_inc(s, 1)
                n += 4
            return n
        RSQ = 18
        LN0_DONE = 3 * TILES + RSQ

        def setup_pool():
            nc.gpsimd.memset(ident[:, :], 0.0).then_inc(s_const, 1)
            nc.gpsimd.memset(ones[:, :], 1.0).then_inc(s_const, 1)
            nc.gpsimd.memset(zeros[:, :], 0.0).then_inc(s_const, 1)
            nc.gpsimd.memset(headsel[:, :, :], 0.0).then_inc(s_const, 1)
            nc.gpsimd.memset(wmask, 257.0).then_inc(s_const, 1)
            nc.gpsimd.memset(zbuf, 0.0).then_inc(s_const, 1)
            nc.gpsimd.iota(trash.bitcast(I32), pattern=[[0, GROUPS]], base=CELLS, channel_multiplier=1).then_inc(s_const, 1)
            nc.gpsimd.wait_ge(s_const, 7)
            nc.gpsimd.affine_select(out=ident[:, :], in_=ident[:, :], compare_op=ALU.not_equal, fill=1.0, base=0,
                                    pattern=[[-1, 128]], channel_multiplier=1).then_inc(s_const, 1)
            nc.gpsimd.affine_select(out=wmask, in_=wmask, compare_op=ALU.is_gt, fill=1.0, base=0,
                                    pattern=[[-1, P]], channel_multiplier=1).then_inc(s_const, 1)
            nc.gpsimd.wait_ge(s_const, 9)
            for c in range(KC):
                for s in range(2):
                    nc.gpsimd.memset(headsel[64 * s:64 * s + 64, c, 2 * c + s:2 * c + s + 1], 1.0).then_inc(s_const, 1)
        CONSTS = 9 + 2 * KC

        def adjacency_pool(pool):
            pool.wait_ge(s_idx, 4)
            pool.wait_ge(s_adjz, 5 * 16)

            def add_group(g):
                nc.gpsimd.tensor_copy(g_idx[:, :], e_idx[:, ds(g, 1)]).then_inc(s_stg, 1)
                nc.gpsimd.tensor_copy(g_cnt[:, :], e_cnt[:, ds(g, 1)]).then_inc(s_stg, 1)
                pool.wait_ge(s_stg, g * 2 + 2)
                hold_pool()
                nc.gpsimd.indirect_dma_start(
                    out=adj, out_offset=bass.IndirectOffsetOnAxis(ap=g_idx[:, :], axis=0), in_=g_cnt[:, :],
                    in_offset=None, bounds_check=CELLS + 127, oob_is_err=True, compute_op=ALU.add).then_inc(s_adj, 16)

            add_group(0)
            with pool.Fori(1, GROUPS) as g:
                pool.wait_ge(s_adj, g * 16)
                add_group(g)

        def setup_sp(sp):
            sp.dma_start(h[:, :, :], tok(a["x"])).then_inc(s_xin, 16)
            for n, name in enumerate(("src", "dst", "edge_type_2")):
                sp.dma_start(e_raw[:, n, :], a[name].rearrange("(p g) -> p g", p=P)).then_inc(s_edge, 16)
            sp.dma_start(att_b[:, 0, :], a["L0_gnn_att1"].rearrange("r b -> (r b)").partition_broadcast(128)).then_inc(s_att, 16)
            sp.dma_start(att_b[:, 1, :], a["L0_gnn_att2"].rearrange("r b -> (r b)").partition_broadcast(128)).then_inc(s_att, 16)
            attn_loads_sp(sp, 0)
            sp.wait_ge(s_cellsb, 2)
            sp.dma_start(cells_t[0:128, :], cell_ts[:, 0, :]).then_inc(s_cellw, 16)
            sp.dma_start(cells_t[128:GROUPS, :], cell_ts[0:GROUPS - 128, 1, :]).then_inc(s_cellw, 16)
            sp.wait_ge(s_cellw, 32)
            sp.dma_start(cellb[:, :, 0:CHUNK * P], cells_t.rearrange("g p -> (g p)").partition_broadcast(P).rearrange("q (c w) -> q c w", c=PAIRS)).then_inc(s_cellb, 16)
            sp.wait_ge(s_ln, LN0_DONE)
            sp.dma_start(tok(xn_d), h[:, :, :]).then_inc(s_xnw, 16)
            sp.wait_ge(s_const, 7)
            for n in range(5):
                sp.dma_start(adj_zero[n], zbuf.unsqueeze(1).to_broadcast([P, 4, CELLS // (20 * P)])).then_inc(s_adjz, 16)
            sp.wait_ge(s_adjz, 5 * 16)
            wo_load_sp(sp, 0)

        def setup_dve(dve):
            dve.wait_ge(s_edge, 48)
            nc.vector.tensor_copy(e_f, e_raw).then_inc(s_cell, 1)
            dve.wait_ge(s_cell, 1)
            nc.vector.tensor_scalar(e_f[:, 2, :], e_f[:, 2, :], 0.0, float(NODES), ALU.not_equal, ALU.mult).then_inc(s_cell, 1)
            dve.wait_ge(s_cell, 2)
            nc.vector.tensor_tensor(e_f[:, 2, :], e_f[:, 2, :], e_f[:, 1, :], ALU.add).then_inc(s_cell, 1)
            dve.wait_ge(s_cell, 3)
            nc.vector.scalar_tensor_tensor(cell, e_f[:, 2, :], float(NODES), e_f[:, 0, :], ALU.mult, ALU.add).then_inc(s_cell, 1)
            dve.wait_ge(s_cellp, 1)
            nc.vector.tensor_copy(cell_ts[:, 0, :], psum[0][:, 0:P]).then_inc(s_cellsb, 1)
            nc.vector.tensor_copy(cell_ts[0:GROUPS - 128, 1, :], psum[0][0:GROUPS - 128, 128:128 + P]).then_inc(s_cellsb, 1)
            dve.wait_ge(s_xin, 16)
            for t in range(TILES):
                nc.vector.bn_stats(st6[:, t, :], h[:, t, :]).then_inc(s_ln, 1)
            dve.wait_ge(s_ln, TILES)
            for t in range(TILES):
                nc.vector.bn_aggr(mv[:, t, :], st6[:, t, :]).then_inc(s_ln, 1)
            dve.wait_ge(s_ln, 2 * TILES)
            rsqrt(dve, s_ln, 2 * TILES, mv[:, :, 1], 0, TILES)
            dve.wait_ge(s_ln, 2 * TILES + RSQ)
            for t in range(TILES):
                nc.vector.tensor_scalar(h[:, t, :], h[:, t, :], mv[:, t, 0:1], rs[:, 0, t:t + 1], ALU.subtract, ALU.mult).then_inc(s_ln, 1)

        def merge_dve(dve, i, first, count):
            dve.wait_ge(s_cellb, 16)
            for n in range(first, first + count):
                part = big[0:P, ds(i * 4096 + P * n, P)]
                nc.vector.scalar_tensor_tensor(part, part, cell[:, ds(i * CHUNK + n, 1)], wmask,
                                               ALU.is_equal, ALU.mult, accum_out=code[:, ds(i * CHUNK + n, 1)]).then_inc(s_code, 1)

        def edge_index_dve(dve):
            dve.wait_ge(s_code, GROUPS)
            nc.vector.tensor_copy(e_cnt[:, :], code).then_inc(s_idx, 1)
            nc.vector.tensor_scalar(flag, code, 256.0, None, ALU.is_ge).then_inc(s_cell, 1)
            nc.vector.tensor_copy(trash, trash.bitcast(I32)).then_inc(s_cell, 1)
            dve.wait_ge(s_cell, 6)
            nc.vector.tensor_tensor(trash, trash, cell, ALU.subtract).then_inc(s_idx, 1)
            dve.wait_ge(s_idx, 2)
            nc.vector.tensor_tensor(trash, trash, flag, ALU.mult).then_inc(s_idx, 1)
            dve.wait_ge(s_idx, 3)
            nc.vector.tensor_tensor(e_idx[:, :], trash, cell, ALU.add).then_inc(s_idx, 1)

        def setup_pe(pe):
            pe.wait_ge(s_const, CONSTS)
            pe.wait_ge(s_cell, 4)
            nc.tensor.transpose(psum[0][:, 0:P], cell[:, 0:128], ident[0:P, 0:P])
            nc.tensor.transpose(psum[0][0:GROUPS - 128, 128:128 + P], cell[:, 128:GROUPS], ident[0:P, 0:P]).then_inc(s_cellp, 1)

        ADDS = dict(w=13 * 16, pj=32, pjT=1, pjS=4, stat=1 + 2 * TILES + RSQ, z=TILES, yT_pe=KC * PAIRS, yT=KC * PAIRS, q_pe=KC * PAIRS,
                    sq=2 * KC * PAIRS, k=KC * PAIRS, k_pe=KC * PAIRS, v_pe=TILES, v=TILES, dg_pe=PAIRS, dg=PAIRS,
                    kd_pe=4 * TILES, kmx=4 * TILES, kd=4 * TILES, gmx=5, gmx_pe=2, kneg=1, kx=TILES, kf=TILES, ctx_pe=TILES, ctx=4,
                    qs=PAIRS, qd_pe=4 * TILES, qm=4 * TILES, qn=4 * TILES, qx=4 * TILES, qT_pe=4 * TILES, qT=4 * TILES, o_pe=TILES,
                    rd=2 * TILES, o=2 * TILES, oT_pe=TILES, oT=TILES, at_pe=TILES, hat=2 * TILES, mw=48, ln2=2 * TILES + RSQ,
                    z2=TILES, y2_pe=KC * PAIRS, y2=KC * PAIRS, f1_pe=HC * PAIRS, f1=HC * PAIRS, f2_pe=TILES, hf=2 * TILES)
        m = {name: sem("mix_" + name) for name in ADDS}
        s_comb = sem("bases_added")
        s_comb0 = sem("relation_sums_zeroed")
        s_basis = [sem(f"basis_ring_{n}") for n in range(4)]
        proj_st = ctx_flat[:, 0:256].rearrange("p (k d) -> p k d", k=2)
        W_LOADS = 12 * 16
        BLOCKS = 2 * BASES // PAIRS
        BRING = 4

        def sq1(ap):
            return ap.rearrange("p a b -> p (a b)")

        def wo_load_sp(sp, l):
            sp.wait_ge(m["w"], l * ADDS["w"] + W_LOADS)
            sp.dma_start(wreg[:, 3, :].rearrange("p (k n) -> p k n", k=KC), a["L0_mix_Wo"][l].rearrange("(k p) n -> p k n", p=128)).then_inc(m["w"], 16)

        def attn_loads_sp(sp, l):
            for n, name in enumerate(("Wq", "Wk", "Wv")):
                sp.dma_start(wreg[:, n, :].rearrange("p (k n) -> p k n", k=KC),
                             a["L0_mix_" + name][l].rearrange("(k p) n -> p k n", p=128)).then_inc(m["w"], 16)
            for c, name in ((c_g1, "ln1_g"), (c_b1, "ln1_b"), (c_g2, "ln2_g"), (c_b2, "ln2_b"), (c_bq, "bq"), (c_bk, "bk"), (c_h1, "b1")):
                sp.dma_start(c, a["L0_mix_" + name][l].rearrange("(k p) -> p k", p=128), allow_slow_non_contiguous=True).then_inc(m["w"], 16)
            for b, name in ((b_v, "bv"), (b_o, "bo")):
                sp.dma_start(b, a["L0_mix_" + name][l].partition_broadcast(P)).then_inc(m["w"], 16)
            for s in range(2):
                sp.dma_start(proj_st[:, :, 64 * s:64 * s + 64], a["L0_mix_proj"][l].rearrange("(k p) d -> p k d", p=128)).then_inc(m["pj"], 16)

        def mlp_loads_sp(sp, l):
            sp.wait_ge(m["ctx"], l * ADDS["ctx"] + 4)
            sp.dma_start(w1_sb, a["L0_mix_W1"][l].rearrange("(k p) n -> p k n", p=128)).then_inc(m["mw"], 16)
            sp.dma_start(w2_sb, a["L0_mix_W2"][l].rearrange("(k p) n -> p k n", p=128)).then_inc(m["mw"], 16)
            sp.dma_start(b_2, a["L0_mix_b2"][l].partition_broadcast(P)).then_inc(m["mw"], 16)

        def bases_sp(sp, l=0):
            sp.wait_ge(m["hat"], 2 + 2 * TILES)
            sp.sem_inc(s_comb, 2 * BRING)
            with sp.Fori(0, PAIRS) as i:
                for n in range(BLOCKS):
                    gl, b = n // (BLOCKS // 2), n % (BLOCKS // 2)
                    sp.wait_ge(s_comb, i * (2 * BLOCKS) + 2 * n + 2)
                    sp.dma_start(wreg[:, n % BRING, :].rearrange("p (k n) -> p k n", k=KC),
                                 a[f"L0_gnn_basis{gl + 1}"][ds(i * (BLOCKS // 2) + b, 1), :, :].rearrange("o (k p) n -> p (o k) n", p=128)
                                 ).then_inc(s_basis[n % BRING], 16)

        KD_BANKS = (6, 7, 4, 5)

        def attn1_dve(dve, l):
            dve.wait_ge(m["pjT"], l * ADDS["pjT"] + 1)
            for s in range(2):
                rows = slice(64 * s, 64 * s + 64)
                nc.vector.memset(projbd[rows, FEATS * (1 - s):FEATS * (2 - s)], 0.0).then_inc(m["pjS"], 1)
                nc.vector.tensor_scalar(projbd[rows, FEATS * s:FEATS * s + FEATS], psum[7][rows, 0:FEATS], NORM, None,
                                        ALU.mult).then_inc(m["pjS"], 1)
            if l == 1:
                dve.wait_ge(g_sem[1]["z"], 4 + 2 * TILES)
                dve.wait_ge(g_sem[1]["st"], 16 + 16 * PAIRS)
            else:
                dve.wait_ge(s_cellw, 32)
                dve.wait_ge(s_const, CONSTS)
                dve.wait_ge(s_ln, LN0_DONE)
            nc.vector.memset(v_aug[:, :, :, HD:HD + 1].rearrange("p t h o -> p (t h) o"), 1.0).then_inc(m["stat"], 1)
            for t in range(TILES):
                nc.vector.bn_stats(st6[:, t, :], h[:, t, :]).then_inc(m["stat"], 1)
            dve.wait_ge(m["stat"], l * ADDS["stat"] + 1 + TILES)
            for t in range(TILES):
                nc.vector.bn_aggr(mv[:, t, :], st6[:, t, :]).then_inc(m["stat"], 1)
            dve.wait_ge(m["stat"], l * ADDS["stat"] + 1 + 2 * TILES)
            n = rsqrt(dve, m["stat"], l * ADDS["stat"] + 1 + 2 * TILES, mv[:, :, 1], 0, TILES)
            dve.wait_ge(m["stat"], n)
            dve.wait_ge(m["w"], l * ADDS["w"] + W_LOADS)
            if l == 0:
                dve.sem_inc(m["yT_pe"], KC)
            def norm1(i):
                dve.wait_ge(m["yT_pe"], l * ADDS["yT_pe"] + i * KC + KC)
                for j in range(2):
                    nc.vector.tensor_scalar(zst[:, j, :], sq1(h[:, ds(i * 2 + j, 1), :]), mv[:, ds(i * 2 + j, 1), 0:1].rearrange("p a b -> p (a b)"),
                                            rs[:, 0, ds(i * 2 + j, 1)], ALU.subtract, ALU.mult).then_inc(m["z"], 1)

            def pair(i, last):
                for c in range(KC):
                    dve.wait_ge(m["k_pe"], l * ADDS["k_pe"] + i * KC + c + 1)
                    nc.vector.tensor_scalar(k_t[:, c, :], psum[4 + c % 2][:, 0:PT], c_bk[:, c:c + 1], None, ALU.add).then_inc(m["k"], 1)
                    if l == 0:
                        merge_dve(dve, i, c * CHUNK // KC, CHUNK // KC)
                for j in range(2):
                    dve.wait_ge(m["v_pe"], l * ADDS["v_pe"] + i * 2 + j + 1)
                    nc.vector.tensor_tensor(v_aug[:, ds(i * 2 + j, 1), :, 0:HD].rearrange("p o h d -> p (o h) d"),
                                            psum[6 + j][0:P, :].rearrange("p (h d) -> p h d", h=HEADS),
                                            b_v.rearrange("p (h d) -> p h d", h=HEADS), ALU.add).then_inc(m["v"], 1)
                if not last:
                    norm1(i + 1)
                dve.wait_ge(m["dg_pe"], l * ADDS["dg_pe"] + i + 1)
                nc.vector.tensor_scalar(diag[:, ds(i * 2, 2), :, :].rearrange("p t s h -> p (t s h)"), psum[0][0:P, 0:32],
                                        0.5 * NORM * NORM, None, ALU.mult).then_inc(m["dg"], 1)
                for n in range(8):
                    j, c = n // 4, n % 4
                    dve.wait_ge(m["kd_pe"], l * ADDS["kd_pe"] + i * 8 + n + 1)
                    nc.vector.tensor_reduce(sq1(kmax[:, ds(i * 2 + j, 1), 2 * c:2 * c + 2]),
                                            psum[KD_BANKS[n % 4]][0:P, :].rearrange("p (s m) -> p s m", s=2), AX, ALU.max).then_inc(m["kmx"], 1)

            norm1(0)
            with dve.Fori(0, PAIRS - 1) as i:
                pair(i, False)
            pair(PAIRS - 1, True)
            dve.wait_ge(m["kmx"], l * ADDS["kmx"] + 4 * TILES)
            nc.vector.tensor_reduce(kmax_all, kmax.rearrange("p t h -> p h t"), AX, ALU.max).then_inc(m["gmx"], 1)
            dve.wait_ge(m["gmx_pe"], l * ADDS["gmx_pe"] + 1)
            nc.vector.tensor_reduce(kmax_t, psum[0][0:HEADS, 0:P], AX, ALU.max).then_inc(m["gmx"], 1)
            dve.wait_ge(m["gmx"], l * ADDS["gmx"] + 2)
            nc.vector.tensor_scalar(kmax_d, ident[0:HEADS, 0:HEADS], kmax_t, None, ALU.mult).then_inc(m["gmx"], 1)
            dve.wait_ge(m["gmx_pe"], l * ADDS["gmx_pe"] + 2)
            nc.vector.tensor_copy(kmax_all, psum[1][0:P, 0:HEADS]).then_inc(m["gmx"], 1)
            dve.wait_ge(m["gmx"], l * ADDS["gmx"] + 4)
            dve.wait_ge(m["dg"], l * ADDS["dg"] + PAIRS)
            nc.vector.tensor_tensor(kneg, diag[:, :, 1, :], kmax_all.unsqueeze(1).to_broadcast([P, TILES, HEADS]), ALU.add).then_inc(m["gmx"], 1)
            dve.wait_ge(m["gmx"], l * ADDS["gmx"] + 5)
            nc.vector.tensor_scalar(kneg, kneg, -1.0, None, ALU.mult).then_inc(m["kneg"], 1)
            if l == 0:
                edge_index_dve(dve)

        def attn1_pe(pe, l):
            pe.wait_ge(m["pj"], l * ADDS["pj"] + 32)
            if l == 0:
                pe.wait_ge(s_const, CONSTS)
            else:
                pe.wait_ge(g_sem[1]["out"], OUT_DONE)
            for k in range(2):
                mm = nc.tensor.transpose(psum[7][:, 128 * k:128 * k + 128], proj_st[:, k, :], ident[:, :])
            mm.then_inc(m["pjT"], 1)
            pe.wait_ge(m["w"], l * ADDS["w"] + W_LOADS)
            pe.wait_ge(m["pjS"], l * ADDS["pjS"] + 4)
            if l == 0:
                pe.sem_inc(m["dg"], 1)
            if l == 0:
                pe.sem_inc(m["sq"], 4)
            if l == 0:
                pe.sem_inc(m["k"], 2)
            if l == 0:
                pe.sem_inc(m["kd"], 4)

            def turn(i):
                pe.wait_ge(m["z"], l * ADDS["z"] + i * 2 + 2)
                pe.wait_ge(m["dg"], l * ADDS["dg"] + i + 1)
                for c in range(KC):
                    for j in range(2):
                        mm = nc.tensor.transpose(psum[c // 2][:, 256 * (c % 2) + P * j:256 * (c % 2) + P * j + P],
                                                 zst[:, j, 128 * c:128 * c + 128], ident[0:P, 0:P])
                    mm.then_inc(m["yT_pe"], 1)

            def pair(i, last):
                pe.wait_ge(m["yT"], l * ADDS["yT"] + i * KC + KC)
                for c in range(KC):
                    pe.wait_ge(m["sq"], l * ADDS["sq"] + i * KC * 2 + 2 * c + 1)
                    for k in range(KC):
                        mm = nc.tensor.matmul(psum[2 + c % 2][:, 0:PT], wreg[:, 0, 512 * k + 128 * c:512 * k + 128 * c + 128],
                                              y_t[:, k, :], start=(k == 0), stop=(k == KC - 1))
                    mm.then_inc(m["q_pe"], 1)
                    pe.wait_ge(m["k"], l * ADDS["k"] + i * KC + c + 1)
                    if c == 0:
                        pe.wait_ge(m["kd"], l * ADDS["kd"] + i * 8 + 4)
                    for k in range(KC):
                        mm = nc.tensor.matmul(psum[4 + c % 2][:, 0:PT], wreg[:, 1, 512 * k + 128 * c:512 * k + 128 * c + 128],
                                              y_t[:, k, :], start=(k == 0), stop=(k == KC - 1))
                    mm.then_inc(m["k_pe"], 1)
                for j in range(2):
                    for k in range(KC):
                        mm = nc.tensor.matmul(psum[6 + j][0:P, :], y_t[:, k, P * j:P * j + P], wreg[:, 2, 512 * k:512 * k + 512],
                                              start=(k == 0), stop=(k == KC - 1))
                    mm.then_inc(m["v_pe"], 1)
                pe.wait_ge(m["sq"], l * ADDS["sq"] + i * KC * 2 + 2 * KC + 4)
                for j in range(2):
                    for s in range(2):
                        for c in range(KC):
                            mm = nc.tensor.matmul(psum[0][0:P, 16 * j + 8 * s:16 * j + 8 * s + 8], sq[:, s, c, P * j:P * j + P],
                                                  headsel[:, c, :], start=(c == 0), stop=(c == KC - 1), skip_group_check=True)
                mm.then_inc(m["dg_pe"], 1)
                pe.wait_ge(m["v"], l * ADDS["v"] + i * 2 + 2)
                for n in range(8):
                    j, c = n // 4, n % 4
                    if n == 2:
                        pe.wait_ge(m["k"], l * ADDS["k"] + i * KC + KC + 2)
                    if n == 4 and not last:
                        turn(i + 1)
                    if n >= 4:
                        pe.wait_ge(m["kd"], l * ADDS["kd"] + i * 8 + n + 1)
                    nc.tensor.matmul(psum[KD_BANKS[n % 4]][0:P, :], k_t[:, c, P * j:P * j + P], projbd[:, :], start=True, stop=True).then_inc(m["kd_pe"], 1)

            turn(0)
            with pe.Fori(0, PAIRS - 1) as i:
                pair(i, False)
            pair(PAIRS - 1, True)
            pe.wait_ge(m["gmx"], l * ADDS["gmx"] + 1)
            pe.wait_ge(m["dg"], l * ADDS["dg"] + 1 + PAIRS)
            nc.tensor.transpose(psum[0][0:HEADS, 0:P], kmax_all, ident[0:P, 0:P]).then_inc(m["gmx_pe"], 1)
            pe.wait_ge(m["gmx"], l * ADDS["gmx"] + 3)
            nc.tensor.matmul(psum[1][0:P, 0:HEADS], ones[:, :], kmax_d, start=True, stop=True).then_inc(m["gmx_pe"], 1)

        def attn1_act(act, l):
            act.wait_ge(m["w"], l * ADDS["w"] + W_LOADS)

            def scale(i):
                for c in range(KC):
                    act.wait_ge(m["yT_pe"], l * ADDS["yT_pe"] + i * KC + 2 * (c // 2) + 2 + KC)
                    nc.scalar.activation(y_t[:, c, :], psum[c // 2][:, 256 * (c % 2):256 * (c % 2) + PT], ACT.Identity,
                                         bias=c_b1[:, c:c + 1], scale=c_g1[:, c:c + 1]).then_inc(m["yT"], 1)

            def pair(i, last):
                for c in range(KC):
                    act.wait_ge(m["q_pe"], l * ADDS["q_pe"] + i * KC + c + 1)
                    nc.scalar.activation(q_t[:, c, ds(i * PT, PT)], psum[2 + c % 2][:, 0:PT], ACT.Identity,
                                         bias=c_bq[:, c:c + 1])
                    nc.scalar.activation(sq[:, 0, c, :], psum[2 + c % 2][:, 0:PT], ACT.Square, bias=c_bq[:, c:c + 1]).then_inc(m["sq"], 1)
                    act.wait_ge(m["k"], l * ADDS["k"] + i * KC + c + 3)
                    nc.scalar.activation(sq[:, 1, c, :], k_t[:, c, :], ACT.Square).then_inc(m["sq"], 1)
                for n in range(8):
                    j, c = n // 4, n % 4
                    act.wait_ge(m["kmx"], l * ADDS["kmx"] + i * 8 + n + 1)
                    nc.scalar.activation(sq1(kdash[:, ds(i * 2 + j, 1), 512 * c:512 * c + 512]), psum[KD_BANKS[n % 4]][0:P, :],
                                         ACT.Copy).then_inc(m["kd"], 1)
                    if n == 5 and not last:
                        scale(i + 1)

            scale(0)
            with act.Fori(0, PAIRS - 1) as i:
                pair(i, False)
            pair(PAIRS - 1, True)

        def attn2_act(act, l):
            act.wait_ge(m["kneg"], l * ADDS["kneg"] + 1)
            act.wait_ge(m["kd"], l * ADDS["kd"] + 4 + 4 * TILES)
            if l == 0:
                act.sem_inc(m["ctx_pe"], 2)
            with act.Fori(0, PAIRS) as i:
                for j in range(2):
                    act.wait_ge(m["ctx_pe"], l * ADDS["ctx_pe"] + i * 2 + j + 1)
                    for hh in range(HEADS):
                        op = nc.scalar.activation(kfeat[:, j, FEATS * hh:FEATS * hh + FEATS],
                                                  sq1(kdash[:, ds(i * 2 + j, 1), FEATS * hh:FEATS * hh + FEATS]), ACT.Exp,
                                                  bias=sq1(kneg[:, ds(i * 2 + j, 1), hh:hh + 1]))
                    op.then_inc(m["kx"], 1)

        def attn2_dve(dve, l):
            with dve.Fori(0, PAIRS) as i:
                for j in range(2):
                    dve.wait_ge(m["kx"], l * ADDS["kx"] + i * 2 + j + 1)
                    nc.vector.tensor_scalar(kfeat[:, j, :], kfeat[:, j, :], EPS_K, None, ALU.add).then_inc(m["kf"], 1)
            dve.wait_ge(m["ctx_pe"], l * ADDS["ctx_pe"] + 2 + TILES)
            for b in range(4):
                nc.vector.tensor_copy(ctx_sb[:, 4 * b:4 * b + 4, :].rearrange("p u d -> p (u d)"), psum[b][:, 0:4 * (HD + 1)]).then_inc(m["ctx"], 1)

        def attn2_pe(pe, l):
            pe.wait_ge(m["gmx"], l * ADDS["gmx"] + 4)
            pe.wait_ge(m["sq"], l * ADDS["sq"] + 4 + 2 * KC * PAIRS)
            for b in range(4):
                nc.tensor.matmul(psum[b][:, 0:4 * (HD + 1)], zeros[:, :], wreg[:, 0, 0:4 * (HD + 1)], start=True, stop=False, skip_group_check=True)
            with pe.Fori(0, PAIRS) as i:
                for j in range(2):
                    pe.wait_ge(m["kf"], l * ADDS["kf"] + i * 2 + j + 1)
                    for u in range(2 * HEADS):
                        mm = nc.tensor.matmul(psum[u // 4][:, (HD + 1) * (u % 4):(HD + 1) * (u % 4 + 1)], kfeat[:, j, 128 * u:128 * u + 128],
                                              v_aug[:, ds(i * 2 + j, 1), u // 2, :].rearrange("p o d -> p (o d)"),
                                              start=False, stop=True, skip_group_check=True)
                    mm.then_inc(m["ctx_pe"], 1)

        STEPS = 2 * KC

        QD_BANKS = (0, 1, 6, 7)

        def attn3_dve(dve, l):
            dve.wait_ge(m["ctx_pe"], l * ADDS["ctx_pe"] + 2 + TILES)
            nc.vector.tensor_copy(q_st, q_t[:, :, 0:PT]).then_inc(m["qs"], 1)

            def pair(i, last):
                def normalize(j):
                    dve.wait_ge(m["o_pe"], l * ADDS["o_pe"] + i * 2 + j + 1)
                    for b in range(2):
                        nc.vector.reciprocal(rden[:, j, 4 * b:4 * b + 4].unsqueeze(2),
                                             psum[4 + b][0:P, 0:4 * (HD + 1)].rearrange("p (h d) -> p h d", h=4)[:, :, HD:HD + 1]).then_inc(m["rd"], 1)
                    dve.wait_ge(m["rd"], l * ADDS["rd"] + i * 4 + 2 * j + 2)
                    for b in range(2):
                        nc.vector.tensor_tensor(o_sb[:, j, 256 * b:256 * b + 256].rearrange("p (h d) -> p h d", h=4),
                                                psum[4 + b][0:P, 0:4 * (HD + 1)].rearrange("p (h d) -> p h d", h=4)[:, :, 0:HD],
                                                rden[:, j, 4 * b:4 * b + 4].unsqueeze(2).to_broadcast([P, 4, HD]), ALU.mult).then_inc(m["o"], 1)

                def residual(j):
                    ht = sq1(h[:, ds(i * 2 + j, 1), :])
                    dve.wait_ge(m["at_pe"], l * ADDS["at_pe"] + i * 2 + j + 1)
                    nc.vector.tensor_tensor(ht, psum[3][0:P, :], ht, ALU.add).then_inc(m["hat"], 1)
                    dve.wait_ge(m["hat"], l * ADDS["hat"] + i * 4 + 2 * j + 3)
                    nc.vector.tensor_tensor(ht, ht, b_o, ALU.add).then_inc(m["hat"], 1)

                for n in range(STEPS + 2):
                    if n == 7:
                        normalize(0)
                    if n < STEPS:
                        j, c = n // KC, n % KC
                        dve.wait_ge(m["qd_pe"], l * ADDS["qd_pe"] + i * STEPS + n + 1)
                        nc.vector.tensor_reduce(qmax[:, n % 4, :], psum[QD_BANKS[n % 4]][0:P, :].rearrange("p (s m) -> p s m", s=2), AX, ALU.max).then_inc(m["qm"], 1)
                        dve.wait_ge(m["qm"], l * ADDS["qm"] + i * STEPS + n + 1)
                        nc.vector.scalar_tensor_tensor(qneg[:, n % 4, :], qmax[:, n % 4, :], -1.0,
                                                       diag[:, ds(i * 2 + j, 1), 0, 2 * c:2 * c + 2].rearrange("p o s -> p (o s)"),
                                                       ALU.mult, ALU.subtract).then_inc(m["qn"], 1)
                    if n == STEPS - 1 and not last:
                        nc.vector.tensor_copy(q_st, q_t[:, :, ds(i * PT + PT, PT)]).then_inc(m["qs"], 1)
                    if n >= 2:
                        dve.wait_ge(m["qT_pe"], l * ADDS["qT_pe"] + i * STEPS + (n - 2) + 5)
                        nc.vector.tensor_scalar(qfeat_t[:, n % 2, :], psum[2 + n % 2][:, 0:4 * P], EPS_K, None, ALU.add).then_inc(m["qT"], 1)
                residual(0)
                normalize(1)
                residual(1)

            with dve.Fori(0, PAIRS - 1) as i:
                pair(i, False)
            pair(PAIRS - 1, True)

        def attn3_act(act, l):
            if l == 0:
                act.sem_inc(m["qT_pe"], 4)
            with act.Fori(0, PAIRS) as i:
                def turn(j):
                    act.wait_ge(m["oT_pe"], l * ADDS["oT_pe"] + i * 2 + j + 1)
                    nc.scalar.activation(o_t[:, j, :], psum[2][:, 0:4 * P], ACT.Copy).then_inc(m["oT"], 1)
                for n in range(STEPS):
                    act.wait_ge(m["qn"], l * ADDS["qn"] + i * STEPS + n + 1)
                    act.wait_ge(m["qT_pe"], l * ADDS["qT_pe"] + i * STEPS + n + 1)
                    for s in range(2):
                        op = nc.scalar.activation(qfeat[:, n % 4, FEATS * s:FEATS * s + FEATS], psum[QD_BANKS[n % 4]][0:P, FEATS * s:FEATS * s + FEATS],
                                                  ACT.Exp, bias=qneg[:, n % 4, s:s + 1])
                    op.then_inc(m["qx"], 1)
                turn(0)
                turn(1)
            if l == 0:
                act.wait_ge(m["qs"], PAIRS)
                nc.scalar.activation(qv[:, 0:8192].rearrange("p (a b) -> p a b", b=128), zeros[:, :].unsqueeze(1).to_broadcast([128, 64, 128]),
                                     ACT.Copy).then_inc(s_comb0, 1)

        def attn3_pe(pe, l):
            pe.wait_ge(m["ctx"], l * ADDS["ctx"] + 4)
            pe.wait_ge(m["w"], l * ADDS["w"] + W_LOADS + 16)
            if l == 0:
                pe.sem_inc(m["qx"], 4)
            if l == 0:
                pe.sem_inc(m["qT"], 2)
            if l == 0:
                pe.sem_inc(m["o"], 2)
            if l == 0:
                pe.sem_inc(m["oT"], 1)
            if l == 0:
                pe.sem_inc(m["hat"], 2)
            with pe.Fori(0, PAIRS) as i:
                pe.wait_ge(m["qs"], l * ADDS["qs"] + i + 1)

                def out_proj(j):
                    pe.wait_ge(m["o"], l * ADDS["o"] + i * 4 + 2 * j + 4)
                    pe.wait_ge(m["oT"], l * ADDS["oT"] + i * 2 + j + 1)
                    for k in range(KC):
                        mm = nc.tensor.transpose(psum[2][:, P * k:P * k + P], o_sb[:, j, 128 * k:128 * k + 128], ident[0:P, 0:P])
                    mm.then_inc(m["oT_pe"], 1)

                def out_mm(j):
                    pe.wait_ge(m["oT"], l * ADDS["oT"] + i * 2 + j + 2)
                    pe.wait_ge(m["hat"], l * ADDS["hat"] + i * 4 + 2 * j + 1)
                    for k in range(KC):
                        mm = nc.tensor.matmul(psum[3][0:P, :], o_t[:, j, P * k:P * k + P], wreg[:, 3, 512 * k:512 * k + 512],
                                              start=(k == 0), stop=(k == KC - 1))
                    mm.then_inc(m["at_pe"], 1)

                for n in range(STEPS + 3):
                    if n < STEPS:
                        j, c = n // KC, n % KC
                        pe.wait_ge(m["qx"], l * ADDS["qx"] + i * STEPS + n + 1)
                        nc.tensor.matmul(psum[QD_BANKS[n % 4]][0:P, :], q_st[:, c, P * j:P * j + P], projbd[:, :], start=True, stop=True).then_inc(m["qd_pe"], 1)
                    if 2 <= n < STEPS + 2:
                        u = n - 2
                        if u == 0:
                            pe.wait_ge(m["oT"], l * ADDS["oT"] + i * 2 + 1)
                            pe.wait_ge(m["hat"], l * ADDS["hat"] + i * 4 + 1)
                        pe.wait_ge(m["qx"], l * ADDS["qx"] + i * STEPS + u + 5)
                        pe.wait_ge(m["qT"], l * ADDS["qT"] + i * STEPS + u + 1)
                        for q in range(4):
                            mm = nc.tensor.transpose(psum[2 + u % 2][:, P * q:P * q + P], qfeat[:, u % 4, 128 * q:128 * q + 128], ident[0:P, 0:P])
                        mm.then_inc(m["qT_pe"], 1)
                    if n >= 3:
                        j, c = (n - 3) // KC, (n - 3) % KC
                        pe.wait_ge(m["qT"], l * ADDS["qT"] + i * STEPS + (n - 3) + 3)
                        if c == 0:
                            pe.wait_ge(m["o"], l * ADDS["o"] + i * 4 + 2 * j + 2)
                        for s in range(2):
                            hh = 2 * c + s
                            for q in range(2):
                                mm = nc.tensor.matmul(psum[4 + hh // 4][0:P, (HD + 1) * (hh % 4):(HD + 1) * (hh % 4 + 1)],
                                                      qfeat_t[:, (n - 3) % 2, P * (2 * s + q):P * (2 * s + q) + P], ctx_sb[:, 2 * hh + q, :],
                                                      start=(q == 0), stop=(q == 1), skip_group_check=True)
                        if c == KC - 1:
                            mm.then_inc(m["o_pe"], 1)
                out_proj(0)
                out_mm(0)
                out_proj(1)
                out_mm(1)

        LN2 = 2 * TILES + RSQ
        F1_BANKS = (2, 3, 4, 7)

        def ln2_dve(dve, l):
            n = l * ADDS["ln2"]
            for t in range(TILES):
                nc.vector.bn_stats(st6[:, t, :], h[:, t, :]).then_inc(m["ln2"], 1)
            dve.wait_ge(m["ln2"], n + TILES)
            for t in range(TILES):
                nc.vector.bn_aggr(mv[:, t, :], st6[:, t, :]).then_inc(m["ln2"], 1)
            dve.wait_ge(m["ln2"], n + 2 * TILES)
            rsqrt(dve, m["ln2"], n + 2 * TILES, mv[:, :, 1], 0, TILES, row=3)
            dve.wait_ge(m["ln2"], n + LN2)

        def norm2(dve, l, i):
            dve.wait_ge(m["y2_pe"], l * ADDS["y2_pe"] + i * KC + KC)
            for j in range(2):
                nc.vector.tensor_scalar(zst[:, j, :], sq1(h[:, ds(i * 2 + j, 1), :]), sq1(mv[:, ds(i * 2 + j, 1), 0:1]), rs[:, 3, ds(i * 2 + j, 1)],
                                        ALU.subtract, ALU.mult).then_inc(m["z2"], 1)

        def ffn_take(dve, l, i):
            for j in range(2):
                ht = sq1(h[:, ds(i * 2 + j, 1), :])
                dve.wait_ge(m["f2_pe"], l * ADDS["f2_pe"] + i * 2 + j + 1)
                nc.vector.tensor_tensor(ht, psum[5 + j][0:P, :], ht, ALU.add).then_inc(m["hf"], 1)
                dve.wait_ge(m["hf"], l * ADDS["hf"] + i * 4 + 2 * j + 3)
                nc.vector.tensor_tensor(ht, ht, b_2, ALU.add).then_inc(m["hf"], 1)

        def mlp_dve(dve):
            dve.wait_ge(s_att, 32)
            dve.wait_ge(m["hat"], 2 + 2 * TILES)
            dve.wait_ge(m["mw"], 48)
            dve.sem_inc(m["y2_pe"], KC)
            ln2_dve(dve, 0)
            norm2(dve, 0, 0)
            dve.wait_ge(s_comb0, 1)

            def combine(i, blocks):
                for n in blocks:
                    gl, b = n // (BLOCKS // 2), n % (BLOCKS // 2)
                    dve.wait_ge(s_basis[n % BRING], i * (16 * BLOCKS // BRING) + 16 * (n // BRING) + 16)
                    dve.wait_ge(s_comb, i * (2 * BLOCKS) + 2 * n + 2 * BRING)
                    for r in range(RELS):
                        nc.vector.scalar_tensor_tensor(wrel[:, gl, r, :], wreg[:, n % BRING, :], att_b[:, gl, ds(i * (BLOCKS // 2) + (r * BASES + b), 1)],
                                                       wrel[:, gl, r, :], ALU.mult, ALU.add).then_inc(s_comb, 1)

            with dve.Fori(0, PAIRS - 1) as i:
                combine(i, range(BLOCKS // 2))
                norm2(dve, 0, i + 1)
                combine(i, range(BLOCKS // 2, BLOCKS))
                ffn_take(dve, 0, i)
            combine(PAIRS - 1, range(BLOCKS))
            ffn_take(dve, 0, PAIRS - 1)
            dve.wait_ge(m["hf"], 2 + 2 * TILES)

        def ffn_turn_pe(pe, l, i):
            pe.wait_ge(m["z2"], l * ADDS["z2"] + i * 2 + 2)
            for c in range(KC):
                for j in range(2):
                    mm = nc.tensor.transpose(psum[c // 2][:, 256 * (c % 2) + P * j:256 * (c % 2) + P * j + P],
                                             zst[:, j, 128 * c:128 * c + 128], ident[0:P, 0:P])
                mm.then_inc(m["y2_pe"], 1)

        def ffn_body_pe(pe, l, i, between=None):
            pe.wait_ge(m["y2"], l * ADDS["y2"] + i * KC + KC)
            for half in range(2):
                for n in range(HH * half, HH * half + HH):
                    pe.wait_ge(m["f1"], l * ADDS["f1"] + i * HC + n + 1)
                    for k in range(KC):
                        mm = nc.tensor.matmul(psum[F1_BANKS[n % 4]][:, 0:PT], w1_sb[:, k, 128 * n:128 * n + 128], y_t[:, k, :],
                                              start=(k == 0), stop=(k == KC - 1))
                    mm.then_inc(m["f1_pe"], 1)
                if half == 1 and between:
                    between()
                if half == 0:
                    pe.wait_ge(m["hf"], l * ADDS["hf"] + i * 4 + 2)
                for j in range(2):
                    for k in range(HH * half, HH * half + HH):
                        if j == 0:
                            pe.wait_ge(m["f1"], l * ADDS["f1"] + i * HC + k + 5)
                        mm = nc.tensor.matmul(psum[5 + j][0:P, :], act_t[:, k % HH, P * j:P * j + P], w2_sb[:, k, :],
                                              start=(k == 0), stop=(k == HC - 1))
                    if half == 1:
                        mm.then_inc(m["f2_pe"], 1)

        def mlp_start_pe(pe, l):
            pe.wait_ge(m["mw"], l * ADDS["mw"] + 48)
            pe.wait_ge(m["hat"], l * ADDS["hat"] + 2 + 2 * TILES)

        def mlp_pe(pe):
            mlp_start_pe(pe, 0)
            pe.sem_inc(m["f1"], 4)
            pe.sem_inc(m["hf"], 2)
            ffn_turn_pe(pe, 0, 0)
            with pe.Fori(0, PAIRS - 1) as i:
                ffn_body_pe(pe, 0, i, between=lambda: ffn_turn_pe(pe, 0, i + 1))
            ffn_body_pe(pe, 0, PAIRS - 1)

        def ffn_scale_act(act, l, i):
            for c in range(KC):
                act.wait_ge(m["y2_pe"], l * ADDS["y2_pe"] + i * KC + 2 * (c // 2) + 2 + KC)
                nc.scalar.activation(y_t[:, c, :], psum[c // 2][:, 256 * (c % 2):256 * (c % 2) + PT], ACT.Identity,
                                     bias=c_b2[:, c:c + 1], scale=c_g2[:, c:c + 1]).then_inc(m["y2"], 1)

        def ffn_gelu_act(act, l, i):
            for n in range(HC):
                act.wait_ge(m["f1_pe"], l * ADDS["f1_pe"] + i * HC + n + 1)
                nc.scalar.activation(act_t[:, n % HH, :], psum[F1_BANKS[n % 4]][:, 0:PT], ACT.Gelu, bias=c_h1[:, n:n + 1]).then_inc(m["f1"], 1)

        def mlp_act(act):
            ffn_scale_act(act, 0, 0)
            with act.Fori(0, PAIRS - 1) as i:
                ffn_gelu_act(act, 0, i)
                ffn_scale_act(act, 0, i + 1)
            ffn_gelu_act(act, 0, PAIRS - 1)

        g_names = "w x xT_pe xT gt_pe gt z_pe z r agg out xin st".split()
        g_sem = [{n: sem(f"gcn{gl}_{n}") for n in g_names} for gl in range(2)]
        s_slab = [[sem(f"gcn{gl}_slab_{j}") for j in range(2)] for gl in range(2)]
        OUT_DONE = 4 + 2 * TILES
        COMB_DONE = 2 * BRING + 2 * 2 * BASES
        b_g = b_v
        xin = view(stage, 2024, [2, DIM], P)

        def gcn_sp(sp, gl):
            g = g_sem[gl]
            if gl == 0:
                sp.wait_ge(s_comb, COMB_DONE)
                sp.wait_ge(m["hf"], 2 + 2 * TILES)
                sp.wait_ge(s_xnw, 16)
            else:
                sp.wait_ge(g_sem[0]["r"], 2 + TILES)
            sp.dma_start(root_sb, a[f"L0_gnn_root{gl + 1}"].rearrange("(k p) n -> p k n", p=128)).then_inc(g["w"], 16)
            for r in range(RELS):
                sp.dma_start(c_gate[:, :, r], a[f"L0_gnn_gate_w{gl + 1}"][r].rearrange("(k p) o -> p (k o)", p=128), allow_slow_non_contiguous=True).then_inc(g["w"], 16)
            sp.dma_start(b_g, a[f"L0_gnn_bias{gl + 1}"].partition_broadcast(P)).then_inc(g["w"], 16)
            if gl == 0:
                with sp.Fori(0, PAIRS) as i:
                    sp.wait_ge(g["xT_pe"], i * 2 + 2)
                    sp.dma_start(gx, tok(xn_d)[:, ds(i * 2, 2), :]).then_inc(g["x"], 16)
            if gl == 0:
                sp.wait_ge(s_adj, 16 * GROUPS)
            else:
                sp.wait_ge(g_sem[0]["agg"], 2 + TILES)
            sp.sem_inc(g["agg"], 2)
            with sp.Fori(0, PAIRS) as i:
                for j in range(2):
                    sp.wait_ge(g["agg"], i * 2 + j + 1)
                    sp.dma_start(slab[:, j, :, :], adj_2d[:, ds(i * PT + j * P, P)].rearrange("(c p) r -> p c r", p=P)).then_inc(s_slab[gl][j], 16)

        def gcn_x_act(act, gl):
            g = g_sem[gl]
            with act.Fori(0, PAIRS) as i:
                act.wait_ge(g["out"], i * 4 + 4)
                act.dma_start(xin, tok(a["x"])[:, ds(i * 2, 2), :]).then_inc(g["xin"], 16)
                act.wait_ge(g["out"], i * 4 + 8)
                act.dma_start(tok(res_d)[:, ds(i * 2, 2), :], gx).then_inc(g["st"], 16)

        def gcn_pe(pe, gl):
            g = g_sem[gl]
            pe.wait_ge(g["w"], 64)
            pe.wait_ge(m["hf"], 2 + 2 * TILES)
            pe.sem_inc(g["z"], 4)
            pe.sem_inc(g["r"], 2)
            with pe.Fori(0, PAIRS) as i:
                pe.wait_ge(g["x"], (i + 1) * (16 if gl == 0 else 1))
                for j in range(2):
                    pe.wait_ge(g["gt"], i * 2 + j + 1)
                    for k in range(KC):
                        mm = nc.tensor.transpose(psum[j][:, P * k:P * k + P], gx[:, j, 128 * k:128 * k + 128], ident[0:P, 0:P])
                    mm.then_inc(g["xT_pe"], 1)
                for j in range(2):
                    pe.wait_ge(g["xT"], i * 2 + j + 1)
                    for k in range(KC):
                        mm = nc.tensor.matmul(psum[j][0:P, 500:502], gx_t[:, j, P * k:P * k + P], c_gate[:, k, :], start=(k == 0), stop=(k == KC - 1))
                    mm.then_inc(g["gt_pe"], 1)
                    for r in range(RELS):
                        pe.wait_ge(g["z"], i * 4 + 2 * j + r + 1)
                        for k in range(KC):
                            mm = nc.tensor.matmul(psum[2 + 3 * j + r][0:P, :], gx_t[:, j, P * k:P * k + P], wrel[:, gl, r, 512 * k:512 * k + 512],
                                                  start=(k == 0), stop=(k == KC - 1))
                        mm.then_inc(g["z_pe"], 1)
                    pe.wait_ge(g["r"], i * 2 + j + 1)
                    for k in range(KC):
                        mm = nc.tensor.matmul(psum[4 + 3 * j][0:P, :], gx_t[:, j, P * k:P * k + P], root_sb[:, k, :], start=(k == 0), stop=(k == KC - 1))
                    mm.then_inc(g["z_pe"], 1)
            pe.wait_ge(g["z"], 4 + 2 * TILES)
            pe.wait_ge(g["gt"], 2 + TILES)
            pe.sem_inc(g["out"], 4)
            with pe.Fori(0, PAIRS) as i:
                for j in range(2):
                    pe.wait_ge(s_slab[gl][j], i * 16 + 16)
                    pe.wait_ge(g["out"], i * 4 + 2 * j + 1)
                    for c in range(COLT):
                        mm = nc.tensor.matmul(psum[j][0:P, :], slab[:, j, c, :], zrel[:, c, :], start=(c == 0), stop=(c == COLT - 1))
                    mm.then_inc(g["agg"], 1)

        def gcn_act(act, gl):
            g = g_sem[gl]
            act.sem_inc(g["gt"], 2)
            act.sem_inc(g["xT_pe"], 2)
            with act.Fori(0, PAIRS) as i:
                for j in range(2):
                    act.wait_ge(g["xT_pe"], i * 2 + j + 3)
                    nc.scalar.activation(gx_t[:, j, :], psum[j][:, 0:4 * P], ACT.Copy).then_inc(g["xT"], 1)
                for j in range(2):
                    act.wait_ge(g["gt_pe"], i * 2 + j + 1)
                    nc.scalar.activation(gate[:, j, :], psum[j][0:P, 500:502], ACT.Sigmoid).then_inc(g["gt"], 1)
                    act.wait_ge(g["gt"], i * 2 + j + 3)
                    for r in range(RELS):
                        act.wait_ge(g["z_pe"], i * 6 + 3 * j + r + 1)
                        nc.scalar.activation(sq1(zrel[:, ds(i * 2 + (j + r * TILES), 1), :]), psum[2 + 3 * j + r][0:P, :], ACT.Identity,
                                             scale=gate[:, j, r:r + 1]).then_inc(g["z"], 1)

        def gcn_dve(dve, gl):
            g = g_sem[gl]
            dve.wait_ge(g["w"], 64)
            dve.sem_inc(g["st"], 16)
            if gl == 1:
                dve.wait_ge(g_sem[0]["out"], OUT_DONE)
            with dve.Fori(0, PAIRS) as i:
                if gl == 1:
                    dve.wait_ge(g["xT_pe"], i * 2 + 2)
                    nc.vector.tensor_copy(gx, x1[:, ds(i * 2, 2), :]).then_inc(g["x"], 1)
                for j in range(2):
                    dve.wait_ge(g["z_pe"], i * 6 + 3 * j + 3)
                    nc.vector.tensor_tensor(sq1(xroot[:, ds(i * 2 + j, 1), :]), psum[4 + 3 * j][0:P, :], b_g, ALU.add).then_inc(g["r"], 1)
            with dve.Fori(0, PAIRS) as i:
                if gl == 1:
                    dve.wait_ge(g["st"], i * 16 + 16)
                for j in range(2):
                    dve.wait_ge(g["agg"], i * 2 + j + 3)
                    t = i * 2 + j
                    dst = sq1(x1[:, ds(t, 1), :]) if gl == 0 else gx[:, j, :]
                    nc.vector.tensor_tensor(dst, psum[j][0:P, :], sq1(xroot[:, ds(t, 1), :]), ALU.add).then_inc(g["out"], 1)
                    dve.wait_ge(g["out"], i * 4 + 2 * j + 5)
                    if gl == 0:
                        nc.vector.tensor_scalar(dst, dst, 0.0, None, ALU.max).then_inc(g["out"], 1)
                    else:
                        dve.wait_ge(g["xin"], i * 16 + 16)
                        nc.vector.tensor_tensor(dst, dst, xin[:, j, :], ALU.add).then_inc(g["out"], 1)

        p_w, p_keys, p_keysT, p_keysS, p_res, p_h, p_ln, p_x, p_xT_pe, p_xT, p_q_pe, p_q, p_s_pe, p_top, p_exp, p_slots, p_vals, p_dn, p_up, p_diag, p_out = (
            sem("mem_" + n) for n in ("weights keys keysT_pe keys_placed residual_in h ln x xT_pe xT q_pe q s_pe top exp slots vals dots_done "
                                      "rows_added weights_placed taken").split())
        s_row = [sem(f"mem_row_{n}") for n in range(RING)]
        s_hold = sem("mem_holds")
        s_out = [sem(f"out_{j}") for j in range(2)]
        keys_st = view(qv, 5592, [2 * PKH, 128])
        slots_of = [slots, biasb[:, 1, 0:SLOTS].bitcast(I32)]
        acc_of = [acc, projbd[0:P, :]]
        QB = 4
        EXP_AT = 48
        TAKE_AT = 40
        LN3 = 4 + RSQ

        def landed(t, j, n):
            return t * (16 * 2 * ROUNDS) + 16 * (j * 2 * ROUNDS + n // RING + 1)

        def mem_sp(sp):
            sp.wait_ge(m["gmx"], ADDS["gmx"] + 5)
            for half in range(2):
                for hh in range(PKH):
                    sp.dma_start(keys_st[:, 2 * hh:2 * hh + 2, HALF * half:HALF * half + HALF],
                                 a["L0_ffn_keys"][hh, half].rearrange("(n p) d -> p n d", p=128)).then_inc(p_keys, 16)
            sp.dma_start(wqf, a["L0_ffn_Wq"].rearrange("(k p) n -> p k n", p=128)).then_inc(p_w, 16)
            sp.dma_start(c_bqf, a["L0_ffn_bq"].rearrange("(h p) -> p h", p=128), allow_slow_non_contiguous=True).then_inc(p_w, 16)
            sp.wait_ge(m["hat"], ADDS["hat"] + 2 + 2 * TILES)
            sp.wait_ge(g_sem[1]["st"], 16 + 16 * PAIRS)
            sp.dma_start(res_p, tok(res_d)[:, 0:2, :]).then_inc(p_res, 16)

            def store(i, j):
                sp.wait_ge(p_out, i * 2 + (j + 2))
                sp.dma_start(tok(out)[:, ds(i * 2 + j, 1), :], acc_of[j].unsqueeze(1)).then_inc(s_out[j], 16)

            with sp.Fori(0, PAIRS - 1) as i:
                sp.wait_ge(p_h, i * 2 + 2)
                sp.dma_start(res_p, tok(res_d)[:, ds(i * 2 + 2, 2), :]).then_inc(p_res, 16)
                store(i, 0)
                store(i, 1)
            store(PAIRS - 1, 0)
            store(PAIRS - 1, 1)
            for j in range(2):
                sp.wait_ge(s_out[j], 16 + 16 * PAIRS)

        def mem_pool(pool):
            pool.wait_ge(m["hat"], ADDS["hat"] + 2 + 2 * TILES)
            for s in range(2):
                nc.gpsimd.memset(keybd[64 * s:64 * s + 64, :, NKEYS * (1 - s):NKEYS * (2 - s)], 0.0).then_inc(p_keysS, 1)
            pool.sem_inc(p_up, RING)
            pool.sem_inc(s_hold, 1)
            pool.sem_inc(p_diag, 1)

            def tile(i, j):
                if j == 0:
                    pool.wait_ge(s_hold, i * (4 * SLOTS // HOLD) + 1)
                pool.wait_ge(p_slots, i * 2 + (j + 1))
                for n in range(2 * SLOTS):
                    s = n % SLOTS
                    if s % HOLD == 0:
                        if (s < RING) == (n < SLOTS):
                            pool.wait_ge(p_up, i * (2 * SLOTS) + (j * SLOTS + s + HOLD))
                        elif n < SLOTS:
                            pool.wait_ge(p_dn, i * (2 * SLOTS) + (j * SLOTS + s - RING + HOLD))
                        else:
                            pool.wait_ge(p_dn, i * (2 * SLOTS) + (j * SLOTS + SLOTS - RING + s + HOLD))
                        hold_pool().then_inc(s_hold, 1)
                    nc.gpsimd.indirect_dma_start(
                        out=ring[n % RING], out_offset=None, in_=a["L0_ffn_w_down" if n < SLOTS else "L0_ffn_w_up"],
                        in_offset=bass.IndirectOffsetOnAxis(ap=slots_of[j][:, s:s + 1], axis=0)).then_inc(s_row[n % RING], 16)

            with pool.Fori(0, PAIRS) as i:
                tile(i, 0)
                tile(i, 1)

        def mem_pe(pe):
            pe.wait_ge(p_keys, 16 * 2 * PKH)
            pe.wait_ge(m["hat"], ADDS["hat"] + 2 + 2 * TILES)
            for u in range(2 * PKH):
                mm = nc.tensor.transpose(psum[2 + u // 4][:, 128 * (u % 4):128 * (u % 4) + 128], keys_st[:, u, :], ident[:, :])
            mm.then_inc(p_keysT, 1)
            pe.wait_ge(p_keysS, 2 + 8)
            mlp_start_pe(pe, 1)
            ffn_turn_pe(pe, 1, 0)
            ffn_body_pe(pe, 1, 0)
            pe.wait_ge(p_w, 32)
            pe.sem_inc(p_top, 4 * 4)
            pe.sem_inc(p_out, 1)

            def scores(t, j, hh):
                pe.wait_ge(p_q, t * PKH + (j * PKH + hh + 1))
                pe.wait_ge(p_top, t * TOPN + (j * TOPN + 4 * max(hh - 1, 0) + 16))
                nc.tensor.matmul(psum[3 + hh % 2][0:P, :], pq_t[:, hh, :], keybd[:, hh, :], start=True, stop=True).then_inc(p_s_pe, 1)

            def queries(b):
                for hh in range(QB * b, QB * b + QB):
                    for k in range(KC):
                        mm = nc.tensor.matmul(psum[1 + b][:, P * (hh % QB):P * (hh % QB) + P], wqf[:, k, 128 * hh:128 * hh + 128],
                                              xl_t[:, P * k:P * k + P], start=(k == 0), stop=(k == KC - 1), skip_group_check=True)
                mm.then_inc(p_q_pe, 1)

            def turn(t, j):
                pe.wait_ge(p_x, t + (j + 1))
                for k in range(KC):
                    mm = nc.tensor.transpose(psum[0][:, P * k:P * k + P], xl[:, j % 2, 128 * k:128 * k + 128], ident[0:P, 0:P])
                mm.then_inc(p_xT_pe, 1)
                pe.wait_ge(p_xT, t + (j + 1))
                queries(0)
                queries(1)

            def rows(t, j, first, n):
                if first == 0:
                    pe.wait_ge(p_out, t + (j + 1))
                for s in range(first, first + n):
                    pe.wait_ge(p_diag, t * SLOTS + (j * SLOTS + s + 2))
                    pe.wait_ge(s_row[s % RING], landed(t, j, SLOTS + s))
                    nc.tensor.matmul(psum[7][0:P, :], diags[:, s % DRING, :], ring[s % RING], start=(s == 0), stop=(s == SLOTS - 1),
                                     skip_group_check=True).then_inc(p_up, 1)

            def tile(t, j):
                scores(t, j + 1, 0)
                scores(t, j + 1, 1)
                for hh in range(2, PKH):
                    rows(t, j, 2 * hh - 4, 2)
                    scores(t, j + 1, hh)
                rows(t, j, 2 * PKH - 4, SLOTS - 2 * PKH + 4)

            turn(0, 0)
            for hh in range(PKH):
                scores(0, 0, hh)
            with pe.Fori(0, PAIRS - 1) as i:
                turn(i * 2, 1)
                pe.wait_ge(p_q, i * (2 * PKH) + 2 * PKH)
                ffn_turn_pe(pe, 1, i + 1)
                ffn_body_pe(pe, 1, i + 1)
                tile(i * 2, 0)
                turn(i * 2, 2)
                tile(i * 2, 1)
            turn(TILES - 2, 1)
            tile(TILES - 2, 0)
            rows(TILES - 1, 0, 0, SLOTS)

        def mem_act(act):
            act.wait_ge(p_keysT, 1)
            act.wait_ge(p_w, 32)
            for s in range(2):
                for b in range(4):
                    rows = slice(64 * s, 64 * s + 64)
                    nc.scalar.activation(keybd[rows, 2 * b:2 * b + 2, NKEYS * s:NKEYS * s + NKEYS],
                                         psum[2 + b][rows, :].rearrange("p (h m) -> p h m", h=2), ACT.Copy).then_inc(p_keysS, 1)
            ffn_scale_act(act, 1, 0)
            ffn_gelu_act(act, 1, 0)

            def turn(t, j):
                act.wait_ge(p_xT_pe, t + (j + 1))
                nc.scalar.activation(xl_t, psum[0][:, 0:4 * P], ACT.Copy).then_inc(p_xT, 1)
                for hh in range(PKH):
                    b = hh // QB
                    if hh % QB == 0:
                        act.wait_ge(p_q_pe, t * 2 + (2 * j + b + 1))
                    nc.scalar.activation(pq_t[:, hh, :], psum[1 + b][:, P * (hh % QB):P * (hh % QB) + P], ACT.Identity,
                                         bias=c_bqf[:, hh:hh + 1]).then_inc(p_q, 1)

            def exps(t, j):
                act.wait_ge(p_exp, t * 2 + (2 * j + 1))
                nc.scalar.activation(probs.rearrange("p h k -> p (h k)"), probs.rearrange("p h k -> p (h k)"), ACT.Exp).then_inc(p_exp, 1)

            def place(t, j, first, n):
                if first == 0:
                    act.wait_ge(p_vals, t + (j + 1))
                for s in range(first, first + n):
                    act.wait_ge(p_up, t * SLOTS + (j * SLOTS + s - DRING + 1 + RING))
                    nc.scalar.activation(diags[:, s % DRING, :], ident[0:P, 0:P], ACT.Copy, scale=vals[:, s:s + 1]).then_inc(p_diag, 1)

            def tile(t, j):
                place(t, j, 0, EXP_AT)
                exps(t, j + 1)
                place(t, j, EXP_AT, SLOTS - EXP_AT)

            turn(0, 0)
            exps(0, 0)
            with act.Fori(0, PAIRS - 1) as i:
                turn(i * 2, 1)
                ffn_scale_act(act, 1, i + 1)
                ffn_gelu_act(act, 1, i + 1)
                tile(i * 2, 0)
                turn(i * 2, 2)
                tile(i * 2, 1)
            turn(TILES - 2, 1)
            tile(TILES - 2, 0)
            place(TILES - 1, 0, 0, SLOTS)

        def top_steps(dve, t, par, emit=True):
            n = 16

            def step(ins, sync=True):
                nonlocal n
                ins.then_inc(p_top, 1)
                n += 1
                if sync:
                    dve.wait_ge(p_top, t * TOPN + n)
                    hold_dve()

            for hh in range(PKH):
                dve.wait_ge(p_s_pe, t * PKH + (hh + 1))
                hold_dve()
                for s in range(2):
                    step(nc.vector.max(top_v[:, hh, s, :], psum[3 + hh % 2][0:P, NKEYS * s:NKEYS * s + NKEYS]), sync=(s == 1))
                for s in range(2):
                    step(nc.vector.max_index(top_i[:, hh, s, :], top_v[:, hh, s, :], psum[3 + hh % 2][0:P, NKEYS * s:NKEYS * s + NKEYS]), sync=False)
            dve.wait_ge(p_top, t * TOPN + n)
            step(nc.vector.tensor_copy(top_f, top_i), sync=False)
            step(nc.vector.tensor_tensor(sums.rearrange("p h (i j) -> p h i j", i=TOPK), top_v[:, :, 0, :].unsqueeze(3).to_broadcast([P, PKH, TOPK, TOPK]),
                                         top_v[:, :, 1, :].unsqueeze(2).to_broadcast([P, PKH, TOPK, TOPK]), ALU.add))
            for hh in range(PKH):
                step(nc.vector.max(best_v[:, hh, :], sums[:, hh, :]), sync=(hh == PKH - 1))
            for hh in range(PKH):
                step(nc.vector.max_index(best_i[:, hh, :], best_v[:, hh, :], sums[:, hh, :]), sync=(hh == PKH - 1))
            bi = best_i.rearrange("p h k -> p (h k)")
            step(nc.vector.tensor_scalar(best_hi, bi, 3, None, ALU.logical_shift_right), sync=False)
            step(nc.vector.tensor_scalar(best_lo, bi, 7, None, ALU.bitwise_and))
            step(nc.vector.tensor_copy(hi_f, best_hi), sync=False)
            step(nc.vector.tensor_copy(lo_f, best_lo))
            for s, (where, got) in enumerate(((hi_f, pick_a), (lo_f, pick_b))):
                step(nc.vector.tensor_tensor(pick.rearrange("p h k j -> p (h k) j"), where.unsqueeze(2).to_broadcast([P, SLOTS, TOPK]),
                                             iota8.unsqueeze(1).to_broadcast([P, SLOTS, TOPK]), ALU.is_equal))
                step(nc.vector.tensor_tensor(pick, pick, top_f[:, :, s, :].unsqueeze(2).to_broadcast([P, PKH, TOPK, TOPK]), ALU.mult))
                step(nc.vector.tensor_reduce(got, pick.rearrange("p h k j -> p (h k) j"), AX, ALU.add))
            step(nc.vector.scalar_tensor_tensor(slot_f, pick_a, float(NKEYS), pick_b, ALU.mult, ALU.add))
            nc.vector.tensor_copy(slots_of[par], slot_f).then_inc(p_slots, 1)
            nc.vector.tensor_tensor(probs, best_v, best_v[:, :, 0:1].to_broadcast([P, PKH, TOPK]), ALU.subtract).then_inc(p_exp, 1)
            dve.wait_ge(p_exp, t * 2 + 2)
            step(nc.vector.tensor_reduce(prob_s, probs, AX, ALU.add))
            step(nc.vector.reciprocal(prob_s, prob_s))
            step(nc.vector.tensor_tensor(probs, probs, prob_s.unsqueeze(2).to_broadcast([P, PKH, TOPK]), ALU.mult))

        TOPN = 4 * PKH + 2 + 2 * PKH + 4 + 6 + 1 + 3

        def mem_dve(dve):
            dve.wait_ge(m["hat"], ADDS["hat"] + 2 + 2 * TILES)
            ln2_dve(dve, 1)

            def finish(i):
                ffn_take(dve, 1, i)
                dve.wait_ge(p_res, i * 16 + 16)
                dve.wait_ge(m["hf"], ADDS["hf"] + i * 4 + 6)
                for j in range(2):
                    ht = sq1(h[:, ds(i * 2 + j, 1), :])
                    nc.vector.tensor_tensor(ht, ht, res_p[:, j, :], ALU.add).then_inc(p_h, 1)
                dve.wait_ge(p_h, i * 2 + 2)
                hold_dve()
                for j in range(2):
                    nc.vector.bn_stats(st6[:, j, :], sq1(h[:, ds(i * 2 + j, 1), :])).then_inc(p_ln, 1)
                dve.wait_ge(p_ln, i * LN3 + 2)
                hold_dve()
                for j in range(2):
                    nc.vector.bn_aggr(mvm[:, j, :], st6[:, j, :]).then_inc(p_ln, 1)
                dve.wait_ge(p_ln, i * LN3 + 4)
                rsqrt(dve, p_ln, i * LN3 + 4, mvm[:, :, 1], 0, 2)
                dve.wait_ge(p_ln, i * LN3 + LN3)

            def norm3(t, j):
                nc.vector.tensor_scalar(xl[:, j, :], sq1(h[:, ds(t, 1), :]), mvm[:, j, 0:1], rs[:, 0, j:j + 1], ALU.subtract, ALU.mult).then_inc(p_x, 1)

            def dots(i, j, first=0, n=SLOTS):
                for s in range(first, first + n):
                    dve.wait_ge(s_row[s % RING], landed(i * 2, j, s))
                    nc.vector.tensor_tensor_reduce(out=ring[s % RING], in0=ring[s % RING], in1=xl[:, j, :], scale=1.0, scalar=0.0,
                                                   op0=ALU.mult, op1=ALU.add, accum_out=inner[:, s:s + 1]).then_inc(p_dn, 1)

            def weigh(i, j):
                dve.wait_ge(p_dn, i * (2 * SLOTS) + ((j + 1) * SLOTS))
                dve.wait_ge(p_diag, i * (2 * SLOTS) + (j * SLOTS + 1))
                nc.vector.scalar_tensor_tensor(vals, inner, 0.0, probs.rearrange("p h k -> p (h k)"), ALU.max, ALU.mult).then_inc(p_vals, 1)

            def take(i, j):
                dve.wait_ge(s_out[j], i * 16 + 16)
                dve.wait_ge(p_up, i * (2 * SLOTS) + (RING + (j + 1) * SLOTS))
                nc.vector.tensor_tensor(acc_of[j], psum[7][0:P, :], sq1(h[:, ds(i * 2 + j, 1), :]), ALU.add).then_inc(p_out, 1)

            for n in range(TOPK):
                nc.vector.memset(iota8[:, n:n + 1], float(n)).then_inc(m["ln2"], 1)
            dve.wait_ge(m["ln2"], ADDS["ln2"] + LN2 + TOPK)
            dve.sem_inc(s_out[0], 16)
            dve.sem_inc(s_out[1], 16)
            norm2(dve, 1, 0)
            finish(0)
            norm3(0, 0)
            top_steps(dve, 0, 0)
            with dve.Fori(0, PAIRS - 1) as i:
                norm3(i * 2 + 1, 1)
                norm2(dve, 1, i + 1)
                dots(i, 0)
                weigh(i, 0)
                top_steps(dve, i * 2 + 1, 1)
                take(i, 0)
                dots(i, 1, 0, TAKE_AT)
                finish(i + 1)
                norm3(i * 2 + 2, 0)
                dots(i, 1, TAKE_AT, SLOTS - TAKE_AT)
                weigh(i, 1)
                top_steps(dve, i * 2 + 2, 0)
                take(i, 1)
            norm3(TILES - 1, 1)
            dots(PAIRS - 1, 0)
            weigh(PAIRS - 1, 0)
            top_steps(dve, TILES - 1, 1)
            take(PAIRS - 1, 0)
            dots(PAIRS - 1, 1)
            weigh(PAIRS - 1, 1)
            take(PAIRS - 1, 1)

        @block.sync
        def _(sp):
            setup_sp(sp)
            mlp_loads_sp(sp, 0)
            bases_sp(sp)
            gcn_sp(sp, 0)
            gcn_sp(sp, 1)
            sp.wait_ge(g_sem[1]["out"], OUT_DONE)
            attn_loads_sp(sp, 1)
            wo_load_sp(sp, 1)
            mlp_loads_sp(sp, 1)
            mem_sp(sp)

        @block.gpsimd
        def _(pool):
            setup_pool()
            adjacency_pool(pool)
            mem_pool(pool)

        @block.tensor
        def _(pe):
            setup_pe(pe)
            for l in range(2):
                attn1_pe(pe, l)
                attn2_pe(pe, l)
                attn3_pe(pe, l)
                if l == 0:
                    mlp_pe(pe)
                    gcn_pe(pe, 0)
                    gcn_pe(pe, 1)
            mem_pe(pe)

        @block.scalar
        def _(act):
            for l in range(2):
                attn1_act(act, l)
                attn2_act(act, l)
                attn3_act(act, l)
                if l == 0:
                    mlp_act(act)
                    gcn_act(act, 0)
                    gcn_act(act, 1)
                    gcn_x_act(act, 1)
            mem_act(act)

        @block.vector
        def _(dve):
            setup_dve(dve)
            for l in range(2):
                attn1_dve(dve, l)
                attn2_dve(dve, l)
                attn3_dve(dve, l)
                if l == 0:
                    mlp_dve(dve)
                    gcn_dve(dve, 0)
                    gcn_dve(dve, 1)
            mem_dve(dve)


def kernel(**inputs):
    import numpy as np
    import concourse.bacc as bacc
    from concourse.bass_utils import run_bass_kernel_spmd

    nc = bacc.Bacc("TRN2", target_bir_lowering=False, num_devices=1)
    arrays, aps = {}, {}
    for name, value in inputs.items():
        v = np.ascontiguousarray(value)
        arrays["in_" + name] = v
        aps[name] = nc.dram_tensor("in_" + name, v.shape, mybir.dt.from_np(v.dtype), kind="ExternalInput").ap()
    out = nc.dram_tensor("out", (NODES, DIM), F32, kind="ExternalOutput").ap()
    build(nc, aps, out)
    r = run_bass_kernel_spmd(nc, [arrays], core_ids=[0])
    return r.results[0]["out"]
```
